# Optimizing a Trainium2 kernel written in Bass

```python
import numpy as np
import jax
import jax.numpy as jnp

def _softmax(x, axis=-1):
    return jax.nn.softmax(x, axis=axis)

def _gelu(x):
    return jax.nn.gelu(x, approximate=True)

def _silu(x):
    return jax.nn.silu(x)

def _sigmoid(x):
    return jax.nn.sigmoid(x)

def _layernorm(x, axis=-1, eps=1e-05):
    m = jnp.mean(x, axis=axis, keepdims=True)
    v = jnp.var(x, axis=axis, keepdims=True)
    return (x - m) / jnp.sqrt(v + eps)

def _scatter_add(tgt, idx, src, axis=0):
    return tgt.at[idx].add(src)

def _segment_sum(src, seg, n):
    return jax.ops.segment_sum(src, seg, n)
kernel_name = 'mk_vit_tower_d4_tok_img768_r4_4efa37'

def setup_inputs(seed: int=0):
    np.random.seed(seed)
    _w = jnp.asarray

    def _rec_inputs():
        import jax
        import jax.numpy as jnp
        _rk = jax.random.key(seed)
        x = -0.000147625 + 0.999875 * jax.random.normal(jax.random.fold_in(_rk, 1), (32, 3, 96, 96), jnp.float32)
        return x
    x = _rec_inputs()

    def _L0_tok_setup():
        import jax, jax.numpy as jnp
        import numpy as np
        IN_CH = 3
        PATCH = 16
        EMB = 192
        IMG = 224
        BATCH = 64
        key = jax.random.key(seed)
        kx, kw, kb = jax.random.split(key, 3)
        x = jax.random.normal(kx, (BATCH, IN_CH, IMG, IMG), dtype=jnp.float32)
        in_feat = IN_CH * PATCH * PATCH
        bound = 1.0 / np.sqrt(in_feat)
        W = jax.random.uniform(kw, (EMB, in_feat), minval=-bound, maxval=bound, dtype=jnp.float32)
        b = jax.random.uniform(kb, (EMB,), minval=-bound, maxval=bound, dtype=jnp.float32)
        return {'x': x, 'W': W, 'b': b}
    _L0_tok_all = _L0_tok_setup()
    _L0_tok_in = {k: v for k, v in _L0_tok_all.items() if k in ('W', 'b')}
    del _L0_tok_all

    def _L0_attn_setup():
        import jax, jax.numpy as jnp
        import numpy as np
        B, L, D, H, F, NL, K, G = (2, 512, 192, 12, 768, 12, 128, 16)
        HD = D // H
        SCALE = HD ** (-0.5)

        def _ln(x, g, b, eps=1e-05):
            m = jnp.mean(x, axis=-1, keepdims=True)
            v = jnp.mean(jnp.square(x - m), axis=-1, keepdims=True)
            return (x - m) * jax.lax.rsqrt(v + eps) * g + b
        key = jax.random.key(seed)
        ks = jax.random.split(key, 8)
        n = lambda k, s, std=0.02: jax.random.normal(k, s, dtype=jnp.float32) * std
        return {'x': jax.random.normal(ks[0], (B, L, D), dtype=jnp.float32), 'pos_conv_w': n(ks[1], (D, D // G, K)), 'pos_conv_b': jnp.zeros((D,), jnp.float32), 'ln0_g': jnp.ones((D,), jnp.float32), 'ln0_b': jnp.zeros((D,), jnp.float32), 'Wq': n(ks[2], (NL, D, D)), 'bq': jnp.zeros((NL, D), jnp.float32), 'Wk': n(ks[3], (NL, D, D)), 'bk': jnp.zeros((NL, D), jnp.float32), 'Wv': n(ks[4], (NL, D, D)), 'bv': jnp.zeros((NL, D), jnp.float32), 'Wo': n(ks[5], (NL, D, D)), 'bo': jnp.zeros((NL, D), jnp.float32), 'ln1_g': jnp.ones((NL, D), jnp.float32), 'ln1_b': jnp.zeros((NL, D), jnp.float32), 'W1': n(ks[6], (NL, D, F)), 'b1': jnp.zeros((NL, F), jnp.float32), 'W2': n(ks[7], (NL, F, D)), 'b2': jnp.zeros((NL, D), jnp.float32), 'ln2_g': jnp.ones((NL, D), jnp.float32), 'ln2_b': jnp.zeros((NL, D), jnp.float32)}
    _L0_attn_all = _L0_attn_setup()
    _L0_attn_in = {k: v for k, v in _L0_attn_all.items() if k in ('pos_conv_w', 'pos_conv_b', 'ln0_g', 'ln0_b', 'Wq', 'bq', 'Wk', 'bk', 'Wv', 'bv', 'Wo', 'bo', 'ln1_g', 'ln1_b', 'W1', 'b1', 'W2', 'b2', 'ln2_g', 'ln2_b')}
    del _L0_attn_all

    def _L0_ffn_setup():
        import jax, jax.numpy as jnp
        import numpy as np
        B, S, D, F = (2, 128, 192, 768)
        L, H, DK = (4, 12, 64)
        E, K = (8, 2)
        NB, MAXD = (32, 128)
        MOE_LAYERS = (1, 3)
        EPS = 1e-06

        def t5_layer_norm(x, w):
            var = jnp.mean(x * x, axis=-1, keepdims=True)
            return w * x * jax.lax.rsqrt(var + EPS)

        def relative_position_bias(rel_emb, seq_len):
            ctx = jnp.arange(seq_len)[:, None]
            mem = jnp.arange(seq_len)[None, :]
            rel = mem - ctx
            nb = NB // 2
            buckets = (rel > 0).astype(jnp.int32) * nb
            n = jnp.abs(rel)
            max_exact = nb // 2
            is_small = n < max_exact
            nf = jnp.maximum(n, 1).astype(jnp.float32)
            large = max_exact + (jnp.log(nf / max_exact) / np.log(MAXD / max_exact) * (nb - max_exact)).astype(jnp.int32)
            large = jnp.minimum(large, nb - 1)
            buckets = buckets + jnp.where(is_small, n, large)
            return rel_emb[buckets].transpose(2, 0, 1)[None]

        def moe_ffn(x2d, gw, w1, w2):
            logits = x2d @ gw
            vals, idx = jax.lax.top_k(logits, K)
            gsc = jax.nn.softmax(vals, axis=-1)
            T = x2d.shape[0]
            cw = jnp.zeros((T, E), x2d.dtype).at[jnp.arange(T)[:, None], idx].add(gsc)

            def body(acc, xs):
                w1e, w2e, cwe = xs
                y = jax.nn.gelu(x2d @ w1e, approximate=False) @ w2e
                return (acc + cwe[:, None] * y, None)
            out, _ = jax.lax.scan(body, jnp.zeros_like(x2d), (w1, w2, cw.T))
            return out
        key = jax.random.key(seed)
        ks = list(jax.random.split(key, 16))

        def nrm(k, shape, scale=0.02):
            return jax.random.normal(k, shape, jnp.float32) * scale
        M = len(MOE_LAYERS)
        return {'x': nrm(ks[0], (B, S, D), 1.0), 'attn_q': nrm(ks[1], (L, D, H * DK)), 'attn_k': nrm(ks[2], (L, D, H * DK)), 'attn_v': nrm(ks[3], (L, D, H * DK)), 'attn_o': nrm(ks[4], (L, H * DK, D)), 'ffn_wi': nrm(ks[5], (L, D, F)), 'ffn_wo': nrm(ks[6], (L, F, D)), 'ln1': jnp.ones((L, D), jnp.float32), 'ln2': jnp.ones((L, D), jnp.float32), 'ln_f': jnp.ones((D,), jnp.float32), 'rel_emb': nrm(ks[7], (NB, H), 0.1), 'gate_w': nrm(ks[8], (M, D, E)), 'moe_w1': nrm(ks[9], (M, E, D, F)), 'moe_w2': nrm(ks[10], (M, E, F, D))}
    _L0_ffn_all = _L0_ffn_setup()
    _L0_ffn_in = {k: v for k, v in _L0_ffn_all.items() if k in ('attn_q', 'attn_k', 'attn_v', 'attn_o', 'ffn_wi', 'ffn_wo', 'ln1', 'ln2', 'ln_f', 'rel_emb', 'gate_w', 'moe_w1', 'moe_w2')}
    del _L0_ffn_all

    def _L1_attn_setup():
        import jax, jax.numpy as jnp
        import numpy as np
        DIM = 192
        NUM_HEADS = 12
        DIM_HEAD = 64
        SCALE = 1.0 / DIM_HEAD ** 0.5
        key = jax.random.key(seed)
        k1, k2, k3 = jax.random.split(key, 3)
        x = jax.random.normal(k1, (8, 256, DIM), dtype=jnp.float32)
        W_qkv = jax.random.normal(k2, (3 * NUM_HEADS * DIM_HEAD, DIM), dtype=jnp.float32) * 0.02
        W_out = jax.random.normal(k3, (DIM, NUM_HEADS * DIM_HEAD), dtype=jnp.float32) * 0.02
        return {'x': x, 'W_qkv': W_qkv, 'W_out': W_out}
    _L1_attn_all = _L1_attn_setup()
    _L1_attn_in = {k: v for k, v in _L1_attn_all.items() if k in ('W_qkv', 'W_out')}
    del _L1_attn_all

    def _L1_ffn_setup():
        import jax, jax.numpy as jnp
        import numpy as np
        B, S, H = (4, 2048, 192)
        E, K = (8, 2)
        key = jax.random.key(seed)
        ks = jax.random.split(key, 5)
        scale = 1.0 / np.sqrt(H)
        x = jax.random.normal(ks[0], (B, S, H), dtype=jnp.float32)
        router_w = jax.random.uniform(ks[1], (E, H), jnp.float32, -scale, scale)
        router_b = jax.random.uniform(ks[2], (E,), jnp.float32, -scale, scale)
        expert_w = jax.random.uniform(ks[3], (E, H, H), jnp.float32, -scale, scale)
        expert_b = jax.random.uniform(ks[4], (E, H), jnp.float32, -scale, scale)
        return {'x': x, 'router_w': router_w, 'router_b': router_b, 'expert_w': expert_w, 'expert_b': expert_b}
    _L1_ffn_all = _L1_ffn_setup()
    _L1_ffn_in = {k: v for k, v in _L1_ffn_all.items() if k in ('router_w', 'router_b', 'expert_w', 'expert_b')}
    del _L1_ffn_all

    def _L2_attn_setup():
        import jax, jax.numpy as jnp
        import numpy as np
        import math
        N_HEAD = 12
        N_EMBD = 192
        HEAD_DIM = N_EMBD // N_HEAD // 2
        DEPTH = 12
        LAMBDA_INIT = 0.8 - 0.6 * math.exp(-0.3 * DEPTH)

        def _sdpa_over_heads(q, k, v):
            scale = 1.0 / math.sqrt(q.shape[-1])
            s = jnp.einsum('bnqd,bnkd->bnqk', q, k) * scale
            a = jax.nn.softmax(s, axis=-1)
            return jnp.einsum('bnqk,bnkd->bnqd', a, v)
        key = jax.random.key(seed)
        ks = jax.random.split(key, 7)
        B, N, D = (4, 2048, N_EMBD)
        s = 0.02
        return {'x': jax.random.normal(ks[0], (B, N, D), dtype=jnp.float32), 'W_attn': jax.random.normal(ks[1], (3 * D, D), dtype=jnp.float32) * s, 'W_out': jax.random.normal(ks[2], (D, D), dtype=jnp.float32) * s, 'lambda_q1': jax.random.normal(ks[3], (HEAD_DIM,), dtype=jnp.float32) * 0.1, 'lambda_k1': jax.random.normal(ks[4], (HEAD_DIM,), dtype=jnp.float32) * 0.1, 'lambda_q2': jax.random.normal(ks[5], (HEAD_DIM,), dtype=jnp.float32) * 0.1, 'lambda_k2': jax.random.normal(ks[6], (HEAD_DIM,), dtype=jnp.float32) * 0.1}
    _L2_attn_all = _L2_attn_setup()
    _L2_attn_in = {k: v for k, v in _L2_attn_all.items() if k in ('W_attn', 'W_out', 'lambda_q1', 'lambda_k1', 'lambda_q2', 'lambda_k2')}
    del _L2_attn_all

    def _L2_ffn_setup():
        import jax, jax.numpy as jnp
        import numpy as np
        N_EMBD = 192
        N_EXPERTS = 8
        TOP_K = 2
        D_FF = 4 * N_EMBD
        key = jax.random.key(seed)
        ks = jax.random.split(key, 7)
        B, T, C, E, H = (4, 512, N_EMBD, N_EXPERTS, D_FF)
        s_gate = 1.0 / np.sqrt(C)
        s1 = 1.0 / np.sqrt(C)
        s2 = 1.0 / np.sqrt(H)
        return {'x': jax.random.normal(ks[0], (B, T, C), dtype=jnp.float32), 'gate_w': jax.random.uniform(ks[1], (C, E), jnp.float32, -s_gate, s_gate), 'gate_b': jax.random.uniform(ks[2], (E,), jnp.float32, -s_gate, s_gate), 'w1': jax.random.uniform(ks[3], (E, C, H), jnp.float32, -s1, s1), 'b1': jax.random.uniform(ks[4], (E, H), jnp.float32, -s1, s1), 'w2': jax.random.uniform(ks[5], (E, H, C), jnp.float32, -s2, s2), 'b2': jax.random.uniform(ks[6], (E, C), jnp.float32, -s2, s2)}
    _L2_ffn_all = _L2_ffn_setup()
    _L2_ffn_in = {k: v for k, v in _L2_ffn_all.items() if k in ('gate_w', 'gate_b', 'w1', 'b1', 'w2', 'b2')}
    del _L2_ffn_all

    def _L3_attn_setup():
        import jax, jax.numpy as jnp
        import numpy as np
        EMBED_DIM = 192
        SEQ_LEN = 256
        BATCH = 32
        ALPHA = 0.99

        def _decay_mask(sl: int, alpha: float) -> jnp.ndarray:
            i = jnp.arange(sl, dtype=jnp.float32)
            diff = i[:, None] - i[None, :]
            return jnp.where(diff >= 0, jnp.float32(alpha) ** diff, 0.0)
        key = jax.random.key(seed)
        k1, k2 = jax.random.split(key)
        x = jax.random.normal(k1, (BATCH, SEQ_LEN, EMBED_DIM), dtype=jnp.float32)
        W_qkv = jax.random.normal(k2, (EMBED_DIM, 3 * EMBED_DIM), dtype=jnp.float32) * EMBED_DIM ** (-0.5)
        b_qkv = jnp.zeros((3 * EMBED_DIM,), dtype=jnp.float32)
        return {'x': x, 'W_qkv': W_qkv, 'b_qkv': b_qkv}
    _L3_attn_all = _L3_attn_setup()
    _L3_attn_in = {k: v for k, v in _L3_attn_all.items() if k in ('W_qkv', 'b_qkv')}
    del _L3_attn_all

    def _L3_ffn_setup():
        import jax, jax.numpy as jnp
        import numpy as np
        H = 192
        I = 96
        E = 16
        G = 4
        TOPK_GROUP = 2
        TOP_K = 4
        SCALE = 2.5
        N_SHARED = 2
        IS = I * N_SHARED
        B, S = (1, 512)

        def _route(x, router_w, router_b, corr_bias):
            logits = x.astype(jnp.float32) @ router_w.T + router_b
            scores = jax.nn.sigmoid(logits)
            sfc = scores + corr_bias[None, :]
            grp = sfc.reshape(-1, G, E // G)
            group_scores = jax.lax.top_k(grp, 2)[0].sum(-1)
            _, gidx = jax.lax.top_k(group_scores, TOPK_GROUP)
            gmask = jax.nn.one_hot(gidx, G, dtype=sfc.dtype).sum(axis=1)
            score_mask = jnp.repeat(gmask, E // G, axis=-1)
            sfc = jnp.where(score_mask > 0, sfc, 0.0)
            _, idx = jax.lax.top_k(sfc, TOP_K)
            w = jnp.take_along_axis(scores, idx, axis=1)
            w = w / (w.sum(-1, keepdims=True) + 1e-20)
            return (idx, w * SCALE)

        def _forward(x3, router_w, router_b, corr_bias, gWg, gbg, gWu, gbu, gWd, gbd, sWg, sbg, sWu, sbu, sWd, sbd):
            orig_shape = x3.shape
            x = x3.reshape(-1, H)
            idx, w = _route(x, router_w, router_b, corr_bias)
            c = (jax.nn.one_hot(idx, E, dtype=w.dtype) * w[..., None]).sum(1)
            h = jax.nn.silu(jnp.einsum('th,ehi->tei', x, gWg) + gbg) * (jnp.einsum('th,ehi->tei', x, gWu) + gbu)
            out_e = jnp.einsum('tei,eih->teh', h, gWd) + gbd
            moe_out = jnp.einsum('te,teh->th', c, out_e)
            hs = jax.nn.silu(x @ sWg + sbg) * (x @ sWu + sbu)
            shared = hs @ sWd + sbd
            return (moe_out + shared).reshape(orig_shape)
        key = jax.random.key(seed)
        ks = jax.random.split(key, 16)
        s = lambda k, shape, fan: jax.random.normal(k, shape, jnp.float32) * fan ** (-0.5)
        return {'hidden_states': jax.random.normal(ks[0], (B, S, H), jnp.float32), 'router_w': s(ks[1], (E, H), H), 'router_b': jnp.zeros((E,), jnp.float32), 'corr_bias': jnp.zeros((E,), jnp.float32), 'gWg': s(ks[2], (E, H, I), H), 'gbg': jnp.zeros((E, I), jnp.float32), 'gWu': s(ks[3], (E, H, I), H), 'gbu': jnp.zeros((E, I), jnp.float32), 'gWd': s(ks[4], (E, I, H), I), 'gbd': jnp.zeros((E, H), jnp.float32), 'sWg': s(ks[5], (H, IS), H), 'sbg': jnp.zeros((IS,), jnp.float32), 'sWu': s(ks[6], (H, IS), H), 'sbu': jnp.zeros((IS,), jnp.float32), 'sWd': s(ks[7], (IS, H), IS), 'sbd': jnp.zeros((H,), jnp.float32)}
    _L3_ffn_all = _L3_ffn_setup()
    _L3_ffn_in = {k: v for k, v in _L3_ffn_all.items() if k in ('router_w', 'router_b', 'corr_bias', 'gWg', 'gbg', 'gWu', 'gbu', 'gWd', 'gbd', 'sWg', 'sbg', 'sWu', 'sbu', 'sWd', 'sbd')}
    del _L3_ffn_all
    return {'x': x, 'L0_tok_W': _L0_tok_in['W'], 'L0_tok_b': _L0_tok_in['b'], 'L0_attn_pos_conv_w': _L0_attn_in['pos_conv_w'], 'L0_attn_pos_conv_b': _L0_attn_in['pos_conv_b'], 'L0_attn_ln0_g': _L0_attn_in['ln0_g'], 'L0_attn_ln0_b': _L0_attn_in['ln0_b'], 'L0_attn_Wq': _L0_attn_in['Wq'], 'L0_attn_bq': _L0_attn_in['bq'], 'L0_attn_Wk': _L0_attn_in['Wk'], 'L0_attn_bk': _L0_attn_in['bk'], 'L0_attn_Wv': _L0_attn_in['Wv'], 'L0_attn_bv': _L0_attn_in['bv'], 'L0_attn_Wo': _L0_attn_in['Wo'], 'L0_attn_bo': _L0_attn_in['bo'], 'L0_attn_ln1_g': _L0_attn_in['ln1_g'], 'L0_attn_ln1_b': _L0_attn_in['ln1_b'], 'L0_attn_W1': _L0_attn_in['W1'], 'L0_attn_b1': _L0_attn_in['b1'], 'L0_attn_W2': _L0_attn_in['W2'], 'L0_attn_b2': _L0_attn_in['b2'], 'L0_attn_ln2_g': _L0_attn_in['ln2_g'], 'L0_attn_ln2_b': _L0_attn_in['ln2_b'], 'L0_ffn_attn_q': _L0_ffn_in['attn_q'], 'L0_ffn_attn_k': _L0_ffn_in['attn_k'], 'L0_ffn_attn_v': _L0_ffn_in['attn_v'], 'L0_ffn_attn_o': _L0_ffn_in['attn_o'], 'L0_ffn_ffn_wi': _L0_ffn_in['ffn_wi'], 'L0_ffn_ffn_wo': _L0_ffn_in['ffn_wo'], 'L0_ffn_ln1': _L0_ffn_in['ln1'], 'L0_ffn_ln2': _L0_ffn_in['ln2'], 'L0_ffn_ln_f': _L0_ffn_in['ln_f'], 'L0_ffn_rel_emb': _L0_ffn_in['rel_emb'], 'L0_ffn_gate_w': _L0_ffn_in['gate_w'], 'L0_ffn_moe_w1': _L0_ffn_in['moe_w1'], 'L0_ffn_moe_w2': _L0_ffn_in['moe_w2'], 'L1_attn_W_qkv': _L1_attn_in['W_qkv'], 'L1_attn_W_out': _L1_attn_in['W_out'], 'L1_ffn_router_w': _L1_ffn_in['router_w'], 'L1_ffn_router_b': _L1_ffn_in['router_b'], 'L1_ffn_expert_w': _L1_ffn_in['expert_w'], 'L1_ffn_expert_b': _L1_ffn_in['expert_b'], 'L2_attn_W_attn': _L2_attn_in['W_attn'], 'L2_attn_W_out': _L2_attn_in['W_out'], 'L2_attn_lambda_q1': _L2_attn_in['lambda_q1'], 'L2_attn_lambda_k1': _L2_attn_in['lambda_k1'], 'L2_attn_lambda_q2': _L2_attn_in['lambda_q2'], 'L2_attn_lambda_k2': _L2_attn_in['lambda_k2'], 'L2_ffn_gate_w': _L2_ffn_in['gate_w'], 'L2_ffn_gate_b': _L2_ffn_in['gate_b'], 'L2_ffn_w1': _L2_ffn_in['w1'], 'L2_ffn_b1': _L2_ffn_in['b1'], 'L2_ffn_w2': _L2_ffn_in['w2'], 'L2_ffn_b2': _L2_ffn_in['b2'], 'L3_attn_W_qkv': _L3_attn_in['W_qkv'], 'L3_attn_b_qkv': _L3_attn_in['b_qkv'], 'L3_ffn_router_w': _L3_ffn_in['router_w'], 'L3_ffn_router_b': _L3_ffn_in['router_b'], 'L3_ffn_corr_bias': _L3_ffn_in['corr_bias'], 'L3_ffn_gWg': _L3_ffn_in['gWg'], 'L3_ffn_gbg': _L3_ffn_in['gbg'], 'L3_ffn_gWu': _L3_ffn_in['gWu'], 'L3_ffn_gbu': _L3_ffn_in['gbu'], 'L3_ffn_gWd': _L3_ffn_in['gWd'], 'L3_ffn_gbd': _L3_ffn_in['gbd'], 'L3_ffn_sWg': _L3_ffn_in['sWg'], 'L3_ffn_sbg': _L3_ffn_in['sbg'], 'L3_ffn_sWu': _L3_ffn_in['sWu'], 'L3_ffn_sbu': _L3_ffn_in['sbu'], 'L3_ffn_sWd': _L3_ffn_in['sWd'], 'L3_ffn_sbd': _L3_ffn_in['sbd']}

def reference(x, L0_tok_W, L0_tok_b, L0_attn_pos_conv_w, L0_attn_pos_conv_b, L0_attn_ln0_g, L0_attn_ln0_b, L0_attn_Wq, L0_attn_bq, L0_attn_Wk, L0_attn_bk, L0_attn_Wv, L0_attn_bv, L0_attn_Wo, L0_attn_bo, L0_attn_ln1_g, L0_attn_ln1_b, L0_attn_W1, L0_attn_b1, L0_attn_W2, L0_attn_b2, L0_attn_ln2_g, L0_attn_ln2_b, L0_ffn_attn_q, L0_ffn_attn_k, L0_ffn_attn_v, L0_ffn_attn_o, L0_ffn_ffn_wi, L0_ffn_ffn_wo, L0_ffn_ln1, L0_ffn_ln2, L0_ffn_ln_f, L0_ffn_rel_emb, L0_ffn_gate_w, L0_ffn_moe_w1, L0_ffn_moe_w2, L1_attn_W_qkv, L1_attn_W_out, L1_ffn_router_w, L1_ffn_router_b, L1_ffn_expert_w, L1_ffn_expert_b, L2_attn_W_attn, L2_attn_W_out, L2_attn_lambda_q1, L2_attn_lambda_k1, L2_attn_lambda_q2, L2_attn_lambda_k2, L2_ffn_gate_w, L2_ffn_gate_b, L2_ffn_w1, L2_ffn_b1, L2_ffn_w2, L2_ffn_b2, L3_attn_W_qkv, L3_attn_b_qkv, L3_ffn_router_w, L3_ffn_router_b, L3_ffn_corr_bias, L3_ffn_gWg, L3_ffn_gbg, L3_ffn_gWu, L3_ffn_gbu, L3_ffn_gWd, L3_ffn_gbd, L3_ffn_sWg, L3_ffn_sbg, L3_ffn_sWu, L3_ffn_sbu, L3_ffn_sWd, L3_ffn_sbd):
    import jax
    import jax.numpy as jnp

    def _L0_tok_ref(x, W, b):
        import jax, jax.numpy as jnp
        import numpy as np
        IN_CH = 3
        PATCH = 16
        EMB = 192
        IMG = 224
        BATCH = 64
        B, C, H, Wd = x.shape
        p = PATCH
        nh, nw = (H // p, Wd // p)
        patches = x.reshape(B, C, nh, p, nw, p).transpose(0, 1, 2, 4, 3, 5)
        patches = patches.reshape(B, C, nh * nw, p, p).transpose(0, 2, 3, 4, 1)
        feats = patches.reshape(B, nh * nw, p * p * C)
        return jnp.einsum('bnf,ef->bne', feats, W) + b

    def _L0_attn_ref(x, pos_conv_w, pos_conv_b, ln0_g, ln0_b, Wq, bq, Wk, bk, Wv, bv, Wo, bo, ln1_g, ln1_b, W1, b1, W2, b2, ln2_g, ln2_b):
        import jax, jax.numpy as jnp
        import numpy as np
        B, L, D, H, F, NL, K, G = (2, 512, 192, 12, 768, 12, 128, 16)
        HD = D // H
        SCALE = HD ** (-0.5)

        def _ln(x, g, b, eps=1e-05):
            m = jnp.mean(x, axis=-1, keepdims=True)
            v = jnp.mean(jnp.square(x - m), axis=-1, keepdims=True)
            return (x - m) * jax.lax.rsqrt(v + eps) * g + b
        b_, l_, d_ = x.shape
        pos = jax.lax.conv_general_dilated(x.transpose(0, 2, 1), pos_conv_w, (1,), [(K // 2, K // 2)], feature_group_count=G)
        pos = pos[:, :, :l_] + pos_conv_b[None, :, None]
        h = x + jax.nn.gelu(pos, approximate=False).transpose(0, 2, 1)
        h = _ln(h, ln0_g, ln0_b)

        def layer(h, p):
            wq, bq_, wk, bk_, wv, bv_, wo, bo_, g1, be1, w1, bf1, w2, bf2, g2, be2 = p
            r = h
            q = (h @ wq + bq_).reshape(b_, l_, H, HD)
            k = (h @ wk + bk_).reshape(b_, l_, H, HD)
            v = (h @ wv + bv_).reshape(b_, l_, H, HD)
            w = jax.nn.softmax(SCALE * jnp.einsum('blhd,bmhd->bhlm', q, k), axis=-1)
            o = jnp.einsum('bhlm,bmhd->blhd', w, v).reshape(b_, l_, d_)
            h = r + (o @ wo + bo_)
            h = _ln(h, g1, be1)
            ff = jax.nn.gelu(h @ w1 + bf1, approximate=False) @ w2 + bf2
            h = _ln(h + ff, g2, be2)
            return (h, None)
        h, _ = jax.lax.scan(layer, h, (Wq, bq, Wk, bk, Wv, bv, Wo, bo, ln1_g, ln1_b, W1, b1, W2, b2, ln2_g, ln2_b))
        return h

    def _L0_ffn_ref(x, attn_q, attn_k, attn_v, attn_o, ffn_wi, ffn_wo, ln1, ln2, ln_f, rel_emb, gate_w, moe_w1, moe_w2):
        import jax, jax.numpy as jnp
        import numpy as np
        B, S, D, F = (2, 128, 192, 768)
        L, H, DK = (4, 12, 64)
        E, K = (8, 2)
        NB, MAXD = (32, 128)
        MOE_LAYERS = (1, 3)
        EPS = 1e-06

        def t5_layer_norm(x, w):
            var = jnp.mean(x * x, axis=-1, keepdims=True)
            return w * x * jax.lax.rsqrt(var + EPS)

        def relative_position_bias(rel_emb, seq_len):
            ctx = jnp.arange(seq_len)[:, None]
            mem = jnp.arange(seq_len)[None, :]
            rel = mem - ctx
            nb = NB // 2
            buckets = (rel > 0).astype(jnp.int32) * nb
            n = jnp.abs(rel)
            max_exact = nb // 2
            is_small = n < max_exact
            nf = jnp.maximum(n, 1).astype(jnp.float32)
            large = max_exact + (jnp.log(nf / max_exact) / np.log(MAXD / max_exact) * (nb - max_exact)).astype(jnp.int32)
            large = jnp.minimum(large, nb - 1)
            buckets = buckets + jnp.where(is_small, n, large)
            return rel_emb[buckets].transpose(2, 0, 1)[None]

        def moe_ffn(x2d, gw, w1, w2):
            logits = x2d @ gw
            vals, idx = jax.lax.top_k(logits, K)
            gsc = jax.nn.softmax(vals, axis=-1)
            T = x2d.shape[0]
            cw = jnp.zeros((T, E), x2d.dtype).at[jnp.arange(T)[:, None], idx].add(gsc)

            def body(acc, xs):
                w1e, w2e, cwe = xs
                y = jax.nn.gelu(x2d @ w1e, approximate=False) @ w2e
                return (acc + cwe[:, None] * y, None)
            out, _ = jax.lax.scan(body, jnp.zeros_like(x2d), (w1, w2, cw.T))
            return out
        b, s, d = x.shape
        bias = relative_position_bias(rel_emb, s)
        h = x
        mi = 0
        for i in range(L):
            nx = t5_layer_norm(h, ln1[i])
            q = (nx @ attn_q[i]).reshape(b, s, H, DK)
            k = (nx @ attn_k[i]).reshape(b, s, H, DK)
            v = (nx @ attn_v[i]).reshape(b, s, H, DK)
            scores = jnp.einsum('bqhd,bkhd->bhqk', q, k) + bias
            attn = jax.nn.softmax(scores, axis=-1)
            ctx = jnp.einsum('bhqk,bkhd->bqhd', attn, v).reshape(b, s, H * DK)
            h = h + ctx @ attn_o[i]
            nx = t5_layer_norm(h, ln2[i])
            y = jax.nn.relu(nx @ ffn_wi[i]) @ ffn_wo[i]
            if i in MOE_LAYERS:
                y = y + moe_ffn(nx.reshape(-1, d), gate_w[mi], moe_w1[mi], moe_w2[mi]).reshape(b, s, d)
                mi += 1
            h = h + y
        return t5_layer_norm(h, ln_f)

    def _L1_attn_ref(x, W_qkv, W_out):
        import jax, jax.numpy as jnp
        import numpy as np
        DIM = 192
        NUM_HEADS = 12
        DIM_HEAD = 64
        SCALE = 1.0 / DIM_HEAD ** 0.5
        B, T, _ = x.shape
        qkv = x @ W_qkv.T
        qkv = qkv.reshape(B, T, 3, NUM_HEADS, DIM_HEAD)
        q, k, v = (qkv[:, :, i].transpose(0, 2, 1, 3) for i in range(3))
        logits = jnp.einsum('bhtd,bhsd->bhts', q, k) / SCALE
        att = jax.nn.softmax(logits, axis=-1)
        o = jnp.einsum('bhts,bhsd->bhtd', att, v)
        cat = o.transpose(0, 2, 1, 3).reshape(B, T, NUM_HEADS * DIM_HEAD)
        return cat @ W_out.T

    def _L1_ffn_ref(x, router_w, router_b, expert_w, expert_b):
        import jax, jax.numpy as jnp
        import numpy as np
        B, S, H = (4, 2048, 192)
        E, K = (8, 2)
        scores = jnp.einsum('bsh,eh->bse', x, router_w) + router_b
        probs = jax.nn.softmax(scores, axis=-1)
        top_probs, expert_ids = jax.lax.top_k(probs, K)
        y = jnp.einsum('bsh,edh->bsed', x, expert_w) + expert_b
        out_k = jnp.take_along_axis(y, expert_ids[..., None], axis=2)
        w = top_probs / (jnp.sum(top_probs, axis=-1, keepdims=True) + 1e-09)
        out = jnp.einsum('bsk,bskh->bsh', w, out_k)
        return out

    def _L2_attn_ref(x, W_attn, W_out, lambda_q1, lambda_k1, lambda_q2, lambda_k2):
        import jax, jax.numpy as jnp
        import numpy as np
        import math
        N_HEAD = 12
        N_EMBD = 192
        HEAD_DIM = N_EMBD // N_HEAD // 2
        DEPTH = 12
        LAMBDA_INIT = 0.8 - 0.6 * math.exp(-0.3 * DEPTH)

        def _sdpa_over_heads(q, k, v):
            scale = 1.0 / math.sqrt(q.shape[-1])
            s = jnp.einsum('bnqd,bnkd->bnqk', q, k) * scale
            a = jax.nn.softmax(s, axis=-1)
            return jnp.einsum('bnqk,bnkd->bnqd', a, v)
        B, N, D = x.shape
        H, hd = (N_HEAD, HEAD_DIM)
        qkv = x @ W_attn.T
        q, k, v = jnp.split(qkv, 3, axis=-1)
        q = q.reshape(B, N, H, 2, hd)
        k = k.reshape(B, N, H, 2, hd)
        v = v.reshape(B, N, H, 2 * hd)
        q1, q2 = (q[:, :, :, 0], q[:, :, :, 1])
        k1, k2 = (k[:, :, :, 0], k[:, :, :, 1])
        o1 = _sdpa_over_heads(q1, k1, v)
        o2 = _sdpa_over_heads(q2, k2, v)
        lam1 = jnp.exp(jnp.sum(lambda_q1 * lambda_k1))
        lam2 = jnp.exp(jnp.sum(lambda_q2 * lambda_k2))
        lam_full = lam1 - lam2 + LAMBDA_INIT
        y = (o1 - lam_full * o2) * (1.0 - LAMBDA_INIT)
        y = y.reshape(B, N, H * 2 * hd)
        return y @ W_out.T

    def _L2_ffn_ref(x, gate_w, gate_b, w1, b1, w2, b2):
        import jax, jax.numpy as jnp
        import numpy as np
        N_EMBD = 192
        N_EXPERTS = 8
        TOP_K = 2
        D_FF = 4 * N_EMBD
        B, T, C = x.shape
        x_flat = x.reshape(B * T, C)
        gate_logits = x_flat @ gate_w + gate_b
        gate_probs = jax.nn.softmax(gate_logits, axis=-1)
        topk_probs, topk_idx = jax.lax.top_k(gate_probs, TOP_K)
        topk_probs = topk_probs / jnp.sum(topk_probs, axis=-1, keepdims=True)
        h = jax.nn.gelu(jnp.einsum('nc,ech->neh', x_flat, w1) + b1[None], approximate=False)
        expert_out = jnp.einsum('neh,ehc->nec', h, w2) + b2[None]
        sel = jnp.take_along_axis(expert_out, topk_idx[:, :, None], axis=1)
        combined = jnp.sum(topk_probs[:, :, None] * sel, axis=1)
        return combined.reshape(B, T, C)

    def _L3_attn_ref(x, W_qkv, b_qkv):
        import jax, jax.numpy as jnp
        import numpy as np
        EMBED_DIM = 192
        SEQ_LEN = 256
        BATCH = 32
        ALPHA = 0.99

        def _decay_mask(sl: int, alpha: float) -> jnp.ndarray:
            i = jnp.arange(sl, dtype=jnp.float32)
            diff = i[:, None] - i[None, :]
            return jnp.where(diff >= 0, jnp.float32(alpha) ** diff, 0.0)
        bs, sl, d = x.shape
        qkv = x @ W_qkv + b_qkv
        q, k, v = jnp.split(qkv, 3, axis=-1)
        M = _decay_mask(sl, ALPHA)
        dim_sqrt = jnp.sqrt(jnp.float32(d))
        scores = jnp.einsum('bsd,btd->bst', q, k) / dim_sqrt * M
        return jnp.einsum('bst,btd->bsd', scores, v)

    def _L3_ffn_ref(hidden_states, router_w, router_b, corr_bias, gWg, gbg, gWu, gbu, gWd, gbd, sWg, sbg, sWu, sbu, sWd, sbd):
        import jax, jax.numpy as jnp
        import numpy as np
        H = 192
        I = 96
        E = 16
        G = 4
        TOPK_GROUP = 2
        TOP_K = 4
        SCALE = 2.5
        N_SHARED = 2
        IS = I * N_SHARED
        B, S = (1, 512)

        def _route(x, router_w, router_b, corr_bias):
            logits = x.astype(jnp.float32) @ router_w.T + router_b
            scores = jax.nn.sigmoid(logits)
            sfc = scores + corr_bias[None, :]
            grp = sfc.reshape(-1, G, E // G)
            group_scores = jax.lax.top_k(grp, 2)[0].sum(-1)
            _, gidx = jax.lax.top_k(group_scores, TOPK_GROUP)
            gmask = jax.nn.one_hot(gidx, G, dtype=sfc.dtype).sum(axis=1)
            score_mask = jnp.repeat(gmask, E // G, axis=-1)
            sfc = jnp.where(score_mask > 0, sfc, 0.0)
            _, idx = jax.lax.top_k(sfc, TOP_K)
            w = jnp.take_along_axis(scores, idx, axis=1)
            w = w / (w.sum(-1, keepdims=True) + 1e-20)
            return (idx, w * SCALE)

        def _forward(x3, router_w, router_b, corr_bias, gWg, gbg, gWu, gbu, gWd, gbd, sWg, sbg, sWu, sbu, sWd, sbd):
            orig_shape = x3.shape
            x = x3.reshape(-1, H)
            idx, w = _route(x, router_w, router_b, corr_bias)
            c = (jax.nn.one_hot(idx, E, dtype=w.dtype) * w[..., None]).sum(1)
            h = jax.nn.silu(jnp.einsum('th,ehi->tei', x, gWg) + gbg) * (jnp.einsum('th,ehi->tei', x, gWu) + gbu)
            out_e = jnp.einsum('tei,eih->teh', h, gWd) + gbd
            moe_out = jnp.einsum('te,teh->th', c, out_e)
            hs = jax.nn.silu(x @ sWg + sbg) * (x @ sWu + sbu)
            shared = hs @ sWd + sbd
            return (moe_out + shared).reshape(orig_shape)
        return _forward(hidden_states, router_w, router_b, corr_bias, gWg, gbg, gWu, gbu, gWd, gbd, sWg, sbg, sWu, sbu, sWd, sbd)
    h = _L0_tok_ref(x, L0_tok_W, L0_tok_b)
    h = h + _L0_attn_ref(_layernorm(h, axis=-1), L0_attn_pos_conv_w, L0_attn_pos_conv_b, L0_attn_ln0_g, L0_attn_ln0_b, L0_attn_Wq, L0_attn_bq, L0_attn_Wk, L0_attn_bk, L0_attn_Wv, L0_attn_bv, L0_attn_Wo, L0_attn_bo, L0_attn_ln1_g, L0_attn_ln1_b, L0_attn_W1, L0_attn_b1, L0_attn_W2, L0_attn_b2, L0_attn_ln2_g, L0_attn_ln2_b)
    h = h + _L0_ffn_ref(_layernorm(h, axis=-1), L0_ffn_attn_q, L0_ffn_attn_k, L0_ffn_attn_v, L0_ffn_attn_o, L0_ffn_ffn_wi, L0_ffn_ffn_wo, L0_ffn_ln1, L0_ffn_ln2, L0_ffn_ln_f, L0_ffn_rel_emb, L0_ffn_gate_w, L0_ffn_moe_w1, L0_ffn_moe_w2)
    h = h + _L1_attn_ref(_layernorm(h, axis=-1), L1_attn_W_qkv, L1_attn_W_out)
    h = h + _L1_ffn_ref(_layernorm(h, axis=-1), L1_ffn_router_w, L1_ffn_router_b, L1_ffn_expert_w, L1_ffn_expert_b)
    h = h + _L2_attn_ref(_layernorm(h, axis=-1), L2_attn_W_attn, L2_attn_W_out, L2_attn_lambda_q1, L2_attn_lambda_k1, L2_attn_lambda_q2, L2_attn_lambda_k2)
    h = h + _L2_ffn_ref(_layernorm(h, axis=-1), L2_ffn_gate_w, L2_ffn_gate_b, L2_ffn_w1, L2_ffn_b1, L2_ffn_w2, L2_ffn_b2)
    h = h + _L3_attn_ref(_layernorm(h, axis=-1), L3_attn_W_qkv, L3_attn_b_qkv)
    h = h + _L3_ffn_ref(_layernorm(h, axis=-1), L3_ffn_router_w, L3_ffn_router_b, L3_ffn_corr_bias, L3_ffn_gWg, L3_ffn_gbg, L3_ffn_gWu, L3_ffn_gbu, L3_ffn_gWd, L3_ffn_gbd, L3_ffn_sWg, L3_ffn_sbg, L3_ffn_sWu, L3_ffn_sbu, L3_ffn_sWd, L3_ffn_sbd)
    return h

_drawn_inputs = setup_inputs


def setup_inputs(seed=0):
    import zlib

    import numpy as np

    out = dict(_drawn_inputs(seed))
    spreads = {'L0_attn_pos_conv_b': (0.0, 0.1),
     'L0_attn_ln0_g': (1.0, 0.2),
     'L0_attn_ln0_b': (0.0, 0.1),
     'L0_attn_bq': (0.0, 0.8),
     'L0_attn_bk': (0.0, 2.0),
     'L0_attn_bv': (0.0, 0.1),
     'L0_attn_bo': (0.0, 0.1),
     'L0_attn_ln1_g': (1.0, 0.2),
     'L0_attn_ln1_b': (0.0, 0.1),
     'L0_attn_b1': (0.0, 0.1),
     'L0_attn_b2': (0.0, 0.1),
     'L0_attn_ln2_g': (1.0, 0.2),
     'L0_attn_ln2_b': (0.0, 0.1),
     'L0_ffn_ln1': (1.0, 0.2),
     'L0_ffn_ln2': (1.0, 0.2),
     'L0_ffn_ln_f': (1.0, 0.2),
     'L3_attn_b_qkv': (0.0, 0.1),
     'L3_ffn_router_b': (0.0, 0.1),
     'L3_ffn_corr_bias': (0.0, 0.1),
     'L3_ffn_gbg': (0.0, 0.712),
     'L3_ffn_gbu': (0.0, 0.733),
     'L3_ffn_gbd': (0.0, 0.444),
     'L3_ffn_sbg': (0.0, 0.8),
     'L3_ffn_sbu': (0.0, 0.8),
     'L3_ffn_sbd': (0.0, 0.59)}
    factors = {'L0_attn_Wq': 4.065,
     'L0_attn_Wk': 4.517,
     'L0_ffn_rel_emb': 5.141,
     'L2_attn_W_attn': 8.0,
     'L2_attn_W_out': 8.0,
     'L2_attn_lambda_q1': 8.0,
     'L2_attn_lambda_k1': 8.0,
     'L2_attn_lambda_q2': 8.0,
     'L2_attn_lambda_k2': 8.0,
     'L2_ffn_gate_b': 9.742,
     'L2_ffn_b1': 14.158,
     'L2_ffn_b2': 4.317}
    for name, (base, spread) in spreads.items():
        noise = np.random.default_rng([zlib.crc32(name.encode()), seed]).standard_normal(out[name].shape)
        drawn = base * np.exp(spread * noise) if base else spread * noise
        out[name] = jnp.asarray(drawn.astype(out[name].dtype))
    for name, factor in factors.items():
        out[name] = (out[name] * factor).astype(out[name].dtype)
    return out
```

```python
from contextlib import ExitStack, contextmanager

import numpy as np
import concourse.bass as bass
from concourse import mybir

F32 = mybir.dt.float32
I32 = mybir.dt.int32
ALU = mybir.AluOpType
ACT = mybir.ActivationFunctionType
AX = mybir.AxisListType

IMAGES, SIDE, PATCH, CHANNELS = 32, 96, 16, 3
LEN = (SIDE // PATCH) ** 2
GROUP = 3
TILE = GROUP * LEN
TILES = -(-IMAGES // GROUP)
PADDED = TILES * GROUP
TOKENS = TILES * TILE
DIM, FF = 192, 768
HALF = DIM // 2
BLOCKS = [[0, 1, 2, 3], [4, 5, 6, 7], [8, 9, 10]]
BLOCK_TILES = 4
FCH = FF // 128
PATCH_DIM = CHANNELS * PATCH * PATCH
OFF = -1e30
BANK = 512

CONV_GROUPS, CONV_CH, CONV_K = 16, 12, 128
CONV_J = 9
CONV_BLOCKS = LEN // CONV_J
CONV_D = 2 * CONV_BLOCKS - 1

MAGIC = float(0x5F3759DF)


@contextmanager
def stage_semaphores(nc):
    made = []

    def semaphore(name):
        made.append(nc.alloc_semaphore(name=name))
        return made[-1]

    yield semaphore
    nc.clear_and_free_semaphores(made)
    nc.all_engine_barrier()


class Loop:

    def __init__(self, sem, per, lead=0):
        self.sem, self.per, self.lead = sem, per, lead

    def at(self, turn, k):
        assert 1 - self.lead <= k <= self.per, (self.sem.name, k, self.per)
        return turn * self.per + (self.lead + k)


class Own:

    def __init__(self, sem):
        self.sem, self.n = sem, 0

    def up(self):
        self.n += 1
        return 1

    def restart(self):
        self.n = 0



def rsqrt_small(dve, own, y, v, t, i):
    dve.tensor_scalar(i, v.bitcast(I32), 1, None, ALU.logical_shift_right).then_inc(own.sem, own.up())
    dve.wait_ge(own.sem, own.n)
    dve.tensor_scalar(y.bitcast(I32), i, -1.0, MAGIC, ALU.mult, ALU.add).then_inc(own.sem, own.up())
    for _ in range(3):
        dve.wait_ge(own.sem, own.n)
        dve.tensor_tensor(t, y, v, ALU.mult).then_inc(own.sem, own.up())
        dve.wait_ge(own.sem, own.n)
        dve.scalar_tensor_tensor(t, t, -0.5, y, ALU.mult, ALU.mult).then_inc(own.sem, own.up())
        dve.wait_ge(own.sem, own.n)
        dve.scalar_tensor_tensor(y, t, 1.5, y, ALU.add, ALU.mult).then_inc(own.sem, own.up())
    dve.wait_ge(own.sem, own.n)


def normalise(dve, own, S, tiles, src, dst, eps, gain=None, shift=None, root=False, extra=None, done=None):
    n, a = len(tiles), tiles[0]
    for g in tiles:
        dve.bn_stats(S.stats[:, g, :], src[:, g, :]).then_inc(own.sem, own.up())
    dve.wait_ge(own.sem, own.n)
    for g in tiles:
        dve.bn_aggr(S.meanvar[:, g, :], S.stats[:, g, :]).then_inc(own.sem, own.up())
    dve.wait_ge(own.sem, own.n)
    mean, var = S.meanvar[:, a:a + n, 0], S.meanvar[:, a:a + n, 1]
    v, y, t, i = S.small[:, 0, 0:n], S.rstd[:, a:a + n], S.small[:, 1, 0:n], S.smalli[:, 0:n]
    if root:
        dve.tensor_tensor(t, mean, mean, ALU.mult).then_inc(own.sem, own.up())
        dve.wait_ge(own.sem, own.n)
        dve.scalar_tensor_tensor(v, t, eps, var, ALU.add, ALU.add).then_inc(own.sem, own.up())
    else:
        dve.tensor_scalar(v, var, eps, None, ALU.add).then_inc(own.sem, own.up())
    dve.wait_ge(own.sem, own.n)
    rsqrt_small(dve, own, y, v, t, i)
    if gain is None and extra is None:
        for g in tiles:
            ins = dve.tensor_scalar(dst[:, g, :], src[:, g, :], S.meanvar[:, g, 0:1], S.rstd[:, g:g + 1],
                                    ALU.subtract, ALU.mult)
            ins.then_inc(done, 1) if done is not None else ins.then_inc(own.sem, own.up())
        return
    if root:
        for g in tiles:
            ins = dve.scalar_tensor_tensor(dst[:, g, :], src[:, g, :], S.rstd[:, g:g + 1], gain,
                                           ALU.mult, ALU.mult)
            ins.then_inc(done, 1) if done is not None else ins.then_inc(own.sem, own.up())
        return
    for g in tiles:
        dve.scalar_tensor_tensor(dst[:, g, :], src[:, g, :], S.meanvar[:, g, 0:1], gain,
                                 ALU.subtract, ALU.mult).then_inc(own.sem, own.up())
    dve.wait_ge(own.sem, own.n)
    for g in tiles:
        ins = dve.scalar_tensor_tensor(dst[:, g, :], dst[:, g, :], S.rstd[:, g:g + 1], shift,
                                       ALU.mult, ALU.add)
        ins.then_inc(done, 1) if done is not None else ins.then_inc(own.sem, own.up())



class Heads:

    def __init__(self, rows, chunks, in_chunk, per_bank, slot, out_chunks, out_rows, v_heads, v_width, v_tiles,
                 scale):
        self.rows, self.chunks, self.in_chunk, self.per_bank = rows, chunks, in_chunk, per_bank
        self.slot, self.out_chunks, self.out_rows = slot, out_chunks, out_rows
        self.v_heads, self.v_width, self.v_tiles = v_heads, v_width, v_tiles
        self.scale = scale
        self.in_unit = 2 * per_bank
        self.units = chunks * in_chunk // self.in_unit
        self.width = per_bank * TILE
        self.outs = out_chunks // self.units

    def bank(self, unit, i):
        first = unit * self.in_unit + i * self.per_bank
        return first // self.in_chunk, first % self.in_chunk * TILE


SMALL = Heads(96, 2, 6, 3, 32, 4, 96, 12, 16, 1, 16 ** -0.5)
LARGE = Heads(128, 6, 2, 2, 64, 6, 128, 12, 64, 2, 1.0)


def pe_transpose(pe, S, A, turn, blk, src, ready, done, out):
    for g in BLOCKS[blk]:
        pe.wait_ge(ready.sem, ready.at(turn, g + 1))
        if g >= 2:
            pe.wait_ge(out.sem, out.at(turn, g - 1))
        for c in range(2):
            ins = pe.transpose(S.ps[0:HALF, 4 + g % 2, c * TILE:(c + 1) * TILE],
                               src[:, g, c * HALF:(c + 1) * HALF], S.ident[0:TILE, 0:TILE])
        ins.then_inc(done.sem, 1)


def act_transposed(act, S, A, turn, blk, done, out):
    for g in BLOCKS[blk]:
        act.wait_ge(done.sem, done.at(turn, g + 1))
        act.activation(S.xt[:, :, g * TILE:(g + 1) * TILE],
                       S.ps[0:HALF, 4 + g % 2, 0:2 * TILE].rearrange("p (c t) -> p c t", c=2),
                       ACT.Copy).then_inc(out.sem, 1)


def pe_qkv(pe, S, A, turn, blk):
    hd, tiles = A.heads, BLOCKS[blk]
    c0, cols = tiles[0] * TILE, len(tiles) * TILE
    pe.wait_ge(A.w_qkv.sem, A.w_qkv.at(turn, A.w_qkv.per))
    pe.wait_ge(A.xt_out.sem, A.xt_out.at(turn, tiles[-1] + 1))
    for m in range(2 * hd.chunks):
        c, keys = m // 2, m % 2
        w = A.wk if keys else A.wq
        if m >= 4:
            pe.wait_ge((A.k_out if keys else A.q_out).sem, (A.k_out if keys else A.q_out).at(turn, blk * hd.chunks + (m - 4) // 2 + 1))
        for kc in range(2):
            ins = pe.matmul(S.ps[0:hd.rows, m % 4, 0:cols], w[:, kc, c * hd.rows:(c + 1) * hd.rows],
                            S.xt[:, kc, c0:c0 + cols], start=kc == 0, stop=kc == 1)
        ins.then_inc(A.pe_qk.sem, 1)
    n = tiles[0] * hd.v_tiles
    wide = hd.v_heads * hd.v_width // hd.v_tiles
    if blk:
        pe.wait_ge(A.y_read.sem, A.y_read.at(turn, tiles[0]))
    else:
        A.pe_banks_free(pe, turn)
    for g in tiles:
        for vt in range(hd.v_tiles):
            if n >= tiles[0] * hd.v_tiles + 2:
                pe.wait_ge(A.v_out.sem, A.v_out.at(turn, n - 1))
            for kc in range(2):
                ins = pe.matmul(S.ps[0:TILE, 6 + n % 2, 0:wide], S.xt[:, kc, g * TILE:(g + 1) * TILE],
                                A.wv[:, kc, vt * wide:(vt + 1) * wide], start=kc == 0, stop=kc == 1)
            ins.then_inc(A.pe_v.sem, 1)
            n += 1


def pe_attend(pe, S, A, turn, blk):
    hd, tiles = A.heads, BLOCKS[blk]
    base, count = tiles[0] * hd.units, len(tiles) * hd.units
    pb, w = hd.per_bank, hd.width
    pe.wait_ge(A.q_out.sem, A.q_out.at(turn, (blk + 1) * hd.chunks))
    pe.wait_ge(A.k_out.sem, A.k_out.at(turn, (blk + 1) * hd.chunks))
    for s in range(count + 3):
        if s < count:
            n, lg, u = base + s, s // hd.units, s % hd.units
            if s >= 2:
                pe.wait_ge(A.s_read.sem, A.s_read.at(turn, n - 1))
            for i in range(2):
                c, k0 = hd.bank(u, i)
                ins = pe.matmul(S.ps[0:TILE, 2 * (s % 2) + i, 0:w], S.qt[0:hd.rows, c, lg * TILE:(lg + 1) * TILE],
                                A.kb[:, c, lg, k0:k0 + w], start=True, stop=True)
            ins.then_inc(A.pe_s.sem, 1)
        if 2 <= s < count + 2:
            r = s - 2
            pe.wait_ge(A.p_norm.sem, A.p_norm.at(turn, base + r + 1))
            if r:
                pe.wait_ge(A.pt_out.sem, A.pt_out.at(turn, base + r))
            for h in range(2 * pb):
                ins = pe.transpose(S.ps[0:TILE, 4 + h // pb, h % pb * TILE:(h % pb + 1) * TILE],
                                   S.p[:, r % 4, h * TILE:(h + 1) * TILE], S.ident[0:TILE, 0:TILE])
            ins.then_inc(A.pe_pt.sem, 1)
        if s >= 3:
            r = s - 3
            lg, u = r // hd.units, r % hd.units
            pe.wait_ge(A.pt_out.sem, A.pt_out.at(turn, base + r + 1))
            if r == 0:
                pe.wait_ge(A.v_out.sem, A.v_out.at(turn, (tiles[-1] + 1) * hd.v_tiles))
            if r >= 2:
                pe.wait_ge(A.o_out.sem, A.o_out.at(turn, base + r - 1))
            for h in range(2 * pb):
                vh, j, i = u * 2 * pb + h, h % pb, h // pb
                ins = pe.matmul(S.ps[j * hd.slot:(j + 1) * hd.slot, 6 + r % 2, i * TILE:(i + 1) * TILE],
                                S.v[:, lg, vh * hd.slot:(vh + 1) * hd.slot], S.pt[:, r % 2, h * TILE:(h + 1) * TILE],
                                start=True, stop=True)
            ins.then_inc(A.pe_o.sem, 1)


def pe_project(pe, S, A, turn, blk):
    hd, tiles = A.heads, BLOCKS[blk]
    pe.wait_ge(A.w_o.sem, A.w_o.at(turn, A.w_o.per))
    pe.wait_ge(A.o_out.sem, A.o_out.at(turn, (tiles[-1] + 1) * hd.units))
    for lg, g in enumerate(tiles):
        if lg >= 2:
            pe.wait_ge(A.y_read.sem, A.y_read.at(turn, g - 1))
        for c in range(hd.out_chunks):
            ins = pe.matmul(S.ps[0:TILE, 6 + lg % 2, 0:DIM], S.ot[0:hd.out_rows, c, lg * TILE:(lg + 1) * TILE],
                            A.wo[:, c, :], start=c == 0, stop=c == hd.out_chunks - 1)
        ins.then_inc(A.pe_y.sem, 1)


def act_qkv(act, S, A, turn, blk):
    hd, tiles = A.heads, BLOCKS[blk]
    cols = len(tiles) * TILE
    for c in range(hd.chunks):
        act.wait_ge(A.pe_qk.sem, A.pe_qk.at(turn, (blk * hd.chunks + c) * 2 + 1))
        src, dst = S.ps[0:hd.rows, 2 * c % 4, 0:cols], S.qt[0:hd.rows, c, 0:cols]
        ins = act.activation(dst, src, ACT.Identity, bias=A.bq[:, c:c + 1]) if A.biased else \
            act.activation(dst, src, ACT.Copy)
        ins.then_inc(A.q_out.sem, 1)
    if not A.biased:
        heads = hd.v_heads // hd.v_tiles
        for n in range(tiles[0] * hd.v_tiles, (tiles[-1] + 1) * hd.v_tiles):
            act.wait_ge(A.pe_v.sem, A.pe_v.at(turn, n + 1))
            lg, vt = n // hd.v_tiles - tiles[0], n % hd.v_tiles
            dst = S.v[:, lg, 0:hd.v_heads * hd.slot].rearrange("p (h d) -> p h d", d=hd.slot)[:, vt * heads:(vt + 1) * heads, 0:hd.v_width]
            act.activation(dst, S.ps[0:TILE, 6 + n % 2, 0:heads * hd.v_width].rearrange("p (h d) -> p h d", h=heads),
                           ACT.Copy).then_inc(A.v_out.sem, 1)


def act_attend(act, S, A, turn, blk):
    hd, tiles = A.heads, BLOCKS[blk]
    base, count = tiles[0] * hd.units, len(tiles) * hd.units
    for s in range(count + 2):
        if s < count:
            act.wait_ge(A.s_max.sem, A.s_max.at(turn, base + s + 1))
            for h in range(hd.in_unit):
                tile = S.p[:, s % 4, h * TILE:(h + 1) * TILE]
                ins = act.activation(tile, tile, ACT.Exp, bias=S.nmax[:, s % 4, h:h + 1],
                                     accum_out=S.sums[:, s % 4, h:h + 1])
            ins.then_inc(A.p_exp.sem, 1)
        if s >= 2:
            r = s - 2
            act.wait_ge(A.pe_pt.sem, A.pe_pt.at(turn, base + r + 1))
            act.activation(S.pt[:, r % 2, 0:2 * hd.width].rearrange("p (b n) -> p b n", b=2),
                           S.ps[0:TILE, 4:6, 0:hd.width], ACT.Copy).then_inc(A.pt_out.sem, 1)


def dve_qkv(dve, own, S, A, turn, blk):
    hd, tiles = A.heads, BLOCKS[blk]
    cols = len(tiles) * TILE
    for c in range(hd.chunks):
        dve.wait_ge(A.pe_qk.sem, A.pe_qk.at(turn, (blk * hd.chunks + c) * 2 + 2))
        src = S.ps[0:hd.rows, (2 * c + 1) % 4, 0:cols].rearrange("p (g t) -> p g t", t=TILE)
        for j in range(hd.in_chunk):
            dst = A.kb[:, c, 0:len(tiles), j * TILE:(j + 1) * TILE]
            if A.biased:
                ins = dve.tensor_scalar(dst, src, A.bk[:, c:c + 1], S.hmask[0:hd.rows, j:j + 1], ALU.add, ALU.mult)
            else:
                ins = dve.tensor_scalar(dst, src, S.hmask[0:hd.rows, j:j + 1], None, ALU.mult)
        ins.then_inc(A.k_out.sem, 1)
    if A.biased:
        for lg, g in enumerate(tiles):
            dve.wait_ge(A.pe_v.sem, A.pe_v.at(turn, g + 1))
            dst = S.v[:, lg, 0:hd.v_heads * hd.slot].rearrange("p (h d) -> p h d", d=hd.slot)[:, :, 0:hd.v_width]
            dve.tensor_tensor(dst, S.ps[0:TILE, 6 + g % 2, 0:DIM].rearrange("p (h d) -> p h d", d=hd.v_width),
                              A.bv.rearrange("p (h d) -> p h d", d=hd.v_width), ALU.add).then_inc(A.v_out.sem, 1)


def dve_attend(dve, own, S, A, turn, blk):
    hd, tiles = A.heads, BLOCKS[blk]
    base, count = tiles[0] * hd.units, len(tiles) * hd.units
    wide = 2 * hd.width
    for s in range(count + 3):
        if s < count:
            n, u = base + s, s % hd.units
            dve.wait_ge(A.pe_s.sem, A.pe_s.at(turn, n + 1))
            if s >= 4:
                dve.wait_ge(A.pe_pt.sem, A.pe_pt.at(turn, n - 3))
            p = S.p[:, s % 4, 0:wide]
            dve.scalar_tensor_tensor(p.rearrange("p (b n) -> p b n", b=2),
                                     S.ps[0:TILE, 2 * (s % 2):2 * (s % 2) + 2, 0:hd.width], hd.scale,
                                     A.mask(u), ALU.mult, ALU.add).then_inc(A.s_read.sem, 1)
            dve.wait_ge(A.s_read.sem, A.s_read.at(turn, n + 1))
            dve.tensor_reduce(S.nmax[:, s % 4, 0:hd.in_unit], p.rearrange("p (h t) -> p h t", t=TILE), AX.X, ALU.max,
                              negate=True).then_inc(A.s_max.sem, 1)
        if s >= 3:
            r = s - 3
            lg, u = r // hd.units, r % hd.units
            dve.wait_ge(A.pe_o.sem, A.pe_o.at(turn, base + r + 1))
            dve.tensor_copy(S.ot[0:hd.out_rows, u * hd.outs:(u + 1) * hd.outs, lg * TILE:(lg + 1) * TILE],
                            S.ps[0:hd.out_rows, 6 + r % 2, 0:hd.outs * TILE].rearrange("p (c t) -> p c t", t=TILE)
                            ).then_inc(A.o_out.sem, 1)
        if 1 <= s <= count:
            r = s - 1
            dve.wait_ge(A.p_exp.sem, A.p_exp.at(turn, base + r + 1))
            dve.reciprocal(S.recs[:, r % 4, 0:hd.in_unit], S.sums[:, r % 4, 0:hd.in_unit]).then_inc(own.sem, own.up())
            dve.wait_ge(own.sem, own.n)
            p = S.p[:, r % 4, 0:wide].rearrange("p (h t) -> p h t", t=TILE)
            dve.tensor_tensor(p, p, S.recs[:, r % 4, 0:hd.in_unit].unsqueeze(2).to_broadcast([TILE, hd.in_unit, TILE]),
                              ALU.mult).then_inc(A.p_norm.sem, 1)



def pe_ff(pe, S, F, turn, blk, bank_free, load_turn=None):
    tiles = BLOCKS[blk]
    c0, cols = tiles[0] * TILE, len(tiles) * TILE
    load_turn = turn if load_turn is None else load_turn
    pe.wait_ge(F.w_1.sem, F.w_1.at(load_turn, F.w_1.per))
    for m in range(FCH):
        if m >= 4:
            pe.wait_ge(F.h_out.sem, F.h_out.at(turn, blk * FCH + m - 3))
        for kc in range(2):
            ins = pe.matmul(S.ps[:, m % 4, 0:cols], F.w1[:, kc, m * 128:(m + 1) * 128], S.xt[:, kc, c0:c0 + cols],
                            start=kc == 0, stop=kc == 1)
        ins.then_inc(F.pe_h.sem, 1)
    pe.wait_ge(F.w_2.sem, F.w_2.at(load_turn, F.w_2.per))
    pe.wait_ge(F.h_out.sem, F.h_out.at(turn, (blk + 1) * FCH))
    if blk == 0:
        bank_free()
    for lg, g in enumerate(tiles):
        if g >= 2:
            pe.wait_ge(F.y_read.sem, F.y_read.at(turn, g - 1))
        for c in range(FCH):
            ins = pe.matmul(S.ps[0:TILE, 6 + g % 2, 0:DIM], S.h1[:, c, lg * TILE:(lg + 1) * TILE], F.w2[:, c, :],
                            start=c == 0, stop=c == FCH - 1)
        ins.then_inc(F.pe_y.sem, 1)


def act_ff(act, S, F, turn, blk, func):
    cols = len(BLOCKS[blk]) * TILE
    for m in range(FCH):
        act.wait_ge(F.pe_h.sem, F.pe_h.at(turn, blk * FCH + m + 1))
        bias = F.b1[:, m:m + 1] if F.b1 is not None else 0.0
        act.activation(S.h1[:, m, 0:cols], S.ps[:, m % 4, 0:cols], func, bias=bias).then_inc(F.h_out.sem, 1)


def pe_router(pe, S, R, E, w):
    for g in range(TILES):
        for kc in range(2):
            ins = pe.matmul(S.ps[0:TILE, 4, g * E:(g + 1) * E], S.xt[:, kc, g * TILE:(g + 1) * TILE], w[:, kc, :],
                            start=kc == 0, stop=kc == 1)
    ins.then_inc(R.logits_done.sem, 1)


def dve_top_mask(dve, own, S, R, mask, scores, E, K, n=TILES):
    mine = scores.unsqueeze(3).to_broadcast([TILE, n, E, E])
    other = scores.unsqueeze(2).to_broadcast([TILE, n, E, E])
    gt = R.gt[:, 0:n * E * E].rearrange("p (n j k) -> p n j k", j=E, k=E)
    eq = R.eq[:, 0:n * E * E].rearrange("p (n j k) -> p n j k", j=E, k=E)
    dve.tensor_tensor(gt, other, mine, ALU.is_gt).then_inc(own.sem, own.up())
    dve.tensor_tensor(eq, other, mine, ALU.is_equal).then_inc(own.sem, own.up())
    dve.wait_ge(own.sem, own.n)
    dve.tensor_tensor(eq, eq, R.before[:, 0:E, 0:E].unsqueeze(1).to_broadcast([TILE, n, E, E]), ALU.mult).then_inc(own.sem, own.up())
    dve.wait_ge(own.sem, own.n)
    dve.tensor_tensor(gt, gt, eq, ALU.add).then_inc(own.sem, own.up())
    dve.wait_ge(own.sem, own.n)
    dve.tensor_reduce(mask, gt, AX.X, ALU.add).then_inc(own.sem, own.up())
    dve.wait_ge(own.sem, own.n)
    dve.tensor_scalar(mask, mask, float(K), None, ALU.is_lt).then_inc(own.sem, own.up())
    dve.wait_ge(own.sem, own.n)


def dve_route(dve, own, S, R, turn, E, K, bias=None, whole=True, eps=0.0):
    dve.wait_ge(R.logits_done.sem, R.logits_done.at(turn, 1))
    lg, ex, cw, mask, col = R.logits, R.ex, R.cw, R.mask, R.col
    src = S.ps[0:TILE, 4, 0:TILES * E].rearrange("p (g e) -> p g e", e=E)
    if bias is None:
        dve.tensor_copy(lg, src).then_inc(own.sem, own.up())
    else:
        dve.tensor_tensor(lg, src, bias.unsqueeze(1).to_broadcast([TILE, TILES, E]), ALU.add).then_inc(own.sem, own.up())
    dve.wait_ge(own.sem, own.n)

    def wide(c):
        return c.unsqueeze(2).to_broadcast([TILE, TILES, E])

    dve.tensor_reduce(col, lg, AX.X, ALU.max).then_inc(own.sem, own.up())
    dve.wait_ge(own.sem, own.n)
    dve.tensor_tensor(ex, lg, wide(col), ALU.subtract).then_inc(R.shifted.sem, 1)
    if not whole:
        dve_top_mask(dve, own, S, R, mask, lg, E, K)
    dve.wait_ge(R.exped.sem, R.exped.at(turn, 1))
    if whole:
        dve.tensor_reduce(col, ex, AX.X, ALU.add).then_inc(own.sem, own.up())
        dve.wait_ge(own.sem, own.n)
        dve.reciprocal(col, col).then_inc(own.sem, own.up())
        dve.wait_ge(own.sem, own.n)
        dve.tensor_tensor(ex, ex, wide(col), ALU.mult).then_inc(own.sem, own.up())
        dve.wait_ge(own.sem, own.n)
        dve_top_mask(dve, own, S, R, mask, ex, E, K)
    dve.tensor_tensor(ex, ex, mask, ALU.mult).then_inc(own.sem, own.up())
    dve.wait_ge(own.sem, own.n)
    dve.tensor_reduce(col, ex, AX.X, ALU.add).then_inc(own.sem, own.up())
    dve.wait_ge(own.sem, own.n)
    dve.tensor_scalar(col, col, eps, None, ALU.add).then_inc(own.sem, own.up())
    dve.wait_ge(own.sem, own.n)
    dve.reciprocal(col, col).then_inc(own.sem, own.up())
    dve.wait_ge(own.sem, own.n)
    dve.tensor_tensor(cw, ex, wide(col), ALU.mult).then_inc(own.sem, own.up())
    dve.wait_ge(own.sem, own.n)


def act_route(act, S, R, turn):
    act.wait_ge(R.shifted.sem, R.shifted.at(turn, 1))
    act.activation(R.ex, R.ex, ACT.Exp).then_inc(R.exped.sem, 1)


def router_buffers(nc, ctx, sem, prefix, E, per=1):
    R = Names()

    def sb(name, shape):
        return ctx.enter_context(nc.sbuf_tensor(prefix + name, shape, F32))

    R.gt, R.eq = sb("gt", [TILE, TILES * E * E])[:, :], sb("eq", [TILE, TILES * E * E])[:, :]
    R.before = sb("before", [TILE, E, E])
    R.logits, R.ex, R.cw, R.mask = (sb(n, [TILE, TILES, E])[:, :, :] for n in ("logits_sb", "ex", "cw", "top"))
    R.col = sb("col", [TILE, TILES])[:, :]
    R.logits_done, R.shifted, R.exped = (
        Loop(sem(prefix + n), per) for n in ("logits_done", "shifted", "exped"))
    return R


def dve_add_scaled(dve, S, F, turn, into, weight, tiles):
    for g in tiles:
        dve.wait_ge(F.pe_y.sem, F.pe_y.at(turn, g + 1))
        dve.wait_ge(F.y_read.sem, F.y_read.at(turn, g + 1 - TILES))
        dve.scalar_tensor_tensor(into[:, g, :], S.ps[0:TILE, 6 + g % 2, 0:DIM], weight(g), into[:, g, :],
                                 ALU.mult, ALU.add).then_inc(F.y_read.sem, 1)


def experts(nc, ctx, sem, prefix, biased):
    def sb(name, shape):
        return ctx.enter_context(nc.sbuf_tensor(prefix + name, shape, F32))

    def loop(name, per, lead=0):
        return Loop(sem(prefix + name), per, lead)

    pe_h, h_out, pe_y = loop("hidden", 3 * FCH), loop("hidden_out", 3 * FCH), loop("ff_done", TILES)
    y_read = loop("ff_read", TILES, lead=TILES)
    both = []
    for k in range(2):
        F = Names()
        F.w1, F.w2 = sb(f"w1_{k}", [HALF, 2, FF]), sb(f"w2_{k}", [128, FCH, DIM])
        F.b1 = sb(f"b1_{k}", [128, FCH]) if biased else None
        F.w_1, F.w_2 = loop(f"w1_loaded_{k}", 32 if biased else 16), loop(f"w2_loaded_{k}", 16)
        F.pe_h, F.h_out, F.pe_y, F.y_read = pe_h, h_out, pe_y, y_read
        both.append(F)
    return both


def sp_expert(sp, F, w1, w2, b1=None):
    sp.dma_start(F.w1[:, :, :], w1).then_inc(F.w_1.sem, 16)
    if b1 is not None:
        sp.dma_start(F.b1[:, :], b1).then_inc(F.w_1.sem, 16)
    sp.dma_start(F.w2[:, :, :], w2).then_inc(F.w_2.sem, 16)



class Names:
    pass


def stage_small_attention(nc, S, IN, layers=12):
    A, F = Names(), Names()
    with ExitStack() as ctx:
        sem = ctx.enter_context(stage_semaphores(nc))
        def sb(name, shape):
            return ctx.enter_context(nc.sbuf_tensor("sa_" + name, shape, F32))

        def loop(name, per):
            return Loop(sem("sa_" + name), per)

        hd = A.heads = SMALL
        A.biased = True
        gate = sb("qkv", [HALF, 2, 3 * DIM])
        A.wq, A.wk, A.wv = gate[:, :, 0:DIM], gate[:, :, DIM:2 * DIM], gate[:, :, 2 * DIM:3 * DIM]
        qkb = sb("qk_bias", [HALF, 4])
        A.bq, A.bk = qkb[:, 0:2], qkb[:, 2:4]
        vo_bias = sb("vo_bias", [TILE, 2 * DIM])
        A.bv = vo_bias[:, 0:DIM]
        A.wo = sb("wo", [hd.out_rows, hd.out_chunks, DIM])
        ln1 = sb("ln1", [TILE, 2 * DIM])
        F.w1 = sb("w1", [HALF, 2, FF])
        F.b1 = sb("b1", [128, FCH])
        F.w2 = sb("w2", [128, FCH, DIM])
        ln2 = sb("ln2", [TILE, 3 * DIM])
        A.kb = sb("keys_apart", [hd.rows, hd.chunks, BLOCK_TILES, hd.in_chunk * TILE])
        plus = sb("x_plus_bias", [TILE, TILES, DIM])
        total = sb("sum", [TILE, TILES, DIM])
        A.mask = lambda u: S.mask[:, 0:2 * hd.width].rearrange("p (b n) -> p b n", b=2)

        units = TILES * hd.units
        A.w_qkv, A.w_o, F.w_1, F.w_2 = loop("qkv_loaded", 48), loop("wo_loaded", 32), loop("w1_loaded", 32), loop("w2_loaded", 32)
        x_ready, A.pe_xt, A.xt_out = loop("x_ready", TILES), loop("x_turned", TILES), loop("xt_out", TILES)
        A.pe_qk, A.q_out, A.k_out = loop("qk_done", 6 * hd.chunks), loop("q_out", 3 * hd.chunks), loop("k_out", 3 * hd.chunks)
        A.pe_v, A.v_out = loop("v_done", TILES), loop("v_out", TILES)
        A.pe_s, A.s_read, A.s_max, A.p_exp = (loop(n, units) for n in ("scores", "scores_read", "max", "exp"))
        A.p_norm, A.pe_pt, A.pt_out, A.pe_o, A.o_out = (loop(n, units) for n in ("probs", "probs_turned", "pt_out", "heads_done", "o_out"))
        A.pe_y, A.y_read, x1_ready = loop("projected", TILES), loop("projected_read", TILES), loop("x1_ready", TILES)
        pe_xt1, xt1_out = loop("x1_turned", TILES), loop("xt1_out", TILES)
        F.pe_h, F.h_out = loop("hidden", 3 * FCH), loop("hidden_out", 3 * FCH)
        F.pe_y, F.y_read = loop("ff_done", TILES), loop("ff_read", TILES)
        plus_ready = loop("plus_ready", 6)
        own_dve = sem("sa_dve_own")
        block = ctx.enter_context(nc.Block())

        @block.sync
        def _(sp):
            def load_qkv(t):
                sp.dma_start(gate[:, :, :], IN["a_qkv"][t]).then_inc(A.w_qkv.sem, 16)
                sp.dma_start(qkb[:, :], IN["a_qkb"][t]).then_inc(A.w_qkv.sem, 16)
                sp.dma_start(vo_bias[:, :], IN["a_vob"][t]).then_inc(A.w_qkv.sem, 16)

            def load_o(t):
                sp.dma_start(A.wo[:, :, :], IN["a_wo"][t]).then_inc(A.w_o.sem, 16)
                sp.dma_start(ln1[:, :], IN["a_ln1"][t]).then_inc(A.w_o.sem, 16)

            def load_1(t):
                sp.dma_start(F.w1[:, :, :], IN["a_w1"][t]).then_inc(F.w_1.sem, 16)
                sp.dma_start(F.b1[:, :], IN["a_b1"][t]).then_inc(F.w_1.sem, 16)

            def load_2(t):
                sp.dma_start(F.w2[:, :, :], IN["a_w2"][t]).then_inc(F.w_2.sem, 16)
                sp.dma_start(ln2[:, :], IN["a_ln2"][t]).then_inc(F.w_2.sem, 16)

            load_qkv(0), load_o(0), load_1(0), load_2(0)
            with sp.Fori(0, layers - 1) as t:
                sp.wait_ge(A.pe_y.sem, A.pe_y.at(t, TILES))
                sp.wait_ge(plus_ready.sem, plus_ready.at(t, 3))
                load_qkv(t + 1)
                sp.wait_ge(x1_ready.sem, x1_ready.at(t, TILES))
                load_o(t + 1)
                sp.wait_ge(F.h_out.sem, F.h_out.at(t, 3 * FCH))
                load_1(t + 1)
                sp.wait_ge(x_ready.sem, x_ready.at(t + 1, TILES))
                load_2(t + 1)

        @block.tensor
        def _(pe):
            with pe.Fori(0, layers) as t:
                A.pe_banks_free = lambda eng, turn: eng.wait_ge(x_ready.sem, x_ready.at(turn, TILES))
                for b in range(3):
                    pe_transpose(pe, S, A, t, b, S.x, x_ready, A.pe_xt, A.xt_out)
                    pe_qkv(pe, S, A, t, b)
                    pe_attend(pe, S, A, t, b)
                    pe_project(pe, S, A, t, b)
                for b in range(3):
                    pe_transpose(pe, S, A, t, b, S.x, x1_ready, pe_xt1, xt1_out)
                    pe.wait_ge(xt1_out.sem, xt1_out.at(t, BLOCKS[b][-1] + 1))
                    pe_ff(pe, S, F, t, b, lambda: pe.wait_ge(A.y_read.sem, A.y_read.at(t, TILES)))

        @block.scalar
        def _(act):
            with act.Fori(0, layers) as t:
                for b in range(3):
                    act_transposed(act, S, A, t, b, A.pe_xt, A.xt_out)
                    act_qkv(act, S, A, t, b)
                    act_attend(act, S, A, t, b)
                for b in range(3):
                    act_transposed(act, S, A, t, b, pe_xt1, xt1_out)
                    act_ff(act, S, F, t, b, ACT.Gelu)

        @block.gpsimd
        def _(pool):
            def add(tiles, bias, done):
                pool.tensor_tensor(plus[:, tiles[0]:tiles[-1] + 1, :], S.x[:, tiles[0]:tiles[-1] + 1, :],
                                   bias.unsqueeze(1).to_broadcast([TILE, len(tiles), DIM]), ALU.add).then_inc(plus_ready.sem, 1)

            with pool.Fori(0, layers) as t:
                pool.wait_ge(A.w_qkv.sem, A.w_qkv.at(t, A.w_qkv.per))
                for b in range(3):
                    pool.wait_ge(x_ready.sem, x_ready.at(t, BLOCKS[b][-1] + 1))
                    add(BLOCKS[b], vo_bias[:, DIM:2 * DIM], plus_ready)
                pool.wait_ge(F.w_2.sem, F.w_2.at(t, F.w_2.per))
                for b in range(3):
                    pool.wait_ge(x1_ready.sem, x1_ready.at(t, BLOCKS[b][-1] + 1))
                    add(BLOCKS[b], ln2[:, 0:DIM], plus_ready)

        @block.vector
        def _(dve):
            own = Own(own_dve)
            dve.nop().then_inc(x_ready.sem, TILES)
            with dve.Fori(0, layers) as t:
                dve.wait_ge(A.w_qkv.sem, A.w_qkv.at(t, A.w_qkv.per))
                for b in range(3):
                    dve_qkv(dve, own, S, A, t, b)
                    dve_attend(dve, own, S, A, t, b)
                    dve.wait_ge(plus_ready.sem, plus_ready.at(t, b + 1))
                    for g in BLOCKS[b]:
                        dve.wait_ge(A.pe_y.sem, A.pe_y.at(t, g + 1))
                        dve.tensor_tensor(total[:, g, :], S.ps[0:TILE, 6 + g % 2, 0:DIM], plus[:, g, :],
                                          ALU.add).then_inc(A.y_read.sem, 1)
                    dve.wait_ge(A.y_read.sem, A.y_read.at(t, BLOCKS[b][-1] + 1))
                    dve.wait_ge(A.w_o.sem, A.w_o.at(t, A.w_o.per))
                    normalise(dve, own, S, BLOCKS[b], total, S.x, 1e-5, ln1[:, 0:DIM], ln1[:, DIM:2 * DIM],
                              done=x1_ready.sem)
                dve.wait_ge(F.w_2.sem, F.w_2.at(t, F.w_2.per))
                for b in range(3):
                    dve.wait_ge(plus_ready.sem, plus_ready.at(t, 3 + b + 1))
                    for g in BLOCKS[b]:
                        dve.wait_ge(F.pe_y.sem, F.pe_y.at(t, g + 1))
                        dve.tensor_tensor(total[:, g, :], S.ps[0:TILE, 6 + g % 2, 0:DIM], plus[:, g, :],
                                          ALU.add).then_inc(F.y_read.sem, 1)
                    dve.wait_ge(F.y_read.sem, F.y_read.at(t, BLOCKS[b][-1] + 1))
                    normalise(dve, own, S, BLOCKS[b], total, S.x, 1e-5, ln2[:, DIM:2 * DIM], ln2[:, 2 * DIM:3 * DIM],
                              done=x_ready.sem)
                dve.sem_clear(own.sem)
                own.restart()
            dve.wait_ge(x_ready.sem, x_ready.at(layers, TILES))
            dve.tensor_tensor(S.h[:, :, :], S.h[:, :, :], S.x[:, :, :], ALU.add).then_inc(own.sem, own.up())
            dve.wait_ge(own.sem, own.n)


def attention_buffers(nc, ctx, sem, prefix, hd, parts_w, parts_o):
    A = Names()

    def loop(name, per, lead=0):
        return Loop(sem(prefix + name), per, lead)

    A.heads, A.biased = hd, False
    wide = hd.chunks * hd.rows
    w = A.w = ctx.enter_context(nc.sbuf_tensor(prefix + "qkv", [HALF, 2, 2 * wide + hd.v_heads * hd.v_width], F32))
    A.wq, A.wk, A.wv = w[:, :, 0:wide], w[:, :, wide:2 * wide], w[:, :, 2 * wide:]
    A.wo = ctx.enter_context(nc.sbuf_tensor(prefix + "wo", [hd.out_rows, hd.out_chunks, DIM], F32))
    A.kb = ctx.enter_context(nc.sbuf_tensor(
        prefix + "keys_apart", [hd.rows, hd.chunks, BLOCK_TILES, hd.in_chunk * TILE], F32))
    units = TILES * hd.units
    A.w_qkv, A.w_o = loop("qkv_loaded", 16 * parts_w), loop("wo_loaded", 16 * parts_o)
    A.x_ready, A.pe_xt, A.xt_out = loop("x_ready", TILES), loop("x_turned", TILES), loop("xt_out", TILES)
    A.pe_qk, A.q_out, A.k_out = loop("qk_done", 6 * hd.chunks), loop("q_out", 3 * hd.chunks), loop("k_out", 3 * hd.chunks)
    A.pe_v, A.v_out = loop("v_done", TILES * hd.v_tiles), loop("v_out", TILES * hd.v_tiles)
    A.pe_s, A.s_read, A.s_max, A.p_exp = (loop(n, units) for n in ("scores", "scores_read", "max", "exp"))
    A.p_norm, A.pe_pt, A.pt_out, A.pe_o, A.o_out = (
        loop(n, units) for n in ("probs", "probs_turned", "pt_out", "heads_done", "o_out"))
    A.pe_y, A.y_read = loop("projected", TILES), loop("projected_read", TILES)
    A.pe_banks_free = lambda pe, turn: None
    return A


def dve_add_output(dve, S, P, turn, into, tiles, bank=None):
    for g in tiles:
        dve.wait_ge(P.pe_y.sem, P.pe_y.at(turn, g + 1))
        dve.tensor_tensor(into[:, g, :], S.ps[0:TILE, bank or 6 + g % 2, 0:DIM], into[:, g, :],
                          ALU.add).then_inc(P.y_read.sem, 1)
    dve.wait_ge(P.y_read.sem, P.y_read.at(turn, tiles[-1] + 1))


def stage_large_attention(nc, S, IN, pairs=2):
    E, K = 8, 2
    layers = 2 * pairs
    with ExitStack() as ctx:
        sem = ctx.enter_context(stage_semaphores(nc))
        hd = LARGE
        A = attention_buffers(nc, ctx, sem, "la_", hd, 1, 1)
        F = Names()

        def sb(name, shape):
            return ctx.enter_context(nc.sbuf_tensor("la_" + name, shape, F32))

        def loop(name, per, lead=0):
            return Loop(sem("la_" + name), per, lead)

        F.w1, F.b1, F.w2 = sb("w1", [HALF, 2, FF]), None, sb("w2", [128, FCH, DIM])
        bias = sb("position_bias", [TILE, 12 * TILE])
        gains = sb("gains", [TILE, 2 * layers + 1, DIM])
        normed = sb("normed", [TILE, TILES, DIM])
        A.mask = lambda u: bias[:, u * 2 * hd.width:(u + 1) * 2 * hd.width].rearrange("p (b n) -> p b n", b=2)
        F.w_1, F.w_2 = loop("w1_loaded", 16), loop("w2_loaded", 16)
        x1_ready, pe_xt1, xt1_out = loop("x1_ready", TILES), loop("x1_turned", TILES), loop("xt1_out", TILES)
        F.pe_h, F.h_out = loop("hidden", 3 * FCH), loop("hidden_out", 3 * FCH)
        F.pe_y, F.y_read = loop("ff_done", TILES), loop("ff_read", TILES)
        R = router_buffers(nc, ctx, sem, "la_r_", E)
        gate = sb("gate", [HALF, 2, E])
        M = experts(nc, ctx, sem, "la_m_", False)
        MF = M[0]
        gate_loaded, consts = loop("gate_loaded", 16), loop("constants_loaded", 64)
        own_dve = sem("la_dve_own")
        block = ctx.enter_context(nc.Block())

        @block.sync
        def _(sp):
            def load_expert(m, e):
                sp_expert(sp, M[e % 2], IN["b_m1"][m, e], IN["b_m2"][m, e])

            sp.dma_start(A.w[:, :, :], IN["b_qkv"][0]).then_inc(A.w_qkv.sem, 16)
            sp.dma_start(gains[:, :, :], IN["b_gains"]).then_inc(consts.sem, 16)
            sp.dma_start(S.hmask[:, :], IN["hmask64"]).then_inc(consts.sem, 16)
            sp.dma_start(bias[:, :], IN["b_bias"]).then_inc(consts.sem, 16)
            sp.dma_start(R.before[:, :, :], IN["before8"]).then_inc(consts.sem, 16)
            sp.dma_start(A.wo[:, :, :], IN["b_wo"][0]).then_inc(A.w_o.sem, 16)
            sp.dma_start(F.w1[:, :, :], IN["b_w1"][0]).then_inc(F.w_1.sem, 16)
            sp.dma_start(F.w2[:, :, :], IN["b_w2"][0]).then_inc(F.w_2.sem, 16)
            sp.dma_start(gate[:, :, :], IN["b_gate"][0]).then_inc(gate_loaded.sem, 16)
            load_expert(0, 0), load_expert(0, 1)
            for t in range(layers):
                more = t + 1 < layers
                if more:
                    sp.wait_ge(A.v_out.sem, A.v_out.at(t, TILES * hd.v_tiles))
                    sp.dma_start(A.w[:, :, :], IN["b_qkv"][t + 1]).then_inc(A.w_qkv.sem, 16)
                    sp.wait_ge(x1_ready.sem, x1_ready.at(t, TILES))
                    sp.dma_start(A.wo[:, :, :], IN["b_wo"][t + 1]).then_inc(A.w_o.sem, 16)
                    sp.wait_ge(F.h_out.sem, F.h_out.at(t, 3 * FCH))
                    sp.dma_start(F.w1[:, :, :], IN["b_w1"][t + 1]).then_inc(F.w_1.sem, 16)
                    sp.wait_ge(F.y_read.sem, F.y_read.at(t, TILES))
                    sp.dma_start(F.w2[:, :, :], IN["b_w2"][t + 1]).then_inc(F.w_2.sem, 16)
                if t % 2 == 0:
                    continue
                m = t // 2
                for e in range(2, E + 2):
                    if e >= E and not more:
                        continue
                    sp.wait_ge(MF.y_read.sem, MF.y_read.at(E * m + e - 2, TILES))
                    if e == E:
                        sp.wait_ge(R.logits_done.sem, R.logits_done.at(m, 1))
                        sp.dma_start(gate[:, :, :], IN["b_gate"][m + 1]).then_inc(gate_loaded.sem, 16)
                    load_expert(m + e // E, e % E)

        @block.tensor
        def _(pe):
            with pe.Fori(0, pairs) as p:
                for odd in range(2):
                    t = 2 * p + odd
                    A.pe_banks_free = lambda eng, turn: eng.wait_ge(A.x_ready.sem, A.x_ready.at(turn, TILES))
                    for b in range(3):
                        pe_transpose(pe, S, A, t, b, normed, A.x_ready, A.pe_xt, A.xt_out)
                        pe_qkv(pe, S, A, t, b)
                        pe_attend(pe, S, A, t, b)
                        pe_project(pe, S, A, t, b)
                    for b in range(3):
                        pe_transpose(pe, S, A, t, b, normed, x1_ready, pe_xt1, xt1_out)
                        pe.wait_ge(xt1_out.sem, xt1_out.at(t, BLOCKS[b][-1] + 1))
                        pe_ff(pe, S, F, t, b, lambda: pe.wait_ge(A.y_read.sem, A.y_read.at(t, TILES)))
                pe.wait_ge(gate_loaded.sem, gate_loaded.at(p, 16))
                pe.wait_ge(F.y_read.sem, F.y_read.at(2 * p + 1, TILES))
                pe_router(pe, S, R, E, gate)
                with pe.Fori(0, E // 2) as q:
                    for k in range(2):
                        e = p * E + 2 * q + k
                        for b in range(3):
                            pe_ff(pe, S, M[k], e, b, lambda: pe.wait_ge(MF.y_read.sem, MF.y_read.at(e, 0)), load_turn=p * (E // 2) + q)

        @block.scalar
        def _(act):
            with act.Fori(0, pairs) as p:
                for odd in range(2):
                    t = 2 * p + odd
                    for b in range(3):
                        act_transposed(act, S, A, t, b, A.pe_xt, A.xt_out)
                        act_qkv(act, S, A, t, b)
                        act_attend(act, S, A, t, b)
                    for b in range(3):
                        act_transposed(act, S, A, t, b, pe_xt1, xt1_out)
                        act_ff(act, S, F, t, b, ACT.Relu)
                act_route(act, S, R, p)
                with act.Fori(0, E // 2) as q:
                    for k in range(2):
                        for b in range(3):
                            act_ff(act, S, M[k], p * E + 2 * q + k, b, ACT.Gelu)

        @block.vector
        def _(dve):
            own = Own(own_dve)
            dve.nop().then_inc(MF.y_read.sem, TILES)
            dve.wait_ge(consts.sem, consts.at(0, 64))
            for b in range(3):
                normalise(dve, own, S, BLOCKS[b], S.h, S.x, 1e-5)
                dve.wait_ge(own.sem, own.n)
                normalise(dve, own, S, BLOCKS[b], S.x, normed, 1e-6, gains[:, 0, :], root=True, done=A.x_ready.sem)
            dve.sem_clear(own.sem)
            own.restart()
            with dve.Fori(0, pairs) as p:
                for odd in range(2):
                    t = 2 * p + odd
                    for b in range(3):
                        dve_qkv(dve, own, S, A, t, b)
                        dve_attend(dve, own, S, A, t, b)
                        dve_add_output(dve, S, A, t, S.x, BLOCKS[b])
                        normalise(dve, own, S, BLOCKS[b], S.x, normed, 1e-6, gains[:, 2 * t + 1, :], root=True,
                                  done=x1_ready.sem)
                    for b in range(3):
                        dve_add_output(dve, S, F, t, S.x, BLOCKS[b])
                        if odd == 0:
                            normalise(dve, own, S, BLOCKS[b], S.x, normed, 1e-6, gains[:, 2 * t + 2, :], root=True,
                                      done=A.x_ready.sem)
                dve_route(dve, own, S, R, p, E, K, whole=False)
                dve.sem_clear(own.sem)
                own.restart()
                with dve.Fori(0, E // 2) as q:
                    for k in range(2):
                        e = p * E + 2 * q + k
                        dve_add_scaled(dve, S, MF, e, S.x, lambda g: R.cw[:, g, bass.ds(2 * q + k, 1)], range(TILES))
                dve.wait_ge(MF.y_read.sem, MF.y_read.at(E * p + E - 1, TILES))
                for b in range(3):
                    normalise(dve, own, S, BLOCKS[b], S.x, normed, 1e-6, gains[:, 4 * p + 4, :], root=True,
                              done=A.x_ready.sem)
                dve.sem_clear(own.sem)
                own.restart()
            dve.wait_ge(A.x_ready.sem, A.x_ready.at(layers, TILES))
            dve.tensor_tensor(S.h[:, :, :], S.h[:, :, :], normed[:, :, :], ALU.add).then_inc(own.sem, own.up())
            dve.wait_ge(own.sem, own.n)


SHARP = Heads(128, 6, 2, 2, 64, 6, 128, 12, 64, 2, 8.0)


def stage_sharp_attention(nc, S, IN, prefix="g_", hd=SHARP):
    with ExitStack() as ctx:
        sem = ctx.enter_context(stage_semaphores(nc))
        A = attention_buffers(nc, ctx, sem, prefix, hd, 1, 1)
        A.mask = lambda u: S.mask[:, 0:2 * hd.width].rearrange("p (b n) -> p b n", b=2)
        small = sem(prefix + "constants_loaded")
        own_dve = sem(prefix + "dve_own")
        block = ctx.enter_context(nc.Block())

        @block.sync
        def _(sp):
            sp.dma_start(A.w[:, :, :], IN[prefix + "qkv"]).then_inc(A.w_qkv.sem, 16)
            sp.dma_start(S.hmask[:, :], IN["hmask64"]).then_inc(small, 16)
            sp.dma_start(A.wo[:, :, :], IN[prefix + "wo"]).then_inc(A.w_o.sem, 16)

        @block.tensor
        def _(pe):
            for b in range(3):
                pe_transpose(pe, S, A, 0, b, S.x, A.x_ready, A.pe_xt, A.xt_out)
                pe_qkv(pe, S, A, 0, b)
                pe_attend(pe, S, A, 0, b)
                pe_project(pe, S, A, 0, b)

        @block.scalar
        def _(act):
            for b in range(3):
                act_transposed(act, S, A, 0, b, A.pe_xt, A.xt_out)
                act_qkv(act, S, A, 0, b)
                act_attend(act, S, A, 0, b)

        @block.vector
        def _(dve):
            own = Own(own_dve)
            for b in range(3):
                normalise(dve, own, S, BLOCKS[b], S.h, S.x, 1e-5, done=A.x_ready.sem)
            dve.wait_ge(small, 16)
            for b in range(3):
                dve_qkv(dve, own, S, A, 0, b)
                dve_attend(dve, own, S, A, 0, b)
                dve_add_output(dve, S, A, 0, S.h, BLOCKS[b])


def stage_difference_attention(nc, S, IN, prefix="d_"):
    NH, HD = 12, 8
    PAIRS = NH * NH
    init = 0.8 - 0.6 * float(np.exp(-0.3 * 12))
    with ExitStack() as ctx:
        sem = ctx.enter_context(stage_semaphores(nc))
        A = Names()

        def sb(name, shape):
            return ctx.enter_context(nc.sbuf_tensor(prefix + name, shape, F32))

        def loop(name, per):
            return Loop(sem(prefix + name), per)

        w, wo = sb("qkv", [HALF, 2, 3 * DIM]), sb("wo", [HALF, 2, DIM])
        lam, dots, coef = sb("lambda", [TILE, 4, HD]), sb("dots", [TILE, 4]), sb("coef", [TILE, 2])
        qkv = sb("qkv_rows", [TILE, 2, 3 * DIM])
        prod = sb("products", [TILE, 2, PAIRS, HD])
        vprod = sb("value_products", [TILE, 2, DIM, NH])
        att = sb("attention", [TILE, 2, 2 * NH, NH])
        both = sb("difference", [TILE, 2, PAIRS])
        col = sb("col", [TILE, 2, 2 * NH])
        y = sb("outputs", [TILE, 2, DIM])
        yt = sb("outputs_T", [HALF, 2, 2, TILE])
        A.x_ready, A.pe_xt, A.xt_out = loop("x_ready", TILES), loop("x_turned", TILES), loop("xt_out", TILES)
        w_loaded, small = loop("weights_loaded", 32), loop("lambda_loaded", 16)
        dots_ready, dots_exped = loop("dots_ready", 1), loop("dots_exped", 1)
        pe_qkv_done, qkv_out = loop("qkv_done", TILES), loop("qkv_out", TILES)
        shifted, exped, diff, vprods, y_ready = (loop(n, TILES) for n in ("shifted", "exped", "diff", "vprods", "y_ready"))
        y_turned, yt_out = loop("y_turned", TILES), loop("yt_out", TILES)
        A.pe_y, A.y_read = loop("projected", TILES), loop("projected_read", TILES)
        own_dve = sem(prefix + "dve_own")
        block = ctx.enter_context(nc.Block())

        @block.sync
        def _(sp):
            sp.dma_start(w[:, :, :], IN[prefix + "qkv"]).then_inc(w_loaded.sem, 16)
            sp.dma_start(wo[:, :, :], IN[prefix + "wo"]).then_inc(w_loaded.sem, 16)
            sp.dma_start(lam[:, :, :], IN[prefix + "lambda"]).then_inc(small.sem, 16)

        @block.tensor
        def _(pe):
            for b in range(3):
                pe_transpose(pe, S, A, 0, b, S.x, A.x_ready, A.pe_xt, A.xt_out)
            pe.wait_ge(w_loaded.sem, w_loaded.at(0, 32))
            for s in range(TILES + 3):
                if s < TILES:
                    pe.wait_ge(A.xt_out.sem, A.xt_out.at(0, s + 1))
                    if s >= 2:
                        pe.wait_ge(qkv_out.sem, qkv_out.at(0, s - 1))
                    for bank, c0, c1 in ((0, 0, 2 * DIM), (1, 2 * DIM, 3 * DIM)):
                        for kc in range(2):
                            ins = pe.matmul(S.ps[0:TILE, 2 * (s % 2) + bank, 0:c1 - c0],
                                            S.xt[:, kc, s * TILE:(s + 1) * TILE], w[:, kc, c0:c1],
                                            start=kc == 0, stop=kc == 1)
                    ins.then_inc(pe_qkv_done.sem, 1)
                if s >= 3:
                    g = s - 3
                    pe.wait_ge(y_ready.sem, y_ready.at(0, g + 1))
                    if g:
                        pe.wait_ge(yt_out.sem, yt_out.at(0, g))
                    for c in range(2):
                        ins = pe.transpose(S.ps[0:HALF, 6, c * TILE:(c + 1) * TILE], y[:, g % 2, c * HALF:(c + 1) * HALF],
                                           S.ident[0:TILE, 0:TILE])
                    ins.then_inc(y_turned.sem, 1)
                    pe.wait_ge(yt_out.sem, yt_out.at(0, g + 1))
                    if g:
                        pe.wait_ge(A.y_read.sem, A.y_read.at(0, g))
                    for c in range(2):
                        ins = pe.matmul(S.ps[0:TILE, 7, 0:DIM], yt[:, g % 2, c, :], wo[:, c, :], start=c == 0, stop=c == 1)
                    ins.then_inc(A.pe_y.sem, 1)

        @block.scalar
        def _(act):
            act.wait_ge(dots_ready.sem, dots_ready.at(0, 1))
            act.activation(dots[:, 0:2], dots[:, 0:2], ACT.Exp).then_inc(dots_exped.sem, 1)
            for b in range(3):
                act_transposed(act, S, A, 0, b, A.pe_xt, A.xt_out)
            for s in range(TILES + 3):
                if s < TILES:
                    act.wait_ge(pe_qkv_done.sem, pe_qkv_done.at(0, s + 1))
                    if s >= 2:
                        act.wait_ge(vprods.sem, vprods.at(0, s - 1))
                    act.activation(qkv[:, s % 2, 0:2 * DIM], S.ps[0:TILE, 2 * (s % 2), 0:2 * DIM], ACT.Copy)
                    act.activation(qkv[:, s % 2, 2 * DIM:], S.ps[0:TILE, 2 * (s % 2) + 1, 0:DIM],
                                   ACT.Copy).then_inc(qkv_out.sem, 1)
                    act.wait_ge(shifted.sem, shifted.at(0, s + 1))
                    act.activation(att[:, s % 2, :, :], att[:, s % 2, :, :], ACT.Exp, scale=HD ** -0.5).then_inc(exped.sem, 1)
                if s >= 3:
                    g = s - 3
                    act.wait_ge(y_turned.sem, y_turned.at(0, g + 1))
                    act.activation(yt[:, g % 2, :, :], S.ps[0:HALF, 6, 0:2 * TILE].rearrange("p (c t) -> p c t", c=2),
                                   ACT.Copy).then_inc(yt_out.sem, 1)

        @block.gpsimd
        def _(pool):
            for g in range(TILES):
                pool.wait_ge(diff.sem, diff.at(0, g + 1))
                if g >= 2:
                    pool.wait_ge(y_ready.sem, y_ready.at(0, g - 1))
                weights = both[:, g % 2, :].rearrange("p (q k) -> p q k", k=NH).unsqueeze(2).to_broadcast([TILE, NH, 2 * HD, NH])
                values = qkv[:, g % 2, 2 * DIM:].rearrange("p (k d) -> p d k", d=2 * HD).unsqueeze(1).to_broadcast(
                    [TILE, NH, 2 * HD, NH])
                pool.tensor_tensor(vprod[:, g % 2, :, :].rearrange("p (q d) k -> p q d k", d=2 * HD), weights, values,
                                   ALU.mult).then_inc(vprods.sem, 1)

        @block.vector
        def _(dve):
            own = Own(own_dve)
            dve.wait_ge(small.sem, small.at(0, 16))
            dve.tensor_tensor(lam[:, 0:2, :], lam[:, 0:2, :], lam[:, 2:4, :], ALU.mult).then_inc(own.sem, own.up())
            dve.wait_ge(own.sem, own.n)
            dve.tensor_reduce(dots[:, 0:2], lam[:, 0:2, :], AX.X, ALU.add).then_inc(dots_ready.sem, 1)
            for b in range(3):
                normalise(dve, own, S, BLOCKS[b], S.h, S.x, 1e-5, done=A.x_ready.sem)
            dve.wait_ge(dots_exped.sem, dots_exped.at(0, 1))
            dve.memset(coef[:, 0:1], 1.0 - init).then_inc(own.sem, own.up())
            dve.tensor_tensor(dots[:, 2:3], dots[:, 0:1], dots[:, 1:2], ALU.subtract).then_inc(own.sem, own.up())
            dve.wait_ge(own.sem, own.n)
            dve.tensor_scalar(coef[:, 1:2], dots[:, 2:3], init, -(1.0 - init), ALU.add, ALU.mult).then_inc(own.sem, own.up())
            for s in range(TILES + 3):
                if s < TILES:
                    dve.wait_ge(qkv_out.sem, qkv_out.at(0, s + 1))
                    shape = [TILE, NH, NH, HD]
                    for half in range(2):
                        q, k = (qkv[:, s % 2, c * DIM:(c + 1) * DIM].rearrange(
                            "p (h t d) -> p t h d", t=2, d=HD)[:, half, :, :] for c in range(2))
                        dve.tensor_tensor(
                   prod[:, half, :, :].rearrange("p (q k) d -> p q k d", k=NH),
                   q.unsqueeze(2).to_broadcast(shape), k.unsqueeze(1).to_broadcast(shape), ALU.mult).then_inc(own.sem, own.up())
                    dve.wait_ge(own.sem, own.n)
                    a, c = att[:, s % 2, :, :], col[:, s % 2, :]
                    dve.tensor_reduce(a.rearrange("p a b -> p (a b)"), prod[:, :, :, :].rearrange(
               "p a b d -> p (a b) d"), AX.X, ALU.add).then_inc(own.sem, own.up())
                    dve.wait_ge(own.sem, own.n)
                    dve.tensor_reduce(c, a, AX.X, ALU.max).then_inc(own.sem, own.up())
                    dve.wait_ge(own.sem, own.n)
                    dve.tensor_tensor(a, a, c.unsqueeze(2).to_broadcast([TILE, 2 * NH, NH]), ALU.subtract).then_inc(shifted.sem, 1)
                if 1 <= s <= TILES:
                    g = s - 1
                    a, c = att[:, g % 2, :, :], col[:, g % 2, :]
                    dve.wait_ge(exped.sem, exped.at(0, g + 1))
                    dve.tensor_reduce(c, a, AX.X, ALU.add).then_inc(own.sem, own.up())
                    dve.wait_ge(own.sem, own.n)
                    dve.reciprocal(c, c).then_inc(own.sem, own.up())
                    dve.wait_ge(own.sem, own.n)
                    dve.tensor_tensor(c.rearrange("p (t h) -> p t h", t=2), c.rearrange("p (t h) -> p t h", t=2),
                                      coef[:, :].unsqueeze(2).to_broadcast([TILE, 2, NH]), ALU.mult).then_inc(own.sem, own.up())
                    dve.wait_ge(own.sem, own.n)
                    dve.tensor_tensor(a, a, c.unsqueeze(2).to_broadcast([TILE, 2 * NH, NH]), ALU.mult).then_inc(own.sem, own.up())
                    dve.wait_ge(own.sem, own.n)
                    dve.tensor_tensor(both[:, g % 2, :].rearrange("p (q k) -> p q k", k=NH), a[:, 0:NH, :], a[:, NH:, :],
                                      ALU.add).then_inc(diff.sem, 1)
                if 2 <= s < TILES + 2:
                    g = s - 2
                    dve.wait_ge(vprods.sem, vprods.at(0, g + 1))
                    if g >= 2:
                        dve.wait_ge(y_turned.sem, y_turned.at(0, g - 1))
                    dve.tensor_reduce(y[:, g % 2, :], vprod[:, g % 2, :, :], AX.X, ALU.add).then_inc(y_ready.sem, 1)
                if s >= 3:
                    dve_add_output(dve, S, A, 0, S.h, [s - 3], bank=7)


class Mixture:

    def __init__(self, nc, ctx, sem, prefix, E, outputs, bias_width=None):
        def sb(name, shape):
            return ctx.enter_context(nc.sbuf_tensor(prefix + name, shape, F32))

        def loop(name, per, lead=0):
            return Loop(sem(prefix + name), per, lead)

        self.E, self.outputs = E, outputs
        self.R = router_buffers(nc, ctx, sem, prefix + "r_", E)
        self.router = sb("router", [HALF, 2, E])
        self.router_bias = sb("router_bias", [TILE, bias_width or E])
        self.cw = sb("weights", [TILE, TILES, outputs])
        self.cwt = sb("weights_T", [outputs, TOKENS])
        self.out_bias = sb("out_bias", [outputs, DIM])
        self.x_ready, self.pe_xt, self.xt_out = loop("x_ready", TILES), loop("x_turned", TILES), loop("xt_out", TILES)
        self.cw_ready, self.cw_turned, self.cwt_out = loop("cw_ready", 1), loop("cw_turned", 3), loop("cwt_out", 3)
        self.small = loop("small_loaded", 64)
        self.pe_y, self.y_read = loop("bias_done", TILES), loop("bias_read", TILES)
        self.own_sem = sem(prefix + "dve_own")

    def sp_small(self, sp, IN, prefix, before):
        sp.dma_start(self.router[:, :, :], IN[prefix + "router"]).then_inc(self.small.sem, 16)
        sp.dma_start(self.router_bias[:, :], IN[prefix + "router_bias"]).then_inc(self.small.sem, 16)
        sp.dma_start(self.R.before[:, :, :], IN[before]).then_inc(self.small.sem, 16)
        sp.dma_start(self.out_bias[:, :], IN[prefix + "out_bias"]).then_inc(self.small.sem, 16)

    def pe_start(self, pe, S):
        for b in range(3):
            pe_transpose(pe, S, self, 0, b, S.x, self.x_ready, self.pe_xt, self.xt_out)
        pe.wait_ge(self.xt_out.sem, self.xt_out.at(0, TILES))
        pe.wait_ge(self.small.sem, self.small.at(0, 64))
        pe_router(pe, S, self.R, self.E, self.router)

    def pe_bias(self, pe, S):
        pe.wait_ge(self.cw_ready.sem, self.cw_ready.at(0, 1))
        for b, tiles in enumerate(BLOCKS):
            if b:
                pe.wait_ge(self.cwt_out.sem, self.cwt_out.at(0, b))
            for lg, g in enumerate(tiles):
                ins = pe.transpose(S.ps[0:self.outputs, 5, lg * TILE:(lg + 1) * TILE], self.cw[:, g, :],
                                   S.ident[0:TILE, 0:TILE])
            ins.then_inc(self.cw_turned.sem, 1)
        pe.wait_ge(self.cwt_out.sem, self.cwt_out.at(0, 3))
        for g in range(TILES):
            if g >= 2:
                pe.wait_ge(self.y_read.sem, self.y_read.at(0, g - 1))
            pe.matmul(S.ps[0:TILE, 6 + g % 2, 0:DIM], self.cwt[:, g * TILE:(g + 1) * TILE], self.out_bias[:, :],
                      start=True, stop=True).then_inc(self.pe_y.sem, 1)

    def act_start(self, act, S):
        for b in range(3):
            act_transposed(act, S, self, 0, b, self.pe_xt, self.xt_out)

    def act_bias(self, act, S):
        for b, tiles in enumerate(BLOCKS):
            act.wait_ge(self.cw_turned.sem, self.cw_turned.at(0, b + 1))
            act.activation(self.cwt[:, tiles[0] * TILE:(tiles[-1] + 1) * TILE],
                           S.ps[0:self.outputs, 5, 0:len(tiles) * TILE], ACT.Copy).then_inc(self.cwt_out.sem, 1)


def stage_two_layer_experts(nc, S, IN, prefix="f_"):
    E, K = 8, 2
    with ExitStack() as ctx:
        sem = ctx.enter_context(stage_semaphores(nc))
        X = Mixture(nc, ctx, sem, prefix, E, E)
        M = experts(nc, ctx, sem, prefix, True)
        F = M[0]
        block = ctx.enter_context(nc.Block())

        @block.sync
        def _(sp):
            X.sp_small(sp, IN, prefix, "before8")
            for e in range(2):
                sp_expert(sp, M[e], IN[prefix + "w1"][e], IN[prefix + "w2"][e], IN[prefix + "b1"][e])
            with sp.Fori(0, E // 2 - 1) as q:
                for k in range(2):
                    sp.wait_ge(F.y_read.sem, F.y_read.at(2 * q + k, TILES))
                    e = 2 * q + 2 + k
                    sp_expert(sp, M[k], IN[prefix + "w1"][e], IN[prefix + "w2"][e], IN[prefix + "b1"][e])

        @block.tensor
        def _(pe):
            X.pe_start(pe, S)
            X.pe_bias(pe, S)
            pe.wait_ge(X.y_read.sem, X.y_read.at(0, TILES))
            with pe.Fori(0, E // 2) as q:
                for k in range(2):
                    for b in range(3):
                        pe_ff(pe, S, M[k], 2 * q + k, b, lambda: pe.wait_ge(F.y_read.sem, F.y_read.at(2 * q + k, 0)), load_turn=q)

        @block.scalar
        def _(act):
            X.act_start(act, S)
            act_route(act, S, X.R, 0)
            X.act_bias(act, S)
            with act.Fori(0, E // 2) as q:
                for k in range(2):
                    act.wait_ge(M[k].w_1.sem, M[k].w_1.at(q, 32))
                    for b in range(3):
                        act_ff(act, S, M[k], 2 * q + k, b, ACT.Gelu)

        @block.vector
        def _(dve):
            own = Own(X.own_sem)
            dve.nop().then_inc(F.y_read.sem, TILES)
            for b in range(3):
                normalise(dve, own, S, BLOCKS[b], S.h, S.x, 1e-5, done=X.x_ready.sem)
            dve.wait_ge(X.small.sem, X.small.at(0, 64))
            X.R.cw = X.cw[:, :, 0:E]
            dve_route(dve, own, S, X.R, 0, E, K, bias=X.router_bias[:, :])
            dve.nop().then_inc(X.cw_ready.sem, 1)
            dve_add_output(dve, S, X, 0, S.h, range(TILES))
            with dve.Fori(0, E // 2) as q:
                for k in range(2):
                    dve_add_scaled(dve, S, F, 2 * q + k, S.h, lambda g: X.cw[:, g, bass.ds(2 * q + k, 1)], range(TILES))
            dve.wait_ge(F.y_read.sem, F.y_read.at(E - 1, TILES))


def stage_linear_experts(nc, S, IN, prefix="e_"):
    E, K = 8, 2
    with ExitStack() as ctx:
        sem = ctx.enter_context(stage_semaphores(nc))
        X = Mixture(nc, ctx, sem, prefix, E, E)
        w = ctx.enter_context(nc.sbuf_tensor(prefix + "w", [HALF, 2, E, DIM], F32))
        loaded = sem(prefix + "experts_loaded")
        Y = Names()
        Y.pe_y = Loop(sem(prefix + "expert_done"), TILES)
        Y.y_read = Loop(sem(prefix + "expert_read"), TILES, TILES)
        block = ctx.enter_context(nc.Block())

        @block.sync
        def _(sp):
            X.sp_small(sp, IN, prefix, "before8")
            sp.dma_start(w[:, :, :, :], IN[prefix + "w"]).then_inc(loaded, 16)

        @block.tensor
        def _(pe):
            X.pe_start(pe, S)
            X.pe_bias(pe, S)
            pe.wait_ge(X.y_read.sem, X.y_read.at(0, TILES))
            pe.wait_ge(loaded, 16)
            with pe.Fori(0, E) as e:
                for g in range(TILES):
                    if g != 1:
                        pe.wait_ge(Y.y_read.sem, Y.y_read.at(e, max(g - 1, 0)))
                    for kc in range(2):
                        ins = pe.matmul(S.ps[0:TILE, 6 + g % 2, 0:DIM], S.xt[:, kc, g * TILE:(g + 1) * TILE],
                                        w[:, kc, e, :], start=kc == 0, stop=kc == 1)
                    ins.then_inc(Y.pe_y.sem, 1)

        @block.scalar
        def _(act):
            X.act_start(act, S)
            act_route(act, S, X.R, 0)
            X.act_bias(act, S)

        @block.vector
        def _(dve):
            own = Own(X.own_sem)
            dve.nop().then_inc(Y.y_read.sem, TILES)
            for b in range(3):
                normalise(dve, own, S, BLOCKS[b], S.h, S.x, 1e-5, done=X.x_ready.sem)
            dve.wait_ge(X.small.sem, X.small.at(0, 64))
            X.R.cw = X.cw[:, :, 0:E]
            dve_route(dve, own, S, X.R, 0, E, K, bias=X.router_bias[:, :], eps=1e-9)
            dve.nop().then_inc(X.cw_ready.sem, 1)
            dve_add_output(dve, S, X, 0, S.h, range(TILES))
            with dve.Fori(0, E) as e:
                dve_add_scaled(dve, S, Y, e, S.h, lambda g: X.cw[:, g, bass.ds(e, 1)], range(TILES))
            dve.wait_ge(Y.y_read.sem, Y.y_read.at(E - 1, TILES))


def allocate(nc, ctx):
    S = Names()

    def sb(name, shape, dt=F32):
        return ctx.enter_context(nc.sbuf_tensor(name, shape, dt))

    S.h = sb("residual", [TILE, TILES, DIM])
    S.x = sb("inner", [TILE, TILES, DIM])
    S.xt = sb("inner_T", [HALF, 2, TOKENS])
    S.ident = sb("identity", [128, 128])
    S.mask = sb("images_apart", [TILE, 6 * TILE])
    S.hmask = sb("head_mask", [128, 12])
    S.stats = sb("stats", [TILE, TILES, 6])
    S.meanvar = sb("meanvar", [TILE, TILES, 2])
    S.rstd = sb("rstd", [TILE, TILES])
    S.small = sb("small", [TILE, 2, TILES])
    S.smalli = sb("smalli", [TILE, TILES], I32)
    S.qt = sb("queries_T", [128, FCH, BLOCK_TILES * TILE])
    S.v = sb("values", [TILE, BLOCK_TILES, FF])
    S.ot = sb("heads_T", [128, FCH, BLOCK_TILES * TILE])
    S.h1 = sb("hidden_T", [128, FCH, BLOCK_TILES * TILE])
    S.p = sb("probs", [TILE, 4, 6 * TILE])
    S.pt = sb("probs_T", [TILE, 2, 6 * TILE])
    S.nmax = sb("nmax", [TILE, 4, 6])
    S.sums = sb("sums", [TILE, 4, 6])
    S.recs = sb("recs", [TILE, 4, 6])
    S.ps = ctx.enter_context(nc.psum_tensor("ps", [128, 8, BANK], F32))
    return S


def stage_start(nc, S, IN):
    with ExitStack() as ctx:
        sem = ctx.enter_context(stage_semaphores(nc))
        loaded = sem("constants_loaded")
        zeroed = sem("values_zeroed")
        block = ctx.enter_context(nc.Block())

        @block.sync
        def _(sp):
            for dst, name in ((S.ident, "ident"), (S.mask, "image_mask"), (S.hmask, "hmask16")):
                sp.dma_start(dst[:, :], IN[name]).then_inc(loaded, 16)
            sp.wait_ge(loaded, 48)

        @block.gpsimd
        def _(pool):
            pool.memset(S.v[:, :, :], 0.0).then_inc(zeroed, 1)
            pool.wait_ge(zeroed, 1)


def stage_patches_and_convolution(nc, S, IN, scratch_in, scratch_out):
    GT = CONV_BLOCKS * PADDED
    with ExitStack() as ctx:
        sem = ctx.enter_context(stage_semaphores(nc))
        A = Names()

        def sb(name, shape):
            return ctx.enter_context(nc.sbuf_tensor("t_" + name, shape, F32))

        def loop(name, per):
            return Loop(sem("t_" + name), per)

        patches = (S.qt, S.ot, S.h1)
        w, bias, ln0 = sb("w", [128, FCH, DIM]), sb("bias", [TILE, DIM]), sb("ln0", [TILE, 2 * DIM])
        taps = sb("taps", [TILE, CONV_GROUPS, CONV_D, TILE])
        cbias = sb("conv_bias", [TILE, CONV_GROUPS])
        xin, xout = sb("conv_in", [TILE, CONV_GROUPS, GT]), sb("conv_out", [TILE, CONV_GROUPS, GT])
        back = sb("conv_T", [HALF, 2, TOKENS])
        patches_loaded = [loop(f"patches_loaded_{b}", 16) for b in range(3)]
        w_loaded, taps_loaded, small = loop("w_loaded", 32), loop("taps_loaded", 16), loop("small_loaded", 32)
        spilled, gathered = loop("spilled", 16), [loop(f"gathered_{k}", 16) for k in range(4)]
        scattered, returned = loop("scattered", 64), loop("returned", 16)
        back_in_order = loop("back_in_order", 2)
        A.pe_y, A.y_read = loop("embedded", TILES), loop("embedded_read", TILES)
        x_ready, x_turned, xt_out = loop("x_ready", TILES), loop("x_turned", TILES), loop("xt_out", TILES)
        conv_done, conv_out = loop("conv_done", CONV_GROUPS), loop("conv_out", CONV_GROUPS)
        pos_turned, pos_read = loop("pos_turned", TILES), loop("pos_read", TILES)
        own_dve = sem("t_dve_own")
        block = ctx.enter_context(nc.Block())

        def groups(t, q):
            rows = t.rearrange("(g c) (j n) -> g (c j) n", c=CONV_CH, j=CONV_J)
            return rows[4 * q:4 * q + 4].rearrange("g r n -> r g n")

        out_of_dram = back[:, :, :].rearrange("p c (j a b) -> p c b a j", b=PADDED, j=CONV_J)
        in_order = S.xt[:, :, :].rearrange("p c (b a j) -> p c b a j", b=PADDED, j=CONV_J)

        @block.sync
        def _(sp):
            sp.dma_start(w[:, :, :], IN["t_w"]).then_inc(w_loaded.sem, 16)
            sp.dma_start(bias[:, :], IN["t_bias"]).then_inc(w_loaded.sem, 16)
            for b, tiles in enumerate(BLOCKS):
                sp.dma_start(patches[b][:, :, 0:len(tiles) * TILE],
                             IN["t_patches"][:, :, tiles[0] * TILE:(tiles[-1] + 1) * TILE]).then_inc(patches_loaded[b].sem, 16)
            sp.dma_start(cbias[:, :], IN["t_conv_bias"]).then_inc(small.sem, 16)
            sp.dma_start(ln0[:, :], IN["t_ln0"]).then_inc(small.sem, 16)
            sp.dma_start(taps[:, :, :, :], IN["t_taps"]).then_inc(taps_loaded.sem, 16)
            sp.wait_ge(xt_out.sem, xt_out.at(0, TILES))
            sp.dma_start(scratch_in.rearrange("(c p) t -> p c t", p=HALF), S.xt[:, :, :]).then_inc(spilled.sem, 16)
            sp.wait_ge(spilled.sem, spilled.at(0, 16))
            for q in range(4):
                sp.dma_start(xin[:, 4 * q:4 * q + 4, :], groups(scratch_in, q)).then_inc(gathered[q].sem, 16)
            for q in range(4):
                sp.wait_ge(conv_out.sem, conv_out.at(0, 4 * q + 4))
                sp.dma_start(groups(scratch_out, q), xout[:, 4 * q:4 * q + 4, :]).then_inc(scattered.sem, 16)
            sp.wait_ge(scattered.sem, scattered.at(0, 64))
            sp.dma_start(back[:, :, :], scratch_out.rearrange("(c p) t -> p c t", p=HALF)).then_inc(returned.sem, 16)

        @block.tensor
        def _(pe):
            pe.wait_ge(w_loaded.sem, w_loaded.at(0, 32))
            for b, tiles in enumerate(BLOCKS):
                pe.wait_ge(patches_loaded[b].sem, patches_loaded[b].at(0, 16))
                for lg, g in enumerate(tiles):
                    if g >= 2:
                        pe.wait_ge(A.y_read.sem, A.y_read.at(0, g - 1))
                    for c in range(FCH):
                        ins = pe.matmul(S.ps[0:TILE, 6 + g % 2, 0:DIM], patches[b][:, c, lg * TILE:(lg + 1) * TILE],
                                        w[:, c, :], start=c == 0, stop=c == FCH - 1)
                    ins.then_inc(A.pe_y.sem, 1)
            for b in range(3):
                pe_transpose(pe, S, A, 0, b, S.x, x_ready, x_turned, xt_out)
            pe.wait_ge(taps_loaded.sem, taps_loaded.at(0, 16))
            distances = sorted(range(1 - CONV_BLOCKS, CONV_BLOCKS), key=abs)
            for g in range(CONV_GROUPS):
                pe.wait_ge(gathered[g // 4].sem, gathered[g // 4].at(0, 16))
                if g >= 4:
                    pe.wait_ge(conv_out.sem, conv_out.at(0, g - 3))
                for n, d in enumerate(distances):
                    out0, in0, k = max(d, 0), max(-d, 0), CONV_BLOCKS - abs(d)
                    ins = pe.matmul(S.ps[0:TILE, g % 4, out0 * PADDED:(out0 + k) * PADDED],
                                    taps[:, g, d + CONV_BLOCKS - 1, :],
                                    xin[:, g, in0 * PADDED:(in0 + k) * PADDED],
                                    start=n == 0, stop=n == CONV_D - 1, skip_group_check=True)
                ins.then_inc(conv_done.sem, 1)
            pe.wait_ge(back_in_order.sem, back_in_order.at(0, 2))
            for g in range(TILES):
                if g >= 2:
                    pe.wait_ge(pos_read.sem, pos_read.at(0, g - 1))
                for c in range(2):
                    tile = S.xt[:, c, g * TILE:(g + 1) * TILE]
                    ins = pe.transpose(S.ps[0:TILE, 6 + g % 2, c * HALF:(c + 1) * HALF], tile, S.ident[0:HALF, 0:HALF])
                ins.then_inc(pos_turned.sem, 1)

        @block.scalar
        def _(act):
            by_image = S.xt[:, :, :].rearrange("p c (j a b) -> p c b a j", b=PADDED, j=CONV_J)
            for g in range(TILES):
                act.wait_ge(x_turned.sem, x_turned.at(0, g + 1))
                for c in range(2):
                    ins = act.activation(by_image[:, c, g * GROUP:(g + 1) * GROUP],
                                         S.ps[0:HALF, 4 + g % 2, c * TILE:(c + 1) * TILE].rearrange(
                                             "p (b a j) -> p b a j", b=GROUP, j=CONV_J), ACT.Copy)
                ins.then_inc(xt_out.sem, 1)
            act.wait_ge(small.sem, small.at(0, 32))
            for g in range(CONV_GROUPS):
                act.wait_ge(conv_done.sem, conv_done.at(0, g + 1))
                act.activation(xout[:, g, :], S.ps[0:TILE, g % 4, 0:GT], ACT.Gelu, bias=cbias[:, g:g + 1]).then_inc(conv_out.sem, 1)
            act.wait_ge(returned.sem, returned.at(0, 16))
            act.activation(in_order[:, 1], out_of_dram[:, 1], ACT.Copy).then_inc(back_in_order.sem, 1)

        @block.vector
        def _(dve):
            own = Own(own_dve)
            dve.wait_ge(w_loaded.sem, w_loaded.at(0, 32))
            for b in range(3):
                for g in BLOCKS[b]:
                    dve.wait_ge(A.pe_y.sem, A.pe_y.at(0, g + 1))
                    dve.tensor_tensor(S.h[:, g, :], S.ps[0:TILE, 6 + g % 2, 0:DIM], bias[:, :], ALU.add).then_inc(A.y_read.sem, 1)
                dve.wait_ge(A.y_read.sem, A.y_read.at(0, BLOCKS[b][-1] + 1))
                normalise(dve, own, S, BLOCKS[b], S.h, S.x, 1e-5, done=x_ready.sem)
            dve.wait_ge(x_ready.sem, x_ready.at(0, TILES))
            dve.wait_ge(returned.sem, returned.at(0, 16))
            dve.tensor_copy(in_order[:, 0], out_of_dram[:, 0]).then_inc(back_in_order.sem, 1)
            dve.wait_ge(small.sem, small.at(0, 32))
            for b in range(3):
                for g in BLOCKS[b]:
                    dve.wait_ge(pos_turned.sem, pos_turned.at(0, g + 1))
                    dve.tensor_tensor(S.x[:, g, :], S.ps[0:TILE, 6 + g % 2, 0:DIM], S.x[:, g, :], ALU.add).then_inc(pos_read.sem, 1)
                dve.wait_ge(pos_read.sem, pos_read.at(0, BLOCKS[b][-1] + 1))
                normalise(dve, own, S, BLOCKS[b], S.x, S.x, 1e-5, ln0[:, 0:DIM], ln0[:, DIM:])
                dve.wait_ge(own.sem, own.n)


def stage_decay_attention(nc, S, IN, prefix="h_"):
    with ExitStack() as ctx:
        sem = ctx.enter_context(stage_semaphores(nc))
        A = Names()

        def sb(name, shape):
            return ctx.enter_context(nc.sbuf_tensor(prefix + name, shape, F32))

        def loop(name, per):
            return Loop(sem(prefix + name), per)

        w, qkb, vb, decay = sb("qkv", [HALF, 2, 3 * DIM]), sb("qk_bias", [HALF, 4]), sb("v_bias", [TILE, DIM]), sb("decay", [TILE, TILE])
        st = sb("scores_T", [TILE, 2, TILE])
        loaded = loop("loaded", 64)
        A.x_ready, A.pe_xt, A.xt_out = loop("x_ready", TILES), loop("x_turned", TILES), loop("xt_out", TILES)
        qk_done, qk_out, v_done, v_out = loop("qk_done", 12), loop("qk_out", 12), loop("v_done", TILES), loop("v_out", TILES)
        s_done, s_out = loop("scores_done", TILES), loop("scores_out", TILES)
        A.pe_y, A.y_read = loop("out_done", TILES), loop("out_read", TILES)
        own_dve = sem(prefix + "dve_own")
        block = ctx.enter_context(nc.Block())

        @block.sync
        def _(sp):
            for dst, name in ((w[:, :, :], "qkv"), (qkb[:, :], "qk_bias"), (vb[:, :], "v_bias"), (decay[:, :], "decay")):
                sp.dma_start(dst, IN[prefix + name]).then_inc(loaded.sem, 16)

        @block.tensor
        def _(pe):
            for b in range(3):
                pe_transpose(pe, S, A, 0, b, S.x, A.x_ready, A.pe_xt, A.xt_out)
            pe.wait_ge(A.xt_out.sem, A.xt_out.at(0, TILES))
            pe.wait_ge(loaded.sem, loaded.at(0, 64))
            for b, tiles in enumerate(BLOCKS):
                c0, cols = tiles[0] * TILE, len(tiles) * TILE
                if b:
                    pe.wait_ge(s_out.sem, s_out.at(0, tiles[0]))
                for m in range(4):
                    for kc in range(2):
                        ins = pe.matmul(S.ps[0:HALF, m, 0:cols], w[:, kc, m * HALF:(m + 1) * HALF],
                                        S.xt[:, kc, c0:c0 + cols], start=kc == 0, stop=kc == 1)
                    ins.then_inc(qk_done.sem, 1)
                for g in tiles:
                    if g >= 2:
                        pe.wait_ge(v_out.sem, v_out.at(0, g - 1))
                    for kc in range(2):
                        ins = pe.matmul(S.ps[0:TILE, 4 + g % 2, 0:DIM], S.xt[:, kc, g * TILE:(g + 1) * TILE],
                                        w[:, kc, 2 * DIM:], start=kc == 0, stop=kc == 1)
                    ins.then_inc(v_done.sem, 1)
                pe.wait_ge(qk_out.sem, qk_out.at(0, 4 * (b + 1)))
                for s in range(len(tiles) + 1):
                    if s < len(tiles):
                        g = tiles[s]
                        if s >= 2:
                            pe.wait_ge(s_out.sem, s_out.at(0, g - 1))
                        for c in range(2):
                            ins = pe.matmul(S.ps[0:TILE, g % 2, 0:TILE], S.qt[0:HALF, 2 + c, s * TILE:(s + 1) * TILE],
                                            S.qt[0:HALF, c, s * TILE:(s + 1) * TILE], start=c == 0, stop=c == 1)
                        ins.then_inc(s_done.sem, 1)
                    if s:
                        g = tiles[s - 1]
                        pe.wait_ge(s_out.sem, s_out.at(0, g + 1))
                        pe.wait_ge(v_out.sem, v_out.at(0, g + 1))
                        if g >= 2:
                            pe.wait_ge(A.y_read.sem, A.y_read.at(0, g - 1))
                        pe.matmul(S.ps[0:TILE, 6 + g % 2, 0:DIM], st[:, g % 2, :], S.v[:, s - 1, 0:DIM],
                                  start=True, stop=True).then_inc(A.pe_y.sem, 1)

        @block.scalar
        def _(act):
            for b in range(3):
                act_transposed(act, S, A, 0, b, A.pe_xt, A.xt_out)
            act.wait_ge(loaded.sem, loaded.at(0, 64))
            for b, tiles in enumerate(BLOCKS):
                for m in range(4):
                    act.wait_ge(qk_done.sem, qk_done.at(0, 4 * b + m + 1))
                    act.activation(S.qt[0:HALF, m, 0:len(tiles) * TILE], S.ps[0:HALF, m, 0:len(tiles) * TILE],
                                   ACT.Identity, bias=qkb[:, m:m + 1]).then_inc(qk_out.sem, 1)

        @block.vector
        def _(dve):
            own = Own(own_dve)
            for b in range(3):
                normalise(dve, own, S, BLOCKS[b], S.h, S.x, 1e-5, done=A.x_ready.sem)
            dve.wait_ge(loaded.sem, loaded.at(0, 64))
            for b, tiles in enumerate(BLOCKS):
                for lg, g in enumerate(tiles):
                    dve.wait_ge(v_done.sem, v_done.at(0, g + 1))
                    dve.tensor_tensor(S.v[:, lg, 0:DIM], S.ps[0:TILE, 4 + g % 2, 0:DIM], vb[:, :], ALU.add).then_inc(v_out.sem, 1)
                for s in range(len(tiles) + 1):
                    if s < len(tiles):
                        g = tiles[s]
                        dve.wait_ge(s_done.sem, s_done.at(0, g + 1))
                        dve.scalar_tensor_tensor(st[:, g % 2, :], S.ps[0:TILE, g % 2, 0:TILE], DIM ** -0.5, decay[:, :],
                                                 ALU.mult, ALU.mult).then_inc(s_out.sem, 1)
                    if s:
                        dve_add_output(dve, S, A, 0, S.h, [tiles[s - 1]])


def stage_gated_experts(nc, S, IN, prefix="i_"):
    E, G, GROUPS, K, ALL = 16, 4, 2, 4, 18
    STEPS = 6
    with ExitStack() as ctx:
        sem = ctx.enter_context(stage_semaphores(nc))
        X = Mixture(nc, ctx, sem, prefix, E, ALL, bias_width=2 * E)
        R = X.R

        def sb(name, shape):
            return ctx.enter_context(nc.sbuf_tensor(prefix + name, shape, F32))

        def loop(name, per, lead=0):
            return Loop(sem(prefix + name), per, lead)

        w = [sb(f"w_{k}", [HALF, 3 * DIM + 2]) for k in range(2)]
        pair, top, gmask = sb("pair_sums", [TILE, TILES * G, 6]), sb("group_scores", [TILE, TILES, G]), sb("group_mask", [TILE, TILES, G])
        chosen = sb("chosen", [TILE, TILES, E])
        silu, hidden = sb("silu", [HALF, 2, BLOCK_TILES * TILE]), sb("hidden", [HALF, 2, BLOCK_TILES * TILE])
        w_loaded = [loop(f"w_loaded_{k}", 16) for k in range(2)]
        gu_done, silu_out = loop("gate_up_done", STEPS), loop("silu_out", STEPS)
        hidden_out = loop("hidden_out", STEPS, STEPS)
        pe_y, y_read = loop("expert_done", 2 * TILES), loop("expert_read", 2 * TILES, 2 * TILES)
        block = ctx.enter_context(nc.Block())

        def up_gate(k, kc, part):
            c0 = kc * DIM + part * HALF
            return w[k][:, c0:c0 + HALF]

        @block.sync
        def _(sp):
            X.sp_small(sp, IN, prefix, "before16")
            for k in range(2):
                sp.dma_start(w[k][:, :], IN[prefix + "w"][k]).then_inc(w_loaded[k].sem, 16)
            with sp.Fori(0, ALL // 2 - 1) as q:
                for k in range(2):
                    sp.wait_ge(pe_y.sem, pe_y.at(q, (k + 1) * TILES))
                    sp.dma_start(w[k][:, :], IN[prefix + "w"][2 * q + 2 + k]).then_inc(w_loaded[k].sem, 16)

        @block.tensor
        def _(pe):
            X.pe_start(pe, S)
            X.pe_bias(pe, S)
            pe.wait_ge(X.y_read.sem, X.y_read.at(0, TILES))
            with pe.Fori(0, ALL // 2) as q:
                for s in range(STEPS + 1):
                    if s < STEPS:
                        k, tiles = s // 3, BLOCKS[s % 3]
                        c0, cols = tiles[0] * TILE, len(tiles) * TILE
                        if s % 3 == 0:
                            pe.wait_ge(w_loaded[k].sem, w_loaded[k].at(q, 16))
                        pe.wait_ge(hidden_out.sem, hidden_out.at(q, s - 1))
                        for part in range(2):
                            for kc in range(2):
                                ins = pe.matmul(S.ps[0:HALF, 2 * (s % 2) + part, 0:cols], up_gate(k, kc, part),
                                                S.xt[:, kc, c0:c0 + cols], start=kc == 0, stop=kc == 1)
                        ins.then_inc(gu_done.sem, 1)
                    if s:
                        r = s - 1
                        k, tiles = r // 3, BLOCKS[r % 3]
                        pe.wait_ge(hidden_out.sem, hidden_out.at(q, r + 1))
                        for lg, g in enumerate(tiles):
                            n = k * TILES + g
                            pe.wait_ge(y_read.sem, y_read.at(q, n - 1))
                            pe.matmul(S.ps[0:TILE, 6 + n % 2, 0:DIM], hidden[:, r % 2, lg * TILE:(lg + 1) * TILE],
                                      w[k][:, 2 * DIM:3 * DIM], start=True, stop=True).then_inc(pe_y.sem, 1)

        @block.scalar
        def _(act):
            X.act_start(act, S)
            act.wait_ge(R.shifted.sem, R.shifted.at(0, 1))
            act.activation(R.ex, R.ex, ACT.Sigmoid).then_inc(R.exped.sem, 1)
            X.act_bias(act, S)
            with act.Fori(0, ALL // 2) as q:
                for s in range(STEPS):
                    k, cols = s // 3, len(BLOCKS[s % 3]) * TILE
                    act.wait_ge(gu_done.sem, gu_done.at(q, s + 1))
                    act.activation(silu[:, s % 2, 0:cols], S.ps[0:HALF, 2 * (s % 2), 0:cols], ACT.Silu,
                                   bias=w[k][:, 3 * DIM:3 * DIM + 1]).then_inc(silu_out.sem, 1)

        @block.vector
        def _(dve):
            own = Own(X.own_sem)
            dve.nop().then_inc(y_read.sem, 2 * TILES)
            dve.nop().then_inc(hidden_out.sem, STEPS)
            for b in range(3):
                normalise(dve, own, S, BLOCKS[b], S.h, S.x, 1e-5, done=X.x_ready.sem)
            dve.wait_ge(X.small.sem, X.small.at(0, 64))
            dve.wait_ge(R.logits_done.sem, R.logits_done.at(0, 1))
            bias = X.router_bias

            def over_tiles(c):
                return c.unsqueeze(1).to_broadcast([TILE, TILES, E])

            dve.tensor_tensor(R.ex, S.ps[0:TILE, 4, 0:TILES * E].rearrange("p (g e) -> p g e", e=E),
                              over_tiles(bias[:, 0:E]), ALU.add).then_inc(R.shifted.sem, 1)
            dve.memset(X.cw[:, :, E:ALL], 1.0).then_inc(own.sem, own.up())
            dve.wait_ge(R.exped.sem, R.exped.at(0, 1))
            dve.tensor_tensor(chosen[:, :, :], R.ex, over_tiles(bias[:, E:2 * E]), ALU.add).then_inc(own.sem, own.up())
            dve.wait_ge(own.sem, own.n)
            c = chosen[:, :, :].rearrange("p t (g e) -> p (t g) e", g=G)
            dve.tensor_tensor(pair[:, :, 0:3], c[:, :, 0:3], c[:, :, 1:4], ALU.add).then_inc(own.sem, own.up())
            dve.tensor_tensor(pair[:, :, 3:5], c[:, :, 0:2], c[:, :, 2:4], ALU.add).then_inc(own.sem, own.up())
            dve.tensor_tensor(pair[:, :, 5:6], c[:, :, 0:1], c[:, :, 3:4], ALU.add).then_inc(own.sem, own.up())
            dve.wait_ge(own.sem, own.n)
            dve.tensor_reduce(top[:, :, :].rearrange("p t g -> p (t g)"), pair[:, :, :], AX.X, ALU.max).then_inc(own.sem, own.up())
            dve.wait_ge(own.sem, own.n)
            dve_top_mask(dve, own, S, R, gmask[:, :, :], top[:, :, :], G, GROUPS)
            dve.tensor_tensor(c, c, gmask[:, :, :].rearrange("p t g -> p (t g)").unsqueeze(2).to_broadcast(
       [TILE, TILES * G, E // G]), ALU.mult).then_inc(own.sem, own.up())
            dve.wait_ge(own.sem, own.n)
            dve_top_mask(dve, own, S, R, R.mask, chosen[:, :, :], E, K)
            dve.tensor_tensor(R.ex, R.ex, R.mask, ALU.mult).then_inc(own.sem, own.up())
            dve.wait_ge(own.sem, own.n)
            dve.tensor_reduce(R.col, R.ex, AX.X, ALU.add).then_inc(own.sem, own.up())
            dve.wait_ge(own.sem, own.n)
            dve.tensor_scalar(R.col, R.col, 1e-20, None, ALU.add).then_inc(own.sem, own.up())
            dve.wait_ge(own.sem, own.n)
            dve.reciprocal(R.col, R.col).then_inc(own.sem, own.up())
            dve.wait_ge(own.sem, own.n)
            dve.tensor_tensor(R.ex, R.ex, R.col.unsqueeze(2).to_broadcast([TILE, TILES, E]), ALU.mult).then_inc(own.sem, own.up())
            dve.wait_ge(own.sem, own.n)
            dve.tensor_scalar(X.cw[:, :, 0:E], R.ex, 2.5, None, ALU.mult).then_inc(own.sem, own.up())
            dve.wait_ge(own.sem, own.n)
            dve.nop().then_inc(X.cw_ready.sem, 1)
            dve_add_output(dve, S, X, 0, S.h, range(TILES))
            with dve.Fori(0, ALL // 2) as q:
                for s in range(STEPS + 1):
                    if s < STEPS:
                        k, cols = s // 3, len(BLOCKS[s % 3]) * TILE
                        dve.wait_ge(silu_out.sem, silu_out.at(q, s + 1))
                        dve.scalar_tensor_tensor(hidden[:, s % 2, 0:cols], S.ps[0:HALF, 2 * (s % 2) + 1, 0:cols],
                                                 w[k][:, 3 * DIM + 1:3 * DIM + 2], silu[:, s % 2, 0:cols],
                                                 ALU.add, ALU.mult).then_inc(hidden_out.sem, 1)
                    if s:
                        r = s - 1
                        k, tiles = r // 3, BLOCKS[r % 3]
                        for g in tiles:
                            n = k * TILES + g
                            dve.wait_ge(pe_y.sem, pe_y.at(q, n + 1))
                            dve.wait_ge(y_read.sem, y_read.at(q, n + 1 - TILES))
                            dve.scalar_tensor_tensor(S.h[:, g, :], S.ps[0:TILE, 6 + n % 2, 0:DIM],
                                                     X.cw[:, g, bass.ds(2 * q + k, 1)], S.h[:, g, :],
                                                     ALU.mult, ALU.add).then_inc(y_read.sem, 1)
            dve.wait_ge(y_read.sem, y_read.at(ALL // 2 - 1, 2 * TILES))


def stage_end(nc, S, out):
    with ExitStack() as ctx:
        sem = ctx.enter_context(stage_semaphores(nc))
        stored = sem("stored")
        block = ctx.enter_context(nc.Block())

        @block.sync
        def _(sp):
            whole = TILES - 1
            sp.dma_start(out[0:whole * GROUP].rearrange("(g b) l d -> (b l) g d", b=GROUP),
                         S.h[:, 0:whole, :]).then_inc(stored, 16)
            left = IMAGES - whole * GROUP
            sp.dma_start(out[whole * GROUP:IMAGES].rearrange("b l d -> (b l) d"), S.h[0:left * LEN, whole, :]).then_inc(stored, 16)
            sp.wait_ge(stored, 32)


def vit_tower(nc, IN, out):
    scratch_in = nc.dram_tensor("conv_scratch_in", [DIM, TOKENS], F32).ap()
    scratch_out = nc.dram_tensor("conv_scratch_out", [DIM, TOKENS], F32).ap()
    with ExitStack() as ctx:
        S = allocate(nc, ctx)
        stage_start(nc, S, IN)
        stage_patches_and_convolution(nc, S, IN, scratch_in, scratch_out)
        stage_small_attention(nc, S, IN)
        stage_large_attention(nc, S, IN)
        stage_sharp_attention(nc, S, IN)
        stage_linear_experts(nc, S, IN)
        stage_difference_attention(nc, S, IN)
        stage_two_layer_experts(nc, S, IN)
        stage_decay_attention(nc, S, IN)
        stage_gated_experts(nc, S, IN)
        stage_end(nc, S, out)


def tiled(a):
    a = np.concatenate([a, a[-1:]], 0)
    return np.ascontiguousarray(a.reshape(TILES, TILE, -1).transpose(1, 0, 2))


def rows_of(w, rows):
    *lead, k, n = w.shape
    return np.ascontiguousarray(np.moveaxis(w.reshape(*lead, k // rows, rows, n), -3, -2))


def spread(v):
    return np.broadcast_to(v[..., None, :], (*v.shape[:-1], TILE, v.shape[-1])).copy()


def lay_out(i):
    f = np.float32
    o = {}
    img = np.arange(TILE) // LEN
    off = np.where(img[:, None] == img[None, :], 0.0, OFF).astype(f)
    o["ident"] = np.eye(128, dtype=f)
    o["image_mask"] = np.tile(off, (1, 6))
    rows = np.arange(128)
    o["hmask16"] = (rows[:, None] // 16 == np.arange(12)[None, :]).astype(f)
    o["hmask64"] = (rows[:, None] // 64 == np.arange(12)[None, :]).astype(f)
    a = {k[8:]: v for k, v in i.items() if k.startswith("L0_attn_")}
    nl = a["Wq"].shape[0]
    o["a_qkv"] = np.concatenate([rows_of(a[k], HALF) for k in ("Wq", "Wk", "Wv")], -1)
    o["a_qkb"] = np.concatenate([a[k].reshape(nl, 2, HALF).transpose(0, 2, 1) for k in ("bq", "bk")], -1)
    o["a_vob"] = np.concatenate([spread(a["bv"]), spread(a["bo"])], -1)
    wo = np.zeros((nl, 12, 32, DIM), f)
    wo[:, :, :16] = a["Wo"].reshape(nl, 12, 16, DIM)
    o["a_wo"] = rows_of(wo.reshape(nl, 384, DIM), 96)
    o["a_ln1"] = np.concatenate([spread(a["ln1_g"]), spread(a["ln1_b"])], -1)
    o["a_w1"] = rows_of(a["W1"], HALF)
    o["a_b1"] = a["b1"].reshape(nl, FCH, 128).transpose(0, 2, 1)
    o["a_w2"] = rows_of(a["W2"], 128)
    o["a_ln2"] = np.concatenate([spread(a[k]) for k in ("b2", "ln2_g", "ln2_b")], -1)
    b = {k[7:]: v for k, v in i.items() if k.startswith("L0_ffn_")}
    o["b_qkv"] = np.concatenate([rows_of(b[k], HALF) for k in ("attn_q", "attn_k", "attn_v")], -1)
    o["b_wo"] = rows_of(b["attn_o"], 128)
    o["b_w1"], o["b_w2"] = rows_of(b["ffn_wi"], HALF), rows_of(b["ffn_wo"], 128)
    o["b_m1"], o["b_m2"] = rows_of(b["moe_w1"], HALF), rows_of(b["moe_w2"], 128)
    o["b_gate"] = rows_of(b["gate_w"], HALF)
    gains = np.stack([b["ln1"], b["ln2"]], 1).reshape(-1, DIM)
    o["b_gains"] = spread(np.concatenate([gains, b["ln_f"][None]], 0)).transpose(1, 0, 2)
    pos = np.arange(TILE) % LEN
    far = pos[None, :] - pos[:, None]
    dist = np.abs(far)
    edges = np.array([8, 12, 16, 23, 32])
    bucket = 16 * (far > 0) + np.where(dist < 8, dist, 7 + (dist[..., None] >= edges).sum(-1))
    table = b["rel_emb"][bucket].transpose(0, 2, 1)
    o["b_bias"] = np.where((img[:, None] == img[None, :])[:, None, :], table, f(OFF)).reshape(TILE, 12 * TILE)
    e8 = np.arange(8)
    o["before8"] = np.broadcast_to((e8[None, :] < e8[:, None]).astype(f), (TILE, 8, 8))
    wt = i["L1_attn_W_qkv"].T
    o["g_qkv"] = rows_of(wt, HALF)
    o["g_wo"] = rows_of(i["L1_attn_W_out"].T, 128)
    o["e_router"] = rows_of(i["L1_ffn_router_w"].T, HALF)
    o["e_router_bias"] = spread(i["L1_ffn_router_b"])
    o["e_out_bias"] = i["L1_ffn_expert_b"]
    o["e_w"] = rows_of(i["L1_ffn_expert_w"].transpose(2, 0, 1).reshape(DIM, -1), HALF).reshape(HALF, 2, 8, DIM)
    o["d_qkv"] = rows_of(i["L2_attn_W_attn"].T, HALF)
    o["d_wo"] = rows_of(i["L2_attn_W_out"].T, HALF)
    o["d_lambda"] = spread(np.stack([i["L2_attn_lambda_" + k] for k in ("q1", "q2", "k1", "k2")])).transpose(1, 0, 2)
    o["f_router"] = rows_of(i["L2_ffn_gate_w"], HALF)
    o["f_router_bias"] = spread(i["L2_ffn_gate_b"])
    o["f_w1"], o["f_w2"] = rows_of(i["L2_ffn_w1"], HALF), rows_of(i["L2_ffn_w2"], 128)
    o["f_b1"] = i["L2_ffn_b1"].reshape(8, FCH, 128).transpose(0, 2, 1)
    o["f_out_bias"] = i["L2_ffn_b2"]
    o["h_qkv"] = rows_of(i["L3_attn_W_qkv"], HALF)
    o["h_qk_bias"] = i["L3_attn_b_qkv"][:2 * DIM].reshape(4, HALF).T
    o["h_v_bias"] = spread(i["L3_attn_b_qkv"][2 * DIM:])
    back = pos[None, :] - pos[:, None]
    o["h_decay"] = np.where((img[:, None] == img[None, :]) & (back >= 0), f(0.99) ** np.maximum(back, 0).astype(f), f(0))
    x = {k[7:]: v for k, v in i.items() if k.startswith("L3_ffn_")}
    o["i_router"] = rows_of(x["router_w"].T, HALF)
    o["i_router_bias"] = np.concatenate([spread(x["router_b"]), spread(x["corr_bias"])], -1)
    o["i_out_bias"] = np.concatenate([x["gbd"], x["sbd"][None], np.zeros((1, DIM), f)], 0)

    def halves(w):
        return np.stack([w[:, :HALF], w[:, HALF:]], 0)

    wg, wu = np.concatenate([x["gWg"], halves(x["sWg"])], 0), np.concatenate([x["gWu"], halves(x["sWu"])], 0)
    wd = np.concatenate([x["gWd"], x["sWd"].reshape(2, HALF, DIM)], 0)
    bg, bu = np.concatenate([x["gbg"], x["sbg"].reshape(2, HALF)], 0), np.concatenate([x["gbu"], x["sbu"].reshape(2, HALF)], 0)
    gu = rows_of(np.concatenate([wg, wu], -1), HALF).reshape(18, HALF, 2 * DIM)
    o["i_w"] = np.concatenate([gu, wd, bg[..., None], bu[..., None]], -1)
    e16 = np.arange(16)
    o["before16"] = np.broadcast_to((e16[None, :] < e16[:, None]).astype(f), (TILE, 16, 16))
    s = SIDE // PATCH
    im = np.concatenate([i["x"], i["x"][-1:]], 0).reshape(PADDED, CHANNELS, s, PATCH, s, PATCH)
    im = im.transpose(3, 5, 1, 0, 2, 4).reshape(PATCH_DIM, TOKENS)
    o["t_patches"] = rows_of(im, 128)
    o["t_w"] = rows_of(i["L0_tok_W"].T, 128)
    o["t_bias"] = spread(i["L0_tok_b"])
    o["t_ln0"] = np.concatenate([spread(a["ln0_g"]), spread(a["ln0_b"])], -1)
    cw = a["pos_conv_w"].reshape(CONV_GROUPS, CONV_CH, CONV_CH, CONV_K)
    apart = np.arange(CONV_D) - (CONV_BLOCKS - 1)
    j = np.arange(CONV_J)
    k = CONV_K // 2 + j[:, None, None] - j - CONV_J * apart[:, None]
    o["t_taps"] = cw[:, :, :, k].transpose(2, 3, 0, 4, 1, 5).reshape(TILE, CONV_GROUPS, CONV_D, TILE)
    o["t_conv_bias"] = np.repeat(a["pos_conv_b"].reshape(CONV_GROUPS, CONV_CH).T, CONV_J, 0)
    return {k: np.ascontiguousarray(v) for k, v in o.items()}


_SHAPE = (IMAGES, LEN, DIM)


def kernel(**inputs):
    import concourse.bacc as _bacc
    from concourse.bass_utils import run_bass_kernel_spmd as _run

    nc = _bacc.Bacc("TRN2", target_bir_lowering=False, num_devices=1)
    arrays, args = {}, {}
    for name, a in lay_out({k: np.asarray(v) for k, v in inputs.items()}).items():
        arrays[f"in_{name}"] = a
        args[name] = nc.dram_tensor(f"in_{name}", a.shape, mybir.dt.from_np(a.dtype), kind="ExternalInput").ap()
    out = nc.dram_tensor("out_tower", _SHAPE, F32, kind="ExternalOutput").ap()
    vit_tower(nc, args, out)
    return _run(nc, [arrays], core_ids=[0]).results[0]["out_tower"]
```

```python
from contextlib import ExitStack, contextmanager

import numpy as np
import concourse.bass as bass
from concourse import mybir

F32 = mybir.dt.float32
I32 = mybir.dt.int32
ALU = mybir.AluOpType
ACT = mybir.ActivationFunctionType
AX = mybir.AxisListType

IMAGES, SIDE, PATCH, CHANNELS = 32, 96, 16, 3
LEN = (SIDE // PATCH) ** 2
GROUP = 3
TILE = GROUP * LEN
TILES = -(-IMAGES // GROUP)
PADDED = TILES * GROUP
TOKENS = TILES * TILE
DIM, FF = 192, 768
HALF = DIM // 2
BLOCKS = [[0, 1, 2, 3], [4, 5, 6, 7], [8, 9, 10]]
BLOCK_TILES = 4
FCH = FF // 128
PATCH_DIM = CHANNELS * PATCH * PATCH
OFF = -1e30
BANK = 512

CONV_GROUPS, CONV_CH, CONV_K = 16, 12, 128
CONV_J = 9
CONV_BLOCKS = LEN // CONV_J
CONV_D = 2 * CONV_BLOCKS - 1

MAGIC = float(0x5F3759DF)


@contextmanager
def stage_semaphores(nc):
    made = []

    def semaphore(name):
        made.append(nc.alloc_semaphore(name=name))
        return made[-1]

    yield semaphore
    nc.clear_and_free_semaphores(made)
    nc.all_engine_barrier()


class Loop:

    def __init__(self, sem, per, lead=0):
        self.sem, self.per, self.lead = sem, per, lead

    def at(self, turn, k):
        assert 1 - self.lead <= k <= self.per, (self.sem.name, k, self.per)
        return turn * self.per + (self.lead + k)


class Own:

    def __init__(self, sem):
        self.sem, self.n = sem, 0

    def up(self):
        self.n += 1
        return 1

    def restart(self):
        self.n = 0



def rsqrt_small(dve, own, y, v, t, i):
    dve.tensor_scalar(i, v.bitcast(I32), 1, None, ALU.logical_shift_right).then_inc(own.sem, own.up())
    dve.wait_ge(own.sem, own.n)
    dve.tensor_scalar(y.bitcast(I32), i, -1.0, MAGIC, ALU.mult, ALU.add).then_inc(own.sem, own.up())
    for _ in range(3):
        dve.wait_ge(own.sem, own.n)
        dve.tensor_tensor(t, y, v, ALU.mult).then_inc(own.sem, own.up())
        dve.wait_ge(own.sem, own.n)
        dve.scalar_tensor_tensor(t, t, -0.5, y, ALU.mult, ALU.mult).then_inc(own.sem, own.up())
        dve.wait_ge(own.sem, own.n)
        dve.scalar_tensor_tensor(y, t, 1.5, y, ALU.add, ALU.mult).then_inc(own.sem, own.up())
    dve.wait_ge(own.sem, own.n)


def norm_stats(dve, own, S, tiles, src):
    for g in tiles:
        dve.bn_stats(S.stats[:, g, :], src[:, g, :]).then_inc(own.sem, own.up())
    dve.wait_ge(own.sem, own.n)
    for g in tiles:
        dve.bn_aggr(S.meanvar[:, g, :], S.stats[:, g, :]).then_inc(own.sem, own.up())


def norm_scale(dve, own, S, tiles, eps, root=False):
    n, a = len(tiles), tiles[0]
    mean, var = S.meanvar[:, a:a + n, 0], S.meanvar[:, a:a + n, 1]
    v, y, t, i = S.small[:, 0, 0:n], S.rstd[:, a:a + n], S.small[:, 1, 0:n], S.smalli[:, 0:n]
    dve.wait_ge(own.sem, own.n)
    if root:
        dve.tensor_tensor(t, mean, mean, ALU.mult).then_inc(own.sem, own.up())
        dve.wait_ge(own.sem, own.n)
        dve.scalar_tensor_tensor(v, t, eps, var, ALU.add, ALU.add).then_inc(own.sem, own.up())
    else:
        dve.tensor_scalar(v, var, eps, None, ALU.add).then_inc(own.sem, own.up())
    dve.wait_ge(own.sem, own.n)
    rsqrt_small(dve, own, y, v, t, i)


def norm_apply(dve, own, S, tiles, src, dst, done, gain=None, shift=None, root=False):
    def signal(ins):
        ins.then_inc(own.sem, own.up()) if done is None else ins.then_inc(done, 1)

    if gain is None:
        for g in tiles:
            signal(dve.tensor_scalar(dst[:, g, :], src[:, g, :], S.meanvar[:, g, 0:1], S.rstd[:, g:g + 1],
                                     ALU.subtract, ALU.mult))
        return
    if root:
        for g in tiles:
            signal(dve.scalar_tensor_tensor(dst[:, g, :], src[:, g, :], S.rstd[:, g:g + 1], gain,
                                            ALU.mult, ALU.mult))
        return
    for g in tiles:
        dve.scalar_tensor_tensor(dst[:, g, :], src[:, g, :], S.meanvar[:, g, 0:1], gain,
                                 ALU.subtract, ALU.mult).then_inc(own.sem, own.up())
    dve.wait_ge(own.sem, own.n)
    for g in tiles:
        signal(dve.scalar_tensor_tensor(dst[:, g, :], dst[:, g, :], S.rstd[:, g:g + 1], shift,
                                        ALU.mult, ALU.add))


def normalise(dve, own, S, tiles, src, dst, eps, gain=None, shift=None, root=False, done=None):
    norm_stats(dve, own, S, tiles, src)
    norm_scale(dve, own, S, tiles, eps, root)
    norm_apply(dve, own, S, tiles, src, dst, done, gain, shift, root)



TURN_LAG, OUT_LAG = 2, 3


class Heads:

    def __init__(self, rows, chunks, in_chunk, per_bank, slot, out_chunks, out_rows, v_heads, v_width, v_tiles,
                 scale, shared=False, mask_rows=0):
        self.shared, self.mask_rows = shared, mask_rows
        self.rows, self.chunks, self.in_chunk, self.per_bank = rows, chunks, in_chunk, per_bank
        self.slot, self.out_chunks, self.out_rows = slot, out_chunks, out_rows
        self.v_heads, self.v_width, self.v_tiles = v_heads, v_width, v_tiles
        self.scale = scale
        self.in_unit = 2 * per_bank
        self.units = chunks * in_chunk // self.in_unit
        self.width = per_bank * TILE
        self.outs = out_chunks // self.units

    def bank(self, unit, i):
        first = unit * self.in_unit + i * self.per_bank
        return first // self.in_chunk, first % self.in_chunk * TILE


SPREAD = HALF + 16
SMALL = Heads(96, 2, 6, 3, SPREAD, 2, 96, 12, 16, 1, 16 ** -0.5, shared=True, mask_rows=GROUP)
LARGE = Heads(128, 6, 2, 2, 64, 6, 128, 12, 64, 2, 1.0)


def pe_transpose(pe, S, A, turn, blk, src, ready, done, out):
    for g in BLOCKS[blk]:
        pe.wait_ge(ready.sem, ready.at(turn, g + 1))
        if g >= 2:
            pe.wait_ge(out.sem, out.at(turn, g - 1))
        for c in range(2):
            ins = pe.transpose(S.ps[0:HALF, 4 + g % 2, c * TILE:(c + 1) * TILE],
                               src[:, g, c * HALF:(c + 1) * HALF], S.ident[0:TILE, 0:TILE])
        ins.then_inc(done.sem, 1)


def act_transposed(act, S, A, turn, blk, done, out):
    for g in BLOCKS[blk]:
        act.wait_ge(done.sem, done.at(turn, g + 1))
        act.activation(S.xt[:, :, g * TILE:(g + 1) * TILE],
                       S.ps[0:HALF, 4 + g % 2, 0:2 * TILE].rearrange("p (c t) -> p c t", c=2),
                       ACT.Copy).then_inc(out.sem, 1)


def pe_queries_keys(pe, S, A, turn, blk, c):
    hd, tiles = A.heads, BLOCKS[blk]
    c0, cols = tiles[0] * TILE, len(tiles) * TILE
    if c == 0:
        pe.wait_ge(A.w_qkv.sem, A.w_qkv.at(turn, A.w_qkv.per))
        pe.wait_ge(A.xt_out.sem, A.xt_out.at(turn, tiles[-1] + 1))
    if c >= 2:
        pe.wait_ge(A.q_out.sem, A.q_out.at(turn, blk * hd.chunks + c - 1))
        pe.wait_ge(A.k_out.sem, A.k_out.at(turn, blk * hd.chunks + c - 1))
        pe.wait_ge(A.k_spread.sem, A.k_spread.at(turn, blk * hd.chunks + c - 1))
    elif blk:
        pe.wait_ge(A.s_free.sem, A.s_free.at(turn, tiles[0] * hd.units - 1 + c))
    for keys, w in enumerate((A.wq, A.wk)):
        for kc in range(2):
            ins = pe.matmul(S.ps[0:hd.rows, (2 * c + keys) % 4, 0:cols], w[:, kc, c * hd.rows:(c + 1) * hd.rows],
                            S.xt[:, kc, c0:c0 + cols], start=kc == 0, stop=kc == 1)
        ins.then_inc(A.pe_qk.sem, 1)


def pe_values(pe, S, A, turn, blk, emptied):
    hd, tiles = A.heads, BLOCKS[blk]
    n = tiles[0] * hd.v_tiles
    wide = hd.v_heads * hd.v_width // hd.v_tiles
    if blk:
        pe.wait_ge(A.o_out.sem, A.o_out.at(turn, tiles[0] * hd.units))
    else:
        free, at_turn, count = emptied
        pe.wait_ge(free.sem, free.at(at_turn, count))
    for g in tiles:
        for vt in range(hd.v_tiles):
            if n >= tiles[0] * hd.v_tiles + 2:
                pe.wait_ge(A.v_out.sem, A.v_out.at(turn, n - 1))
            for kc in range(2):
                ins = pe.matmul(S.ps[0:TILE, 6 + n % 2, 0:wide], S.xt[:, kc, g * TILE:(g + 1) * TILE],
                                A.wv[:, kc, vt * wide:(vt + 1) * wide], start=kc == 0, stop=kc == 1)
            ins.then_inc(A.pe_v.sem, 1)
            n += 1


def pe_attend(pe, S, A, turn, blk, src):
    hd, tiles = A.heads, BLOCKS[blk]
    base, count = tiles[0] * hd.units, len(tiles) * hd.units
    pb, w = hd.per_bank, hd.width
    pe.wait_ge(A.q_out.sem, A.q_out.at(turn, (blk + 1) * hd.chunks))
    pe.wait_ge(A.k_out.sem, A.k_out.at(turn, (blk + 1) * hd.chunks))
    pe.wait_ge(A.k_spread.sem, A.k_spread.at(turn, (blk + 1) * hd.chunks))
    for s in range(count + OUT_LAG):
        if s == 2:
            if blk:
                pe_project(pe, S, A, turn, blk - 1)
            else:
                for b in (1, 2):
                    pe_transpose(pe, S, A, turn, b, src, A.x_ready, A.pe_xt, A.xt_out)
        if s < count:
            n, lg, u = base + s, s // hd.units, s % hd.units
            if s >= 2:
                pe.wait_ge(A.s_free.sem, A.s_free.at(turn, n - 1))
            for i in range(2):
                c, k0 = hd.bank(u, i)
                ins = pe.matmul(S.ps[0:TILE, 2 * (s % 2) + i, 0:w], S.qt[0:hd.rows + hd.mask_rows, c, lg * TILE:(lg + 1) * TILE],
                                A.kb[:, c, lg, k0:k0 + w], start=True, stop=True)
            ins.then_inc(A.pe_s.sem, 1)
        if TURN_LAG <= s < count + TURN_LAG:
            r = s - TURN_LAG
            pe.wait_ge(A.p_norm.sem, A.p_norm.at(turn, base + r + 1))
            if r:
                pe.wait_ge(A.pt_out.sem, A.pt_out.at(turn, base + r))
            elif blk == 0:
                pe.wait_ge(A.xt_out.sem, A.xt_out.at(turn, TILES))
            for h in range(2 * pb):
                ins = pe.transpose(S.ps[0:TILE, 4 + h // pb, h % pb * TILE:(h % pb + 1) * TILE],
                                   S.p[:, r % 4, h * TILE:(h + 1) * TILE], S.ident[0:TILE, 0:TILE])
            ins.then_inc(A.pe_pt.sem, 1)
        if s >= OUT_LAG:
            r = s - OUT_LAG
            lg, u = r // hd.units, r % hd.units
            pe.wait_ge(A.pt_out.sem, A.pt_out.at(turn, base + r + 1))
            if r == 0:
                pe.wait_ge(A.v_out.sem, A.v_out.at(turn, (tiles[-1] + 1) * hd.v_tiles))
                if blk:
                    pe.wait_ge(A.y_read.sem, A.y_read.at(turn, tiles[0]))
            if r >= 2:
                pe.wait_ge(A.o_out.sem, A.o_out.at(turn, base + r - 1))
            for h in range(2 * pb):
                turned = S.pt[:, r % 2, h * TILE:(h + 1) * TILE]
                if hd.shared:
                    v0 = u * SPREAD * hd.in_unit + h * hd.rows
                    ins = pe.matmul(S.ps[0:hd.rows, 6 + r % 2, 0:TILE], A.v[:, lg, v0:v0 + hd.rows], turned,
                                    start=h == 0, stop=h == 2 * pb - 1)
                else:
                    vh, j, i = u * 2 * pb + h, h % pb, h // pb
                    ins = pe.matmul(S.ps[j * hd.slot:(j + 1) * hd.slot, 6 + r % 2, i * TILE:(i + 1) * TILE],
                                    A.v[:, lg, vh * hd.slot:(vh + 1) * hd.slot], turned, start=True, stop=True)
            ins.then_inc(A.pe_o.sem, 1)
        if blk < 2 and count <= s < count + 2:
            pe_queries_keys(pe, S, A, turn, blk + 1, s - count)


def pe_attention(pe, S, A, turn, src, emptied):
    hd = A.heads
    pe_transpose(pe, S, A, turn, 0, src, A.x_ready, A.pe_xt, A.xt_out)
    for b in range(3):
        for c in range(2 if b else 0, hd.chunks):
            pe_queries_keys(pe, S, A, turn, b, c)
        pe_values(pe, S, A, turn, b, emptied)
        pe_attend(pe, S, A, turn, b, src)
    pe_project(pe, S, A, turn, 2)


def pe_project(pe, S, A, turn, blk):
    hd, tiles = A.heads, BLOCKS[blk]
    pe.wait_ge(A.w_o.sem, A.w_o.at(turn, A.w_o.per))
    pe.wait_ge(A.o_out.sem, A.o_out.at(turn, (tiles[-1] + 1) * hd.units))
    if blk < 2:
        pe.wait_ge(A.v_out.sem, A.v_out.at(turn, (BLOCKS[blk + 1][-1] + 1) * hd.v_tiles))
    for lg, g in enumerate(tiles):
        if lg >= 2:
            pe.wait_ge(A.y_read.sem, A.y_read.at(turn, g - 1))
        for c in range(hd.out_chunks):
            ins = pe.matmul(S.ps[0:TILE, 6 + lg % 2, 0:DIM], S.ot[0:hd.out_rows, c, lg * TILE:(lg + 1) * TILE],
                            A.wo[:, c, :], start=c == 0, stop=c == hd.out_chunks - 1)
        ins.then_inc(A.pe_y.sem, 1)


def act_queries_keys(act, S, A, turn, blk, c):
    hd, cols = A.heads, len(BLOCKS[blk]) * TILE
    act.wait_ge(A.pe_qk.sem, A.pe_qk.at(turn, (blk * hd.chunks + c) * 2 + 1))
    src, dst = S.ps[0:hd.rows, 2 * c % 4, 0:cols], S.qt[0:hd.rows, c, 0:cols]
    ins = act.activation(dst, src, ACT.Identity, bias=A.bq[:, c:c + 1]) if A.biased else \
        act.activation(dst, src, ACT.Copy)
    ins.then_inc(A.q_out.sem, 1)
    act.wait_ge(A.k_out.sem, A.k_out.at(turn, blk * hd.chunks + c + 1))
    src = S.ps[0:hd.rows, (2 * c + 1) % 4, 0:cols].rearrange("p (g t) -> p g t", t=TILE)
    for j in range(hd.in_chunk // 2):
        dst = A.kb[0:hd.rows, c, 0:len(BLOCKS[blk]), j * TILE:(j + 1) * TILE]
        head = S.hmask[0:hd.rows, j:j + 1]
        ins = act.activation(dst, src, ACT.Identity, scale=head, bias=A.bk_spread[:, c * 6 + j:c * 6 + j + 1]) \
            if A.biased else act.activation(dst, src, ACT.Copy, scale=head)
    ins.then_inc(A.k_spread.sem, 1)


def act_values(act, S, A, turn, blk):
    hd, tiles = A.heads, BLOCKS[blk]
    heads = hd.v_heads // hd.v_tiles
    for n in range(tiles[0] * hd.v_tiles, (tiles[-1] + 1) * hd.v_tiles):
        act.wait_ge(A.pe_v.sem, A.pe_v.at(turn, n + 1))
        lg, vt = n // hd.v_tiles - tiles[0], n % hd.v_tiles
        slots = A.v[:, lg, 0:hd.v_heads * hd.slot].rearrange("p (h d) -> p h d", d=hd.slot)
        act.activation(slots[:, vt * heads:(vt + 1) * heads, 0:hd.v_width],
                       S.ps[0:TILE, 6 + n % 2, 0:heads * hd.v_width].rearrange("p (h d) -> p h d", h=heads),
                       ACT.Copy).then_inc(A.v_out.sem, 1)


def act_attend(act, S, A, turn, blk):
    hd, tiles = A.heads, BLOCKS[blk]
    base, count = tiles[0] * hd.units, len(tiles) * hd.units
    for s in range(count + TURN_LAG):
        if s < count:
            act.wait_ge(A.s_max.sem, A.s_max.at(turn, base + s + 1))
            if hd.mask_rows and s >= 4:
                act.wait_ge(A.pe_pt.sem, A.pe_pt.at(turn, base + s - 3))
            for h in range(hd.in_unit):
                tile = S.p[:, s % 4, h * TILE:(h + 1) * TILE]
                src, scale = tile, 1.0
                if hd.mask_rows:
                    c0 = h % hd.per_bank * TILE
                    src, scale = S.ps[0:TILE, 2 * (s % 2) + h // hd.per_bank, c0:c0 + TILE], hd.scale
                ins = act.activation(tile, src, ACT.Exp, bias=S.nmax[:, s % 4, h:h + 1], scale=scale,
                                     accum_out=S.sums[:, s % 4, h:h + 1])
            ins.then_inc(A.p_exp.sem, 1)
        if s >= TURN_LAG:
            r = s - TURN_LAG
            act.wait_ge(A.pe_pt.sem, A.pe_pt.at(turn, base + r + 1))
            act.activation(S.pt[:, r % 2, 0:2 * hd.width].rearrange("p (b n) -> p b n", b=2),
                           S.ps[0:TILE, 4:6, 0:hd.width], ACT.Copy).then_inc(A.pt_out.sem, 1)
        if blk == 0 and s == 1:
            for b in (1, 2):
                act_transposed(act, S, A, turn, b, A.pe_xt, A.xt_out)
        if blk < 2 and count <= s < count + 2:
            act_queries_keys(act, S, A, turn, blk + 1, s - count)


def act_attention(act, S, A, turn):
    act_transposed(act, S, A, turn, 0, A.pe_xt, A.xt_out)
    for b in range(3):
        for c in range(2 if b else 0, A.heads.chunks):
            act_queries_keys(act, S, A, turn, b, c)
        act_values(act, S, A, turn, b)
        act_attend(act, S, A, turn, b)


def dve_keys(dve, S, A, turn, blk, c):
    hd, tiles = A.heads, BLOCKS[blk]
    dve.wait_ge(A.pe_qk.sem, A.pe_qk.at(turn, (blk * hd.chunks + c) * 2 + 2))
    src = S.ps[0:hd.rows, (2 * c + 1) % 4, 0:len(tiles) * TILE].rearrange("p (g t) -> p g t", t=TILE)
    for j in range(hd.in_chunk // 2, hd.in_chunk):
        dst = A.kb[0:hd.rows, c, 0:len(tiles), j * TILE:(j + 1) * TILE]
        if A.biased:
            ins = dve.tensor_scalar(dst, src, A.bk[:, c:c + 1], S.hmask[0:hd.rows, j:j + 1], ALU.add, ALU.mult)
        else:
            ins = dve.tensor_scalar(dst, src, S.hmask[0:hd.rows, j:j + 1], None, ALU.mult)
    ins.then_inc(A.k_out.sem, 1)


def dve_attend(dve, own, S, A, turn, blk, add):
    hd, tiles = A.heads, BLOCKS[blk]
    base, count = tiles[0] * hd.units, len(tiles) * hd.units
    wide = 2 * hd.width
    for s in range(count + OUT_LAG):
        if s < count:
            n, u = base + s, s % hd.units
            dve.wait_ge(A.pe_s.sem, A.pe_s.at(turn, n + 1))
            nmax = S.nmax[:, s % 4, 0:hd.in_unit]
            if hd.mask_rows:
                dve.tensor_reduce(nmax.rearrange("p (b h) -> p b h", b=2),
                                  S.ps[0:TILE, 2 * (s % 2):2 * (s % 2) + 2, 0:hd.width].rearrange(
                                      "p b (h t) -> p b h t", t=TILE),
                                  AX.X, ALU.max, negate=True).then_inc(own.sem, own.up())
                dve.wait_ge(own.sem, own.n)
                dve.tensor_scalar(nmax, nmax, hd.scale, None, ALU.mult).then_inc(A.s_max.sem, 1)
            else:
                if s >= 4:
                    dve.wait_ge(A.pe_pt.sem, A.pe_pt.at(turn, n - 3))
                p = S.p[:, s % 4, 0:wide]
                dve.scalar_tensor_tensor(p.rearrange("p (b n) -> p b n", b=2),
                                         S.ps[0:TILE, 2 * (s % 2):2 * (s % 2) + 2, 0:hd.width], hd.scale,
                                         A.mask(u), ALU.mult, ALU.add).then_inc(A.s_read.sem, 1)
                dve.wait_ge(A.s_read.sem, A.s_read.at(turn, n + 1))
                dve.tensor_reduce(S.nmax[:, s % 4, 0:hd.in_unit], p.rearrange("p (h t) -> p h t", t=TILE), AX.X, ALU.max,
                                  negate=True).then_inc(A.s_max.sem, 1)
        if blk and s == 1:
            add(BLOCKS[blk - 1][:2])
        if 1 <= s <= count:
            r = s - 1
            dve.wait_ge(A.p_exp.sem, A.p_exp.at(turn, base + r + 1))
            dve.reciprocal(S.recs[:, r % 4, 0:hd.in_unit], S.sums[:, r % 4, 0:hd.in_unit]).then_inc(own.sem, own.up())
            dve.wait_ge(own.sem, own.n)
            p = S.p[:, r % 4, 0:wide].rearrange("p (h t) -> p h t", t=TILE)
            dve.tensor_tensor(p, p, S.recs[:, r % 4, 0:hd.in_unit].unsqueeze(2).to_broadcast([TILE, hd.in_unit, TILE]),
                              ALU.mult).then_inc(A.p_norm.sem, 1)
        if s >= OUT_LAG:
            r = s - OUT_LAG
            lg, u = r // hd.units, r % hd.units
            dve.wait_ge(A.pe_o.sem, A.pe_o.at(turn, base + r + 1))
            dst = S.ot[0:hd.out_rows, u * hd.outs:(u + 1) * hd.outs, lg * TILE:(lg + 1) * TILE]
            src = S.ps[0:hd.out_rows, 6 + r % 2, 0:hd.outs * TILE].rearrange("p (c t) -> p c t", t=TILE)
            ins = dve.tensor_scalar(dst, src, A.bv[:, u:u + 1], None, ALU.add) if A.biased else \
                dve.tensor_copy(dst, src)
            ins.then_inc(A.o_out.sem, 1)
        if blk and s == 1:
            add(BLOCKS[blk - 1][2:])
        if blk < 2 and count <= s < count + 2:
            dve_keys(dve, S, A, turn, blk + 1, s - count)


def dve_attention(dve, own, S, A, turn, add, norm):
    for b in range(3):
        for c in range(2 if b else 0, A.heads.chunks):
            dve_keys(dve, S, A, turn, b, c)
        if b == 2 and norm is not None:
            norm(BLOCKS[0])
        dve_attend(dve, own, S, A, turn, b, add)
    add(BLOCKS[2])
    if norm is not None:
        norm(BLOCKS[1])
        norm(BLOCKS[2])



def pe_hidden(pe, S, F, turn, blk, load_turn=None):
    tiles = BLOCKS[blk]
    c0, cols = tiles[0] * TILE, len(tiles) * TILE
    load_turn = turn if load_turn is None else load_turn
    pe.wait_ge(F.w_1.sem, F.w_1.at(load_turn, F.w_1.per))
    for m in range(FCH):
        if m >= 4:
            pe.wait_ge(F.h_out.sem, F.h_out.at(turn, blk * FCH + m - 3))
        for kc in range(2):
            ins = pe.matmul(S.ps[:, m % 4, 0:cols], F.w1[:, kc, m * 128:(m + 1) * 128], S.xt[:, kc, c0:c0 + cols],
                            start=kc == 0, stop=kc == 1)
        ins.then_inc(F.pe_h.sem, 1)


def pe_outputs(pe, S, F, turn, blk, emptied, load_turn=None):
    tiles = BLOCKS[blk]
    load_turn = turn if load_turn is None else load_turn
    pe.wait_ge(F.w_2.sem, F.w_2.at(load_turn, F.w_2.per))
    if blk == 0:
        free, at_turn, count = emptied
        pe.wait_ge(free.sem, free.at(at_turn, count))
    for lg, g in enumerate(tiles):
        if g >= 2:
            pe.wait_ge(F.y_read.sem, F.y_read.at(turn, g - 1))
        for c in range(FCH):
            if lg == 0:
                pe.wait_ge(F.h_out.sem, F.h_out.at(turn, blk * FCH + c + 1))
            ins = pe.matmul(S.ps[0:TILE, 6 + g % 2, 0:DIM], S.h1[:, c, lg * TILE:(lg + 1) * TILE], F.w2[:, c, :],
                            start=c == 0, stop=c == FCH - 1)
        ins.then_inc(F.pe_y.sem, 1)


def pe_ff(pe, S, F, turn, blk, emptied, load_turn=None):
    pe_hidden(pe, S, F, turn, blk, load_turn)
    pe_outputs(pe, S, F, turn, blk, emptied, load_turn)


def pe_turned_ff(pe, S, A, F, turn, src):
    pe_transpose(pe, S, A, turn, 0, src, F.x_ready, F.pe_xt, F.xt_out)
    for b in range(3):
        pe.wait_ge(F.xt_out.sem, F.xt_out.at(turn, BLOCKS[b][-1] + 1))
        pe_hidden(pe, S, F, turn, b)
        if b < 2:
            pe_transpose(pe, S, A, turn, b + 1, src, F.x_ready, F.pe_xt, F.xt_out)
        pe_outputs(pe, S, F, turn, b, (A.y_read, turn, TILES))


def act_turned_ff(act, S, A, F, turn, func):
    act_transposed(act, S, A, turn, 0, F.pe_xt, F.xt_out)
    for b in range(3):
        act_ff(act, S, F, turn, b, func)
        if b < 2:
            act_transposed(act, S, A, turn, b + 1, F.pe_xt, F.xt_out)


def act_ff(act, S, F, turn, blk, func):
    cols = len(BLOCKS[blk]) * TILE
    for m in range(FCH):
        act.wait_ge(F.pe_h.sem, F.pe_h.at(turn, blk * FCH + m + 1))
        bias = F.b1[:, m:m + 1] if F.b1 is not None else 0.0
        act.activation(S.h1[:, m, 0:cols], S.ps[:, m % 4, 0:cols], func, bias=bias).then_inc(F.h_out.sem, 1)


def pe_router(pe, S, R, E, w):
    for g in range(TILES):
        for kc in range(2):
            ins = pe.matmul(S.ps[0:TILE, 4, g * E:(g + 1) * E], S.xt[:, kc, g * TILE:(g + 1) * TILE], w[:, kc, :],
                            start=kc == 0, stop=kc == 1)
    ins.then_inc(R.logits_done.sem, 1)


def dve_top_mask(dve, own, S, R, mask, scores, E, K, n=TILES):
    mine = scores.unsqueeze(3).to_broadcast([TILE, n, E, E])
    other = scores.unsqueeze(2).to_broadcast([TILE, n, E, E])
    gt = R.gt[:, 0:n * E * E].rearrange("p (n j k) -> p n j k", j=E, k=E)
    eq = R.eq[:, 0:n * E * E].rearrange("p (n j k) -> p n j k", j=E, k=E)
    dve.tensor_tensor(gt, other, mine, ALU.is_gt).then_inc(own.sem, own.up())
    dve.tensor_tensor(eq, other, mine, ALU.is_equal).then_inc(own.sem, own.up())
    dve.wait_ge(own.sem, own.n)
    dve.tensor_tensor(eq, eq, R.before[:, 0:E, 0:E].unsqueeze(1).to_broadcast([TILE, n, E, E]), ALU.mult).then_inc(own.sem, own.up())
    dve.wait_ge(own.sem, own.n)
    dve.tensor_tensor(gt, gt, eq, ALU.add).then_inc(own.sem, own.up())
    dve.wait_ge(own.sem, own.n)
    dve.tensor_reduce(mask, gt, AX.X, ALU.add).then_inc(own.sem, own.up())
    dve.wait_ge(own.sem, own.n)
    dve.tensor_scalar(mask, mask, float(K), None, ALU.is_lt).then_inc(own.sem, own.up())
    dve.wait_ge(own.sem, own.n)


def dve_route(dve, own, S, R, turn, E, K, bias=None, whole=True, eps=0.0):
    dve.wait_ge(R.logits_done.sem, R.logits_done.at(turn, 1))
    lg, ex, cw, mask, col = R.logits, R.ex, R.cw, R.mask, R.col
    src = S.ps[0:TILE, 4, 0:TILES * E].rearrange("p (g e) -> p g e", e=E)
    if bias is None:
        dve.tensor_copy(lg, src).then_inc(own.sem, own.up())
    else:
        dve.tensor_tensor(lg, src, bias.unsqueeze(1).to_broadcast([TILE, TILES, E]), ALU.add).then_inc(own.sem, own.up())
    dve.wait_ge(own.sem, own.n)

    def wide(c):
        return c.unsqueeze(2).to_broadcast([TILE, TILES, E])

    dve.tensor_reduce(col, lg, AX.X, ALU.max).then_inc(own.sem, own.up())
    dve.wait_ge(own.sem, own.n)
    dve.tensor_tensor(ex, lg, wide(col), ALU.subtract).then_inc(R.shifted.sem, 1)
    if not whole:
        dve_top_mask(dve, own, S, R, mask, lg, E, K)
    dve.wait_ge(R.exped.sem, R.exped.at(turn, 1))
    if whole:
        dve.tensor_reduce(col, ex, AX.X, ALU.add).then_inc(own.sem, own.up())
        dve.wait_ge(own.sem, own.n)
        dve.reciprocal(col, col).then_inc(own.sem, own.up())
        dve.wait_ge(own.sem, own.n)
        dve.tensor_tensor(ex, ex, wide(col), ALU.mult).then_inc(own.sem, own.up())
        dve.wait_ge(own.sem, own.n)
        dve_top_mask(dve, own, S, R, mask, ex, E, K)
    dve.tensor_tensor(ex, ex, mask, ALU.mult).then_inc(own.sem, own.up())
    dve.wait_ge(own.sem, own.n)
    dve.tensor_reduce(col, ex, AX.X, ALU.add).then_inc(own.sem, own.up())
    dve.wait_ge(own.sem, own.n)
    dve.tensor_scalar(col, col, eps, None, ALU.add).then_inc(own.sem, own.up())
    dve.wait_ge(own.sem, own.n)
    dve.reciprocal(col, col).then_inc(own.sem, own.up())
    dve.wait_ge(own.sem, own.n)
    dve.tensor_tensor(cw, ex, wide(col), ALU.mult).then_inc(own.sem, own.up())
    dve.wait_ge(own.sem, own.n)


def act_route(act, S, R, turn):
    act.wait_ge(R.shifted.sem, R.shifted.at(turn, 1))
    act.activation(R.ex, R.ex, ACT.Exp).then_inc(R.exped.sem, 1)


def router_buffers(nc, ctx, sem, prefix, E, per=1):
    R = Names()

    def sb(name, shape):
        return ctx.enter_context(nc.sbuf_tensor(prefix + name, shape, F32))

    R.gt, R.eq = sb("gt", [TILE, TILES * E * E])[:, :], sb("eq", [TILE, TILES * E * E])[:, :]
    R.before = sb("before", [TILE, E, E])
    R.logits, R.ex, R.cw, R.mask = (sb(n, [TILE, TILES, E])[:, :, :] for n in ("logits_sb", "ex", "cw", "top"))
    R.col = sb("col", [TILE, TILES])[:, :]
    R.logits_done, R.shifted, R.exped = (
        Loop(sem(prefix + n), per) for n in ("logits_done", "shifted", "exped"))
    return R


def dve_add_scaled(dve, S, F, turn, into, weight, tiles):
    for g in tiles:
        dve.wait_ge(F.pe_y.sem, F.pe_y.at(turn, g + 1))
        dve.wait_ge(F.y_read.sem, F.y_read.at(turn, g + 1 - TILES))
        dve.scalar_tensor_tensor(into[:, g, :], S.ps[0:TILE, 6 + g % 2, 0:DIM], weight(g), into[:, g, :],
                                 ALU.mult, ALU.add).then_inc(F.y_read.sem, 1)


def experts(nc, ctx, sem, prefix, biased):
    def sb(name, shape):
        return ctx.enter_context(nc.sbuf_tensor(prefix + name, shape, F32))

    def loop(name, per, lead=0):
        return Loop(sem(prefix + name), per, lead)

    pe_h, h_out, pe_y = loop("hidden", 3 * FCH), loop("hidden_out", 3 * FCH), loop("ff_done", TILES)
    y_read = loop("ff_read", TILES, lead=TILES)
    both = []
    for k in range(2):
        F = Names()
        F.w1, F.w2 = sb(f"w1_{k}", [HALF, 2, FF]), sb(f"w2_{k}", [128, FCH, DIM])
        F.b1 = sb(f"b1_{k}", [128, FCH]) if biased else None
        F.w_1, F.w_2 = loop(f"w1_loaded_{k}", 32 if biased else 16), loop(f"w2_loaded_{k}", 16)
        F.pe_h, F.h_out, F.pe_y, F.y_read = pe_h, h_out, pe_y, y_read
        both.append(F)
    return both


def sp_expert(sp, F, w1, w2, b1=None):
    sp.dma_start(F.w1[:, :, :], w1).then_inc(F.w_1.sem, 16)
    if b1 is not None:
        sp.dma_start(F.b1[:, :], b1).then_inc(F.w_1.sem, 16)
    sp.dma_start(F.w2[:, :, :], w2).then_inc(F.w_2.sem, 16)



class Names:
    pass


def stage_small_attention(nc, S, IN, layers=12):
    A, F = Names(), Names()
    with ExitStack() as ctx:
        sem = ctx.enter_context(stage_semaphores(nc))
        def sb(name, shape):
            return ctx.enter_context(nc.sbuf_tensor("sa_" + name, shape, F32))

        def loop(name, per, lead=0):
            return Loop(sem("sa_" + name), per, lead)

        hd = A.heads = SMALL
        A.biased = True
        gate = sb("qkv", [HALF, 2, 3 * DIM])
        A.wq, A.wk, A.wv = gate[:, :, 0:DIM], gate[:, :, DIM:2 * DIM], gate[:, :, 2 * DIM:3 * DIM]
        qkvb = sb("qkv_bias", [HALF, 18])
        A.bq, A.bk, A.bv, A.bk_spread = qkvb[:, 0:2], qkvb[:, 2:4], qkvb[:, 4:6], qkvb[:, 6:18]
        o_bias = sb("o_bias", [TILE, DIM])
        A.v = sb("values_apart", [TILE, BLOCK_TILES, 12 * SPREAD])
        A.wo = sb("wo", [hd.out_rows, hd.out_chunks, DIM])
        ln1 = sb("ln1", [TILE, 2 * DIM])
        F.w1 = sb("w1", [HALF, 2, FF])
        F.b1 = sb("b1", [128, FCH])
        F.w2 = sb("w2", [128, FCH, DIM])
        ln2 = sb("ln2", [TILE, 3 * DIM])
        A.kb = sb("keys_apart", [hd.rows + hd.mask_rows, hd.chunks, BLOCK_TILES, hd.in_chunk * TILE])
        plus = sb("x_plus_bias", [TILE, TILES, DIM])
        total = sb("sum", [TILE, TILES, DIM])

        units = TILES * hd.units
        A.w_qkv, A.w_o, F.w_1, F.w_2 = loop("qkv_loaded", 48), loop("wo_loaded", 32), loop("w1_loaded", 32), loop("w2_loaded", 32)
        A.x_ready, A.pe_xt, A.xt_out = loop("x_ready", TILES), loop("x_turned", TILES), loop("xt_out", TILES)
        A.pe_qk, A.q_out, A.k_out = loop("qk_done", 6 * hd.chunks), loop("q_out", 3 * hd.chunks), loop("k_out", 3 * hd.chunks)
        A.k_spread = loop("k_spread", 3 * hd.chunks)
        A.pe_v, A.v_out = loop("v_done", TILES), loop("v_out", TILES)
        A.pe_s, A.s_max, A.p_exp = (loop(n, units) for n in ("scores", "max", "exp"))
        A.s_free = A.p_exp
        A.p_norm, A.pe_pt, A.pt_out, A.pe_o, A.o_out = (loop(n, units) for n in ("probs", "probs_turned", "pt_out", "heads_done", "o_out"))
        A.pe_y, A.y_read, F.x_ready = loop("projected", TILES), loop("projected_read", TILES), loop("x1_ready", TILES)
        F.pe_xt, F.xt_out = loop("x1_turned", TILES), loop("xt1_out", TILES)
        F.pe_h, F.h_out = loop("hidden", 3 * FCH), loop("hidden_out", 3 * FCH)
        F.pe_y, F.y_read = loop("ff_done", TILES), loop("ff_read", TILES, TILES)
        plus_ready = loop("plus_ready", 6)
        own_dve, zeroed, mask_loaded = sem("sa_dve_own"), sem("sa_values_zeroed"), sem("sa_mask_loaded")
        block = ctx.enter_context(nc.Block())

        @block.sync
        def _(sp):
            def load_qkv(t):
                sp.dma_start(gate[:, :, :], IN["a_qkv"][t]).then_inc(A.w_qkv.sem, 16)
                sp.dma_start(qkvb[:, :], IN["a_qkvb"][t]).then_inc(A.w_qkv.sem, 16)
                sp.dma_start(o_bias[:, :], IN["a_ob"][t]).then_inc(A.w_qkv.sem, 16)

            def load_o(t):
                sp.dma_start(A.wo[:, :, :], IN["a_wo"][t]).then_inc(A.w_o.sem, 16)
                sp.dma_start(ln1[:, :], IN["a_ln1"][t]).then_inc(A.w_o.sem, 16)

            def load_1(t):
                sp.dma_start(F.w1[:, :, :], IN["a_w1"][t]).then_inc(F.w_1.sem, 16)
                sp.dma_start(F.b1[:, :], IN["a_b1"][t]).then_inc(F.w_1.sem, 16)

            def load_2(t):
                sp.dma_start(F.w2[:, :, :], IN["a_w2"][t]).then_inc(F.w_2.sem, 16)
                sp.dma_start(ln2[:, :], IN["a_ln2"][t]).then_inc(F.w_2.sem, 16)

            rows = slice(hd.rows, hd.rows + hd.mask_rows)
            sp.dma_start(S.qt[rows, 0:hd.chunks, :], IN["a_query_image"]).then_inc(mask_loaded, 16)
            sp.dma_start(A.kb[rows, :, :, :], IN["a_key_off"]).then_inc(mask_loaded, 16)
            load_qkv(0), load_o(0), load_1(0), load_2(0)
            with sp.Fori(0, layers - 1) as t:
                sp.wait_ge(A.pe_y.sem, A.pe_y.at(t, TILES))
                sp.wait_ge(plus_ready.sem, plus_ready.at(t, 3))
                load_qkv(t + 1)
                sp.wait_ge(F.x_ready.sem, F.x_ready.at(t, TILES))
                load_o(t + 1)
                sp.wait_ge(F.h_out.sem, F.h_out.at(t, 3 * FCH))
                load_1(t + 1)
                sp.wait_ge(A.x_ready.sem, A.x_ready.at(t + 1, TILES))
                load_2(t + 1)

        @block.tensor
        def _(pe):
            pe.wait_ge(mask_loaded, 32)
            with pe.Fori(0, layers) as t:
                pe_attention(pe, S, A, t, S.x, (F.y_read, t, 0))
                pe_turned_ff(pe, S, A, F, t, S.x)

        @block.scalar
        def _(act):
            act.wait_ge(zeroed, 1)
            with act.Fori(0, layers) as t:
                act.wait_ge(A.w_qkv.sem, A.w_qkv.at(t, A.w_qkv.per))
                act_attention(act, S, A, t)
                act_turned_ff(act, S, A, F, t, ACT.Gelu)

        @block.gpsimd
        def _(pool):
            def add(tiles, bias, done):
                pool.tensor_tensor(plus[:, tiles[0]:tiles[-1] + 1, :], S.x[:, tiles[0]:tiles[-1] + 1, :],
                                   bias.unsqueeze(1).to_broadcast([TILE, len(tiles), DIM]), ALU.add).then_inc(plus_ready.sem, 1)

            pool.memset(A.v[:, :, :], 0.0).then_inc(zeroed, 1)
            with pool.Fori(0, layers) as t:
                pool.wait_ge(A.w_qkv.sem, A.w_qkv.at(t, A.w_qkv.per))
                for b in range(3):
                    pool.wait_ge(A.x_ready.sem, A.x_ready.at(t, BLOCKS[b][-1] + 1))
                    add(BLOCKS[b], o_bias[:, :], plus_ready)
                pool.wait_ge(F.w_2.sem, F.w_2.at(t, F.w_2.per))
                for b in range(3):
                    pool.wait_ge(F.x_ready.sem, F.x_ready.at(t, BLOCKS[b][-1] + 1))
                    add(BLOCKS[b], ln2[:, 0:DIM], plus_ready)

        @block.vector
        def _(dve):
            own = Own(own_dve)
            dve.nop().then_inc(A.x_ready.sem, TILES)
            dve.nop().then_inc(F.y_read.sem, TILES)
            with dve.Fori(0, layers) as t:
                dve.wait_ge(A.w_qkv.sem, A.w_qkv.at(t, A.w_qkv.per))

                def add(tiles):
                    blk = tiles[0] // BLOCK_TILES
                    dve.wait_ge(plus_ready.sem, plus_ready.at(t, blk + 1))
                    for g in tiles:
                        dve.wait_ge(A.pe_y.sem, A.pe_y.at(t, g + 1))
                        dve.tensor_tensor(total[:, g, :], S.ps[0:TILE, 6 + g % 2, 0:DIM], plus[:, g, :],
                                          ALU.add).then_inc(A.y_read.sem, 1)

                def norm(tiles):
                    dve.wait_ge(A.y_read.sem, A.y_read.at(t, tiles[-1] + 1))
                    dve.wait_ge(A.w_o.sem, A.w_o.at(t, A.w_o.per))
                    normalise(dve, own, S, tiles, total, S.x, 1e-5, ln1[:, 0:DIM], ln1[:, DIM:2 * DIM],
                              done=F.x_ready.sem)

                dve_attention(dve, own, S, A, t, add, norm)
                dve.wait_ge(F.w_2.sem, F.w_2.at(t, F.w_2.per))
                for b in range(3):
                    dve.wait_ge(plus_ready.sem, plus_ready.at(t, 3 + b + 1))
                    for g in BLOCKS[b]:
                        dve.wait_ge(F.pe_y.sem, F.pe_y.at(t, g + 1))
                        dve.tensor_tensor(total[:, g, :], S.ps[0:TILE, 6 + g % 2, 0:DIM], plus[:, g, :],
                                          ALU.add).then_inc(F.y_read.sem, 1)
                    dve.wait_ge(F.y_read.sem, F.y_read.at(t, BLOCKS[b][-1] + 1))
                    normalise(dve, own, S, BLOCKS[b], total, S.x, 1e-5, ln2[:, DIM:2 * DIM], ln2[:, 2 * DIM:3 * DIM],
                              done=A.x_ready.sem)
                dve.sem_clear(own.sem)
                own.restart()
            dve.wait_ge(A.x_ready.sem, A.x_ready.at(layers, TILES))
            dve.tensor_tensor(S.h[:, :, :], S.h[:, :, :], S.x[:, :, :], ALU.add).then_inc(own.sem, own.up())
            dve.wait_ge(own.sem, own.n)


def attention_buffers(nc, ctx, sem, prefix, hd, S):
    A = Names()

    def loop(name, per, lead=0):
        return Loop(sem(prefix + name), per, lead)

    A.heads, A.biased, A.v = hd, False, S.v
    wide = hd.chunks * hd.rows
    w = A.w = ctx.enter_context(nc.sbuf_tensor(prefix + "qkv", [HALF, 2, 2 * wide + hd.v_heads * hd.v_width], F32))
    A.wq, A.wk, A.wv = w[:, :, 0:wide], w[:, :, wide:2 * wide], w[:, :, 2 * wide:]
    A.wo = ctx.enter_context(nc.sbuf_tensor(prefix + "wo", [hd.out_rows, hd.out_chunks, DIM], F32))
    A.kb = ctx.enter_context(nc.sbuf_tensor(
        prefix + "keys_apart", [hd.rows, hd.chunks, BLOCK_TILES, hd.in_chunk * TILE], F32))
    units = TILES * hd.units
    A.w_qkv, A.w_o = loop("qkv_loaded", 16), loop("wo_loaded", 16)
    A.x_ready, A.pe_xt, A.xt_out = loop("x_ready", TILES), loop("x_turned", TILES), loop("xt_out", TILES)
    A.pe_qk, A.q_out, A.k_out = loop("qk_done", 6 * hd.chunks), loop("q_out", 3 * hd.chunks), loop("k_out", 3 * hd.chunks)
    A.k_spread = loop("k_spread", 3 * hd.chunks)
    A.pe_v, A.v_out = loop("v_done", TILES * hd.v_tiles), loop("v_out", TILES * hd.v_tiles)
    A.pe_s, A.s_read, A.s_max, A.p_exp = (loop(n, units) for n in ("scores", "scores_read", "max", "exp"))
    A.s_free = A.s_read
    A.p_norm, A.pe_pt, A.pt_out, A.pe_o, A.o_out = (
        loop(n, units) for n in ("probs", "probs_turned", "pt_out", "heads_done", "o_out"))
    A.pe_y, A.y_read = loop("projected", TILES), loop("projected_read", TILES)
    return A


def dve_add_output(dve, S, P, turn, into, tiles, bank=None):
    for g in tiles:
        dve.wait_ge(P.pe_y.sem, P.pe_y.at(turn, g + 1))
        dve.tensor_tensor(into[:, g, :], S.ps[0:TILE, bank or 6 + g % 2, 0:DIM], into[:, g, :],
                          ALU.add).then_inc(P.y_read.sem, 1)
    dve.wait_ge(P.y_read.sem, P.y_read.at(turn, tiles[-1] + 1))


def stage_large_attention(nc, S, IN, pairs=2):
    E, K = 8, 2
    layers = 2 * pairs
    with ExitStack() as ctx:
        sem = ctx.enter_context(stage_semaphores(nc))
        hd = LARGE
        A = attention_buffers(nc, ctx, sem, "la_", hd, S)
        F = Names()

        def sb(name, shape):
            return ctx.enter_context(nc.sbuf_tensor("la_" + name, shape, F32))

        def loop(name, per, lead=0):
            return Loop(sem("la_" + name), per, lead)

        F.w1, F.b1, F.w2 = sb("w1", [HALF, 2, FF]), None, sb("w2", [128, FCH, DIM])
        bias = sb("position_bias", [TILE, 12 * TILE])
        gains = sb("gains", [TILE, 2 * layers + 1, DIM])
        normed = sb("normed", [TILE, TILES, DIM])
        A.mask = lambda u: bias[:, u * 2 * hd.width:(u + 1) * 2 * hd.width].rearrange("p (b n) -> p b n", b=2)
        F.w_1, F.w_2 = loop("w1_loaded", 16), loop("w2_loaded", 16)
        F.x_ready, F.pe_xt, F.xt_out = loop("x1_ready", TILES), loop("x1_turned", TILES), loop("xt1_out", TILES)
        F.pe_h, F.h_out = loop("hidden", 3 * FCH), loop("hidden_out", 3 * FCH)
        F.pe_y, F.y_read = loop("ff_done", TILES), loop("ff_read", TILES)
        R = router_buffers(nc, ctx, sem, "la_r_", E)
        gate = sb("gate", [HALF, 2, E])
        M = experts(nc, ctx, sem, "la_m_", False)
        MF = M[0]
        gate_loaded, consts = loop("gate_loaded", 16), loop("constants_loaded", 64)
        own_dve = sem("la_dve_own")
        block = ctx.enter_context(nc.Block())

        @block.sync
        def _(sp):
            def load_expert(m, e):
                sp_expert(sp, M[e % 2], IN["b_m1"][m, e], IN["b_m2"][m, e])

            sp.dma_start(A.w[:, :, :], IN["b_qkv"][0]).then_inc(A.w_qkv.sem, 16)
            sp.dma_start(gains[:, :, :], IN["b_gains"]).then_inc(consts.sem, 16)
            sp.dma_start(S.hmask[:, :], IN["hmask64"]).then_inc(consts.sem, 16)
            sp.dma_start(bias[:, :], IN["b_bias"]).then_inc(consts.sem, 16)
            sp.dma_start(R.before[:, :, :], IN["before8"]).then_inc(consts.sem, 16)
            sp.dma_start(A.wo[:, :, :], IN["b_wo"][0]).then_inc(A.w_o.sem, 16)
            sp.dma_start(F.w1[:, :, :], IN["b_w1"][0]).then_inc(F.w_1.sem, 16)
            sp.dma_start(F.w2[:, :, :], IN["b_w2"][0]).then_inc(F.w_2.sem, 16)
            sp.dma_start(gate[:, :, :], IN["b_gate"][0]).then_inc(gate_loaded.sem, 16)
            load_expert(0, 0), load_expert(0, 1)
            for t in range(layers):
                more = t + 1 < layers
                if more:
                    sp.wait_ge(A.v_out.sem, A.v_out.at(t, TILES * hd.v_tiles))
                    sp.dma_start(A.w[:, :, :], IN["b_qkv"][t + 1]).then_inc(A.w_qkv.sem, 16)
                    sp.wait_ge(F.x_ready.sem, F.x_ready.at(t, TILES))
                    sp.dma_start(A.wo[:, :, :], IN["b_wo"][t + 1]).then_inc(A.w_o.sem, 16)
                    sp.wait_ge(F.h_out.sem, F.h_out.at(t, 3 * FCH))
                    sp.dma_start(F.w1[:, :, :], IN["b_w1"][t + 1]).then_inc(F.w_1.sem, 16)
                    sp.wait_ge(F.y_read.sem, F.y_read.at(t, TILES))
                    sp.dma_start(F.w2[:, :, :], IN["b_w2"][t + 1]).then_inc(F.w_2.sem, 16)
                if t % 2 == 0:
                    continue
                m = t // 2
                for e in range(2, E + 2):
                    if e >= E and not more:
                        continue
                    sp.wait_ge(MF.y_read.sem, MF.y_read.at(E * m + e - 2, TILES))
                    if e == E:
                        sp.wait_ge(R.logits_done.sem, R.logits_done.at(m, 1))
                        sp.dma_start(gate[:, :, :], IN["b_gate"][m + 1]).then_inc(gate_loaded.sem, 16)
                    load_expert(m + e // E, e % E)

        @block.tensor
        def _(pe):
            with pe.Fori(0, pairs) as p:
                for odd in range(2):
                    t = 2 * p + odd
                    pe_attention(pe, S, A, t, normed, (A.x_ready, t, TILES))
                    pe_turned_ff(pe, S, A, F, t, normed)
                pe.wait_ge(gate_loaded.sem, gate_loaded.at(p, 16))
                pe.wait_ge(F.y_read.sem, F.y_read.at(2 * p + 1, TILES))
                pe_router(pe, S, R, E, gate)
                with pe.Fori(0, E // 2) as q:
                    for k in range(2):
                        e = p * E + 2 * q + k
                        for b in range(3):
                            pe_ff(pe, S, M[k], e, b, (MF.y_read, e, 0),
                                  load_turn=p * (E // 2) + q)

        @block.scalar
        def _(act):
            with act.Fori(0, pairs) as p:
                for odd in range(2):
                    t = 2 * p + odd
                    act_attention(act, S, A, t)
                    act_turned_ff(act, S, A, F, t, ACT.Relu)
                act_route(act, S, R, p)
                with act.Fori(0, E // 2) as q:
                    for k in range(2):
                        for b in range(3):
                            act_ff(act, S, M[k], p * E + 2 * q + k, b, ACT.Gelu)

        @block.vector
        def _(dve):
            own = Own(own_dve)
            dve.nop().then_inc(MF.y_read.sem, TILES)
            for b in range(3):
                normalise(dve, own, S, BLOCKS[b], S.h, S.x, 1e-5)
                dve.wait_ge(own.sem, own.n)
                if b == 0:
                    dve.wait_ge(consts.sem, consts.at(0, 64))
                normalise(dve, own, S, BLOCKS[b], S.x, normed, 1e-6, gains[:, 0, :], root=True, done=A.x_ready.sem)
            dve.sem_clear(own.sem)
            own.restart()
            with dve.Fori(0, pairs) as p:
                for odd in range(2):
                    t = 2 * p + odd

                    def add(tiles):
                        dve_add_output(dve, S, A, t, S.x, tiles)

                    def norm(tiles):
                        normalise(dve, own, S, tiles, S.x, normed, 1e-6, gains[:, 2 * t + 1, :], root=True,
                                  done=F.x_ready.sem)

                    dve_attention(dve, own, S, A, t, add, norm)
                    for b in range(3):
                        dve_add_output(dve, S, F, t, S.x, BLOCKS[b])
                        if odd == 0:
                            normalise(dve, own, S, BLOCKS[b], S.x, normed, 1e-6, gains[:, 2 * t + 2, :], root=True,
                                      done=A.x_ready.sem)
                dve_route(dve, own, S, R, p, E, K, whole=False)
                dve.sem_clear(own.sem)
                own.restart()
                with dve.Fori(0, E // 2) as q:
                    for k in range(2):
                        e = p * E + 2 * q + k
                        dve_add_scaled(dve, S, MF, e, S.x, lambda g: R.cw[:, g, bass.ds(2 * q + k, 1)], range(TILES))
                dve.wait_ge(MF.y_read.sem, MF.y_read.at(E * p + E - 1, TILES))
                for b in range(3):
                    normalise(dve, own, S, BLOCKS[b], S.x, normed, 1e-6, gains[:, 4 * p + 4, :], root=True,
                              done=A.x_ready.sem)
                dve.sem_clear(own.sem)
                own.restart()
            dve.wait_ge(A.x_ready.sem, A.x_ready.at(layers, TILES))
            dve.tensor_tensor(S.h[:, :, :], S.h[:, :, :], normed[:, :, :], ALU.add).then_inc(own.sem, own.up())
            dve.wait_ge(own.sem, own.n)


SHARP = Heads(128, 6, 2, 2, 64, 6, 128, 12, 64, 2, 8.0)


def stage_sharp_attention(nc, S, IN, prefix="g_", hd=SHARP):
    with ExitStack() as ctx:
        sem = ctx.enter_context(stage_semaphores(nc))
        A = attention_buffers(nc, ctx, sem, prefix, hd, S)
        A.mask = lambda u: S.mask[:, 0:2 * hd.width].rearrange("p (b n) -> p b n", b=2)
        small = sem(prefix + "constants_loaded")
        own_dve = sem(prefix + "dve_own")
        block = ctx.enter_context(nc.Block())

        @block.sync
        def _(sp):
            sp.dma_start(A.w[:, :, :], IN[prefix + "qkv"]).then_inc(A.w_qkv.sem, 16)
            sp.dma_start(S.hmask[:, :], IN["hmask64"]).then_inc(small, 16)
            sp.dma_start(A.wo[:, :, :], IN[prefix + "wo"]).then_inc(A.w_o.sem, 16)

        @block.tensor
        def _(pe):
            pe_attention(pe, S, A, 0, S.x, (A.x_ready, 0, TILES))

        @block.scalar
        def _(act):
            act_attention(act, S, A, 0)

        @block.vector
        def _(dve):
            own = Own(own_dve)
            for b in range(3):
                normalise(dve, own, S, BLOCKS[b], S.h, S.x, 1e-5, done=A.x_ready.sem)
            dve.wait_ge(small, 16)

            def add(tiles):
                dve_add_output(dve, S, A, 0, S.h, tiles)

            dve_attention(dve, own, S, A, 0, add, None)


def stage_difference_attention(nc, S, IN, prefix="d_"):
    NH, HD = 12, 8
    PAIRS = NH * NH
    init = 0.8 - 0.6 * float(np.exp(-0.3 * 12))
    with ExitStack() as ctx:
        sem = ctx.enter_context(stage_semaphores(nc))
        A = Names()

        def sb(name, shape):
            return ctx.enter_context(nc.sbuf_tensor(prefix + name, shape, F32))

        def loop(name, per):
            return Loop(sem(prefix + name), per)

        w, wo = sb("qkv", [HALF, 2, 3 * DIM]), sb("wo", [HALF, 2, DIM])
        lam, dots, coef = sb("lambda", [TILE, 4, HD]), sb("dots", [TILE, 4]), sb("coef", [TILE, 2])
        qkv = sb("qkv_rows", [TILE, 3, 3 * DIM])
        prod = sb("products", [TILE, 2, PAIRS, HD])
        vprod = sb("value_products", [TILE, 2, DIM, NH])
        att = sb("attention", [TILE, 2, 2 * NH, NH])
        both = sb("difference", [TILE, 2, PAIRS])
        col = sb("col", [TILE, 2, 2 * NH])
        y = sb("outputs", [TILE, 2, DIM])
        yt = sb("outputs_T", [HALF, 2, 2, TILE])
        A.x_ready, A.pe_xt, A.xt_out = loop("x_ready", TILES), loop("x_turned", TILES), loop("xt_out", TILES)
        w_loaded, small = loop("weights_loaded", 32), loop("lambda_loaded", 16)
        dots_ready, dots_exped = loop("dots_ready", 1), loop("dots_exped", 1)
        pe_qkv_done, qkv_out = loop("qkv_done", TILES), loop("qkv_out", TILES)
        shifted, exped, diff, vprods, y_ready = (loop(n, TILES) for n in ("shifted", "exped", "diff", "vprods", "y_ready"))
        y_turned, yt_out = loop("y_turned", TILES), loop("yt_out", TILES)
        A.pe_y, A.y_read = loop("projected", TILES), loop("projected_read", TILES)
        own_dve = sem(prefix + "dve_own")
        block = ctx.enter_context(nc.Block())

        @block.sync
        def _(sp):
            sp.dma_start(w[:, :, :], IN[prefix + "qkv"]).then_inc(w_loaded.sem, 16)
            sp.dma_start(wo[:, :, :], IN[prefix + "wo"]).then_inc(w_loaded.sem, 16)
            sp.dma_start(lam[:, :, :], IN[prefix + "lambda"]).then_inc(small.sem, 16)

        @block.tensor
        def _(pe):
            for b in range(3):
                pe_transpose(pe, S, A, 0, b, S.x, A.x_ready, A.pe_xt, A.xt_out)
            pe.wait_ge(w_loaded.sem, w_loaded.at(0, 32))
            for s in range(TILES + 3):
                if s < TILES:
                    pe.wait_ge(A.xt_out.sem, A.xt_out.at(0, s + 1))
                    if s >= 2:
                        pe.wait_ge(qkv_out.sem, qkv_out.at(0, s - 1))
                    for bank, c0, c1 in ((0, 0, 2 * DIM), (1, 2 * DIM, 3 * DIM)):
                        for kc in range(2):
                            ins = pe.matmul(S.ps[0:TILE, 2 * (s % 2) + bank, 0:c1 - c0],
                                            S.xt[:, kc, s * TILE:(s + 1) * TILE], w[:, kc, c0:c1],
                                            start=kc == 0, stop=kc == 1)
                    ins.then_inc(pe_qkv_done.sem, 1)
                if s >= 3:
                    g = s - 3
                    pe.wait_ge(y_ready.sem, y_ready.at(0, g + 1))
                    if g:
                        pe.wait_ge(yt_out.sem, yt_out.at(0, g))
                    for c in range(2):
                        ins = pe.transpose(S.ps[0:HALF, 6, c * TILE:(c + 1) * TILE], y[:, g % 2, c * HALF:(c + 1) * HALF],
                                           S.ident[0:TILE, 0:TILE])
                    ins.then_inc(y_turned.sem, 1)
                    pe.wait_ge(yt_out.sem, yt_out.at(0, g + 1))
                    if g:
                        pe.wait_ge(A.y_read.sem, A.y_read.at(0, g))
                    for c in range(2):
                        ins = pe.matmul(S.ps[0:TILE, 7, 0:DIM], yt[:, g % 2, c, :], wo[:, c, :], start=c == 0, stop=c == 1)
                    ins.then_inc(A.pe_y.sem, 1)

        @block.scalar
        def _(act):
            act.wait_ge(dots_ready.sem, dots_ready.at(0, 1))
            act.activation(dots[:, 0:2], dots[:, 0:2], ACT.Exp).then_inc(dots_exped.sem, 1)
            for b in range(3):
                act_transposed(act, S, A, 0, b, A.pe_xt, A.xt_out)
            for s in range(-1, TILES + 3):
                if 0 <= s < TILES:
                    act.wait_ge(shifted.sem, shifted.at(0, s + 1))
                    act.activation(att[:, s % 2, :, :], att[:, s % 2, :, :], ACT.Exp, scale=HD ** -0.5).then_inc(exped.sem, 1)
                if s >= 3:
                    g = s - 3
                    act.wait_ge(y_turned.sem, y_turned.at(0, g + 1))
                    act.activation(yt[:, g % 2, :, :], S.ps[0:HALF, 6, 0:2 * TILE].rearrange("p (c t) -> p c t", c=2),
                                   ACT.Copy).then_inc(yt_out.sem, 1)
                g = s + 1
                if g < TILES:
                    act.wait_ge(pe_qkv_done.sem, pe_qkv_done.at(0, g + 1))
                    if g >= 3:
                        act.wait_ge(vprods.sem, vprods.at(0, g - 2))
                    act.activation(qkv[:, g % 3, 0:2 * DIM], S.ps[0:TILE, 2 * (g % 2), 0:2 * DIM], ACT.Copy)
                    act.activation(qkv[:, g % 3, 2 * DIM:], S.ps[0:TILE, 2 * (g % 2) + 1, 0:DIM],
                                   ACT.Copy).then_inc(qkv_out.sem, 1)

        @block.gpsimd
        def _(pool):
            for g in range(TILES):
                pool.wait_ge(diff.sem, diff.at(0, g + 1))
                if g >= 2:
                    pool.wait_ge(y_ready.sem, y_ready.at(0, g - 1))
                weights = both[:, g % 2, :].rearrange("p (q k) -> p q k", k=NH).unsqueeze(2).to_broadcast([TILE, NH, 2 * HD, NH])
                values = qkv[:, g % 3, 2 * DIM:].rearrange("p (k d) -> p d k", d=2 * HD).unsqueeze(1).to_broadcast(
                    [TILE, NH, 2 * HD, NH])
                pool.tensor_tensor(vprod[:, g % 2, :, :].rearrange("p (q d) k -> p q d k", d=2 * HD), weights, values,
                                   ALU.mult).then_inc(vprods.sem, 1)

        @block.vector
        def _(dve):
            own = Own(own_dve)
            dve.wait_ge(small.sem, small.at(0, 16))
            dve.tensor_tensor(lam[:, 0:2, :], lam[:, 0:2, :], lam[:, 2:4, :], ALU.mult).then_inc(own.sem, own.up())
            dve.wait_ge(own.sem, own.n)
            dve.tensor_reduce(dots[:, 0:2], lam[:, 0:2, :], AX.X, ALU.add).then_inc(dots_ready.sem, 1)
            for b in range(3):
                normalise(dve, own, S, BLOCKS[b], S.h, S.x, 1e-5, done=A.x_ready.sem)
            dve.wait_ge(dots_exped.sem, dots_exped.at(0, 1))
            dve.memset(coef[:, 0:1], 1.0 - init).then_inc(own.sem, own.up())
            dve.tensor_tensor(dots[:, 2:3], dots[:, 0:1], dots[:, 1:2], ALU.subtract).then_inc(own.sem, own.up())
            dve.wait_ge(own.sem, own.n)
            dve.tensor_scalar(coef[:, 1:2], dots[:, 2:3], init, -(1.0 - init), ALU.add, ALU.mult).then_inc(own.sem, own.up())
            for s in range(TILES + 3):
                if s < TILES:
                    dve.wait_ge(qkv_out.sem, qkv_out.at(0, s + 1))
                    shape = [TILE, NH, NH, HD]
                    for half in range(2):
                        q, k = (qkv[:, s % 3, c * DIM:(c + 1) * DIM].rearrange(
                            "p (h t d) -> p t h d", t=2, d=HD)[:, half, :, :] for c in range(2))
                        dve.tensor_tensor(
                            prod[:, half, :, :].rearrange("p (q k) d -> p q k d", k=NH),
                            q.unsqueeze(2).to_broadcast(shape), k.unsqueeze(1).to_broadcast(shape),
                            ALU.mult).then_inc(own.sem, own.up())
                    dve.wait_ge(own.sem, own.n)
                    a, c = att[:, s % 2, :, :], col[:, s % 2, :]
                    dve.tensor_reduce(a.rearrange("p a b -> p (a b)"), prod[:, :, :, :].rearrange(
                        "p a b d -> p (a b) d"), AX.X, ALU.add).then_inc(own.sem, own.up())
                    dve.wait_ge(own.sem, own.n)
                    dve.tensor_reduce(c, a, AX.X, ALU.max).then_inc(own.sem, own.up())
                    dve.wait_ge(own.sem, own.n)
                    dve.tensor_tensor(a, a, c.unsqueeze(2).to_broadcast([TILE, 2 * NH, NH]), ALU.subtract).then_inc(shifted.sem, 1)
                if 1 <= s <= TILES:
                    g = s - 1
                    a, c = att[:, g % 2, :, :], col[:, g % 2, :]
                    dve.wait_ge(exped.sem, exped.at(0, g + 1))
                    dve.tensor_reduce(c, a, AX.X, ALU.add).then_inc(own.sem, own.up())
                    dve.wait_ge(own.sem, own.n)
                    dve.reciprocal(c, c).then_inc(own.sem, own.up())
                    dve.wait_ge(own.sem, own.n)
                    dve.tensor_tensor(c.rearrange("p (t h) -> p t h", t=2), c.rearrange("p (t h) -> p t h", t=2),
                                      coef[:, :].unsqueeze(2).to_broadcast([TILE, 2, NH]), ALU.mult).then_inc(own.sem, own.up())
                    dve.wait_ge(own.sem, own.n)
                    dve.tensor_tensor(a, a, c.unsqueeze(2).to_broadcast([TILE, 2 * NH, NH]), ALU.mult).then_inc(own.sem, own.up())
                    dve.wait_ge(own.sem, own.n)
                    dve.tensor_tensor(both[:, g % 2, :].rearrange("p (q k) -> p q k", k=NH), a[:, 0:NH, :], a[:, NH:, :],
                                      ALU.add).then_inc(diff.sem, 1)
                if 2 <= s < TILES + 2:
                    g = s - 2
                    dve.wait_ge(vprods.sem, vprods.at(0, g + 1))
                    if g >= 2:
                        dve.wait_ge(y_turned.sem, y_turned.at(0, g - 1))
                    dve.tensor_reduce(y[:, g % 2, :], vprod[:, g % 2, :, :], AX.X, ALU.add).then_inc(y_ready.sem, 1)
                if s >= 3:
                    dve_add_output(dve, S, A, 0, S.h, [s - 3], bank=7)


class Mixture:

    def __init__(self, nc, ctx, sem, prefix, E, outputs, bias_width=None):
        def sb(name, shape):
            return ctx.enter_context(nc.sbuf_tensor(prefix + name, shape, F32))

        def loop(name, per, lead=0):
            return Loop(sem(prefix + name), per, lead)

        self.E, self.outputs = E, outputs
        self.R = router_buffers(nc, ctx, sem, prefix + "r_", E)
        self.router = sb("router", [HALF, 2, E])
        self.router_bias = sb("router_bias", [TILE, bias_width or E])
        self.cw = sb("weights", [TILE, TILES, outputs])
        self.cwt = sb("weights_T", [outputs, TOKENS])
        self.out_bias = sb("out_bias", [outputs, DIM])
        self.x_ready, self.pe_xt, self.xt_out = loop("x_ready", TILES), loop("x_turned", TILES), loop("xt_out", TILES)
        self.cw_ready, self.cw_turned, self.cwt_out = loop("cw_ready", 1), loop("cw_turned", 3), loop("cwt_out", 3)
        self.small = loop("small_loaded", 64)
        self.pe_y, self.y_read = loop("bias_done", TILES), loop("bias_read", TILES)
        self.own_sem = sem(prefix + "dve_own")

    def sp_small(self, sp, IN, prefix, before):
        sp.dma_start(self.router[:, :, :], IN[prefix + "router"]).then_inc(self.small.sem, 16)
        sp.dma_start(self.router_bias[:, :], IN[prefix + "router_bias"]).then_inc(self.small.sem, 16)
        sp.dma_start(self.R.before[:, :, :], IN[before]).then_inc(self.small.sem, 16)
        sp.dma_start(self.out_bias[:, :], IN[prefix + "out_bias"]).then_inc(self.small.sem, 16)

    def pe_start(self, pe, S):
        for b in range(3):
            pe_transpose(pe, S, self, 0, b, S.x, self.x_ready, self.pe_xt, self.xt_out)
        pe.wait_ge(self.xt_out.sem, self.xt_out.at(0, TILES))
        pe.wait_ge(self.small.sem, self.small.at(0, 64))
        pe_router(pe, S, self.R, self.E, self.router)

    def pe_bias(self, pe, S):
        pe.wait_ge(self.cw_ready.sem, self.cw_ready.at(0, 1))
        for b, tiles in enumerate(BLOCKS):
            if b:
                pe.wait_ge(self.cwt_out.sem, self.cwt_out.at(0, b))
            for lg, g in enumerate(tiles):
                ins = pe.transpose(S.ps[0:self.outputs, 5, lg * TILE:(lg + 1) * TILE], self.cw[:, g, :],
                                   S.ident[0:TILE, 0:TILE])
            ins.then_inc(self.cw_turned.sem, 1)
        pe.wait_ge(self.cwt_out.sem, self.cwt_out.at(0, 3))
        for g in range(TILES):
            if g >= 2:
                pe.wait_ge(self.y_read.sem, self.y_read.at(0, g - 1))
            pe.matmul(S.ps[0:TILE, 6 + g % 2, 0:DIM], self.cwt[:, g * TILE:(g + 1) * TILE], self.out_bias[:, :],
                      start=True, stop=True).then_inc(self.pe_y.sem, 1)

    def act_start(self, act, S):
        for b in range(3):
            act_transposed(act, S, self, 0, b, self.pe_xt, self.xt_out)

    def act_bias(self, act, S):
        for b, tiles in enumerate(BLOCKS):
            act.wait_ge(self.cw_turned.sem, self.cw_turned.at(0, b + 1))
            act.activation(self.cwt[:, tiles[0] * TILE:(tiles[-1] + 1) * TILE],
                           S.ps[0:self.outputs, 5, 0:len(tiles) * TILE], ACT.Copy).then_inc(self.cwt_out.sem, 1)


def stage_two_layer_experts(nc, S, IN, prefix="f_"):
    E, K = 8, 2
    with ExitStack() as ctx:
        sem = ctx.enter_context(stage_semaphores(nc))
        X = Mixture(nc, ctx, sem, prefix, E, E)
        M = experts(nc, ctx, sem, prefix, True)
        F = M[0]
        block = ctx.enter_context(nc.Block())

        @block.sync
        def _(sp):
            X.sp_small(sp, IN, prefix, "before8")
            for e in range(2):
                sp_expert(sp, M[e], IN[prefix + "w1"][e], IN[prefix + "w2"][e], IN[prefix + "b1"][e])
            with sp.Fori(0, E // 2 - 1) as q:
                for k in range(2):
                    sp.wait_ge(F.y_read.sem, F.y_read.at(2 * q + k, TILES))
                    e = 2 * q + 2 + k
                    sp_expert(sp, M[k], IN[prefix + "w1"][e], IN[prefix + "w2"][e], IN[prefix + "b1"][e])

        @block.tensor
        def _(pe):
            X.pe_start(pe, S)
            with pe.Fori(0, E // 2) as q:
                for k in range(2):
                    for b in range(3):
                        pe_ff(pe, S, M[k], 2 * q + k, b, (F.y_read, 2 * q + k, 0), load_turn=q)
            pe.wait_ge(F.y_read.sem, F.y_read.at(E - 1, TILES))
            X.pe_bias(pe, S)

        @block.scalar
        def _(act):
            X.act_start(act, S)
            act_route(act, S, X.R, 0)
            with act.Fori(0, E // 2) as q:
                for k in range(2):
                    act.wait_ge(M[k].w_1.sem, M[k].w_1.at(q, 32))
                    for b in range(3):
                        act_ff(act, S, M[k], 2 * q + k, b, ACT.Gelu)
            X.act_bias(act, S)

        @block.vector
        def _(dve):
            own = Own(X.own_sem)
            dve.nop().then_inc(F.y_read.sem, TILES)
            for b in range(3):
                normalise(dve, own, S, BLOCKS[b], S.h, S.x, 1e-5, done=X.x_ready.sem)
            dve.wait_ge(X.small.sem, X.small.at(0, 64))
            X.R.cw = X.cw[:, :, 0:E]
            dve_route(dve, own, S, X.R, 0, E, K, bias=X.router_bias[:, :])
            dve.nop().then_inc(X.cw_ready.sem, 1)
            with dve.Fori(0, E // 2) as q:
                for k in range(2):
                    dve_add_scaled(dve, S, F, 2 * q + k, S.h, lambda g: X.cw[:, g, bass.ds(2 * q + k, 1)], range(TILES))
            dve.wait_ge(F.y_read.sem, F.y_read.at(E - 1, TILES))
            dve_add_output(dve, S, X, 0, S.h, range(TILES))


def stage_linear_experts(nc, S, IN, prefix="e_"):
    E, K = 8, 2
    with ExitStack() as ctx:
        sem = ctx.enter_context(stage_semaphores(nc))
        X = Mixture(nc, ctx, sem, prefix, E, E)
        w = ctx.enter_context(nc.sbuf_tensor(prefix + "w", [HALF, 2, E, DIM], F32))
        loaded = sem(prefix + "experts_loaded")
        Y = Names()
        Y.pe_y = Loop(sem(prefix + "expert_done"), TILES)
        Y.y_read = Loop(sem(prefix + "expert_read"), TILES, TILES)
        block = ctx.enter_context(nc.Block())

        @block.sync
        def _(sp):
            X.sp_small(sp, IN, prefix, "before8")
            sp.dma_start(w[:, :, :, :], IN[prefix + "w"]).then_inc(loaded, 16)

        @block.tensor
        def _(pe):
            X.pe_start(pe, S)
            X.pe_bias(pe, S)
            pe.wait_ge(X.y_read.sem, X.y_read.at(0, TILES))
            pe.wait_ge(loaded, 16)
            with pe.Fori(0, E) as e:
                for g in range(TILES):
                    if g != 1:
                        pe.wait_ge(Y.y_read.sem, Y.y_read.at(e, max(g - 1, 0)))
                    for kc in range(2):
                        ins = pe.matmul(S.ps[0:TILE, 6 + g % 2, 0:DIM], S.xt[:, kc, g * TILE:(g + 1) * TILE],
                                        w[:, kc, e, :], start=kc == 0, stop=kc == 1)
                    ins.then_inc(Y.pe_y.sem, 1)

        @block.scalar
        def _(act):
            X.act_start(act, S)
            act_route(act, S, X.R, 0)
            X.act_bias(act, S)

        @block.vector
        def _(dve):
            own = Own(X.own_sem)
            dve.nop().then_inc(Y.y_read.sem, TILES)
            for b in range(3):
                normalise(dve, own, S, BLOCKS[b], S.h, S.x, 1e-5, done=X.x_ready.sem)
            dve.wait_ge(X.small.sem, X.small.at(0, 64))
            X.R.cw = X.cw[:, :, 0:E]
            dve_route(dve, own, S, X.R, 0, E, K, bias=X.router_bias[:, :], eps=1e-9)
            dve.nop().then_inc(X.cw_ready.sem, 1)
            dve_add_output(dve, S, X, 0, S.h, range(TILES))
            with dve.Fori(0, E) as e:
                dve_add_scaled(dve, S, Y, e, S.h, lambda g: X.cw[:, g, bass.ds(e, 1)], range(TILES))
            dve.wait_ge(Y.y_read.sem, Y.y_read.at(E - 1, TILES))


def allocate(nc, ctx):
    S = Names()

    def sb(name, shape, dt=F32):
        return ctx.enter_context(nc.sbuf_tensor(name, shape, dt))

    S.h = sb("residual", [TILE, TILES, DIM])
    S.x = sb("inner", [TILE, TILES, DIM])
    S.xt = sb("inner_T", [HALF, 2, TOKENS])
    S.ident = sb("identity", [128, 128])
    S.mask = sb("images_apart", [TILE, 6 * TILE])
    S.hmask = sb("head_mask", [128, 12])
    S.stats = sb("stats", [TILE, TILES, 6])
    S.meanvar = sb("meanvar", [TILE, TILES, 2])
    S.rstd = sb("rstd", [TILE, TILES])
    S.small = sb("small", [TILE, 2, TILES])
    S.smalli = sb("smalli", [TILE, TILES], I32)
    S.qt = sb("queries_T", [128, FCH, BLOCK_TILES * TILE])
    S.v = sb("values", [TILE, BLOCK_TILES, FF])
    S.ot = sb("heads_T", [128, FCH, BLOCK_TILES * TILE])
    S.h1 = sb("hidden_T", [128, FCH, BLOCK_TILES * TILE])
    S.p = sb("probs", [TILE, 4, 6 * TILE])
    S.pt = sb("probs_T", [TILE, 2, 6 * TILE])
    S.nmax = sb("nmax", [TILE, 4, 6])
    S.sums = sb("sums", [TILE, 4, 6])
    S.recs = sb("recs", [TILE, 4, 6])
    S.ps = ctx.enter_context(nc.psum_tensor("ps", [128, 8, BANK], F32))
    return S


def stage_start(nc, S, IN):
    with ExitStack() as ctx:
        sem = ctx.enter_context(stage_semaphores(nc))
        loaded = sem("constants_loaded")
        block = ctx.enter_context(nc.Block())

        @block.sync
        def _(sp):
            for dst, name in ((S.ident, "ident"), (S.mask, "image_mask"), (S.hmask, "hmask16")):
                sp.dma_start(dst[:, :], IN[name]).then_inc(loaded, 16)
            sp.wait_ge(loaded, 48)


def stage_patches_and_convolution(nc, S, IN, scratch_in, scratch_out):
    GT = CONV_BLOCKS * PADDED
    with ExitStack() as ctx:
        sem = ctx.enter_context(stage_semaphores(nc))
        A = Names()

        def sb(name, shape):
            return ctx.enter_context(nc.sbuf_tensor("t_" + name, shape, F32))

        def loop(name, per):
            return Loop(sem("t_" + name), per)

        patches = (S.qt, S.ot, S.h1)
        w, bias, ln0 = sb("w", [128, FCH, DIM]), sb("bias", [TILE, DIM]), sb("ln0", [TILE, 2 * DIM])
        taps = sb("taps", [TILE, CONV_GROUPS, CONV_D, TILE])
        cbias = sb("conv_bias", [TILE, CONV_GROUPS])
        xin, xout = sb("conv_in", [TILE, CONV_GROUPS, GT]), sb("conv_out", [TILE, CONV_GROUPS, GT])
        back = sb("conv_T", [HALF, 2, TOKENS])
        patches_loaded = [loop(f"patches_loaded_{b}", 16) for b in range(3)]
        w_loaded, taps_loaded, small = loop("w_loaded", 32), loop("taps_loaded", 16), loop("small_loaded", 32)
        spilled, gathered = loop("spilled", 16), [loop(f"gathered_{k}", 16) for k in range(4)]
        scattered, returned = loop("scattered", 64), loop("returned", 16)
        back_in_order = loop("back_in_order", 2)
        A.pe_y, A.y_read = loop("embedded", TILES), loop("embedded_read", TILES)
        x_ready, x_turned, xt_out = loop("x_ready", TILES), loop("x_turned", TILES), loop("xt_out", TILES)
        conv_done, conv_out = loop("conv_done", CONV_GROUPS), loop("conv_out", CONV_GROUPS)
        pos_turned, pos_read = loop("pos_turned", TILES), loop("pos_read", TILES)
        own_dve = sem("t_dve_own")
        block = ctx.enter_context(nc.Block())

        def groups(t, q):
            rows = t.rearrange("(g c) (j n) -> g (c j) n", c=CONV_CH, j=CONV_J)
            return rows[4 * q:4 * q + 4].rearrange("g r n -> r g n")

        out_of_dram = back[:, :, :].rearrange("p c (j a b) -> p c b a j", b=PADDED, j=CONV_J)
        in_order = S.xt[:, :, :].rearrange("p c (b a j) -> p c b a j", b=PADDED, j=CONV_J)

        @block.sync
        def _(sp):
            sp.dma_start(w[:, :, :], IN["t_w"]).then_inc(w_loaded.sem, 16)
            sp.dma_start(bias[:, :], IN["t_bias"]).then_inc(w_loaded.sem, 16)
            for b, tiles in enumerate(BLOCKS):
                sp.dma_start(patches[b][:, :, 0:len(tiles) * TILE],
                             IN["t_patches"][:, :, tiles[0] * TILE:(tiles[-1] + 1) * TILE]).then_inc(patches_loaded[b].sem, 16)
            sp.dma_start(cbias[:, :], IN["t_conv_bias"]).then_inc(small.sem, 16)
            sp.dma_start(ln0[:, :], IN["t_ln0"]).then_inc(small.sem, 16)
            sp.dma_start(taps[:, :, :, :], IN["t_taps"]).then_inc(taps_loaded.sem, 16)
            sp.wait_ge(xt_out.sem, xt_out.at(0, TILES))
            sp.dma_start(scratch_in.rearrange("(c p) t -> p c t", p=HALF), S.xt[:, :, :]).then_inc(spilled.sem, 16)
            sp.wait_ge(spilled.sem, spilled.at(0, 16))
            for q in range(4):
                sp.dma_start(xin[:, 4 * q:4 * q + 4, :], groups(scratch_in, q)).then_inc(gathered[q].sem, 16)
            for q in range(4):
                sp.wait_ge(conv_out.sem, conv_out.at(0, 4 * q + 4))
                sp.dma_start(groups(scratch_out, q), xout[:, 4 * q:4 * q + 4, :]).then_inc(scattered.sem, 16)
            sp.wait_ge(scattered.sem, scattered.at(0, 64))
            sp.dma_start(back[:, :, :], scratch_out.rearrange("(c p) t -> p c t", p=HALF)).then_inc(returned.sem, 16)

        @block.tensor
        def _(pe):
            pe.wait_ge(w_loaded.sem, w_loaded.at(0, 32))
            for b, tiles in enumerate(BLOCKS):
                pe.wait_ge(patches_loaded[b].sem, patches_loaded[b].at(0, 16))
                for lg, g in enumerate(tiles):
                    if g >= 2:
                        pe.wait_ge(A.y_read.sem, A.y_read.at(0, g - 1))
                    for c in range(FCH):
                        ins = pe.matmul(S.ps[0:TILE, 6 + g % 2, 0:DIM], patches[b][:, c, lg * TILE:(lg + 1) * TILE],
                                        w[:, c, :], start=c == 0, stop=c == FCH - 1)
                    ins.then_inc(A.pe_y.sem, 1)
            for b in range(3):
                pe_transpose(pe, S, A, 0, b, S.x, x_ready, x_turned, xt_out)
            pe.wait_ge(taps_loaded.sem, taps_loaded.at(0, 16))
            distances = sorted(range(1 - CONV_BLOCKS, CONV_BLOCKS), key=abs)
            for g in range(CONV_GROUPS):
                pe.wait_ge(gathered[g // 4].sem, gathered[g // 4].at(0, 16))
                if g >= 4:
                    pe.wait_ge(conv_out.sem, conv_out.at(0, g - 3))
                for n, d in enumerate(distances):
                    out0, in0, k = max(d, 0), max(-d, 0), CONV_BLOCKS - abs(d)
                    ins = pe.matmul(S.ps[0:TILE, g % 4, out0 * PADDED:(out0 + k) * PADDED],
                                    taps[:, g, d + CONV_BLOCKS - 1, :],
                                    xin[:, g, in0 * PADDED:(in0 + k) * PADDED],
                                    start=n == 0, stop=n == CONV_D - 1, skip_group_check=True)
                ins.then_inc(conv_done.sem, 1)
            pe.wait_ge(back_in_order.sem, back_in_order.at(0, 2))
            for g in range(TILES):
                if g >= 2:
                    pe.wait_ge(pos_read.sem, pos_read.at(0, g - 1))
                for c in range(2):
                    tile = S.xt[:, c, g * TILE:(g + 1) * TILE]
                    ins = pe.transpose(S.ps[0:TILE, 6 + g % 2, c * HALF:(c + 1) * HALF], tile, S.ident[0:HALF, 0:HALF])
                ins.then_inc(pos_turned.sem, 1)

        @block.scalar
        def _(act):
            by_image = S.xt[:, :, :].rearrange("p c (j a b) -> p c b a j", b=PADDED, j=CONV_J)
            for g in range(TILES):
                act.wait_ge(x_turned.sem, x_turned.at(0, g + 1))
                for c in range(2):
                    ins = act.activation(by_image[:, c, g * GROUP:(g + 1) * GROUP],
                                         S.ps[0:HALF, 4 + g % 2, c * TILE:(c + 1) * TILE].rearrange(
                                             "p (b a j) -> p b a j", b=GROUP, j=CONV_J), ACT.Copy)
                ins.then_inc(xt_out.sem, 1)
            act.wait_ge(small.sem, small.at(0, 32))
            for g in range(CONV_GROUPS):
                act.wait_ge(conv_done.sem, conv_done.at(0, g + 1))
                act.activation(xout[:, g, :], S.ps[0:TILE, g % 4, 0:GT], ACT.Gelu, bias=cbias[:, g:g + 1]).then_inc(conv_out.sem, 1)
            act.wait_ge(returned.sem, returned.at(0, 16))
            act.activation(in_order[:, 1], out_of_dram[:, 1], ACT.Copy).then_inc(back_in_order.sem, 1)

        @block.vector
        def _(dve):
            own = Own(own_dve)
            dve.wait_ge(w_loaded.sem, w_loaded.at(0, 32))
            for b in range(3):
                for g in BLOCKS[b]:
                    dve.wait_ge(A.pe_y.sem, A.pe_y.at(0, g + 1))
                    dve.tensor_tensor(S.h[:, g, :], S.ps[0:TILE, 6 + g % 2, 0:DIM], bias[:, :], ALU.add).then_inc(A.y_read.sem, 1)
                dve.wait_ge(A.y_read.sem, A.y_read.at(0, BLOCKS[b][-1] + 1))
                normalise(dve, own, S, BLOCKS[b], S.h, S.x, 1e-5, done=x_ready.sem)
            dve.wait_ge(x_ready.sem, x_ready.at(0, TILES))
            dve.wait_ge(returned.sem, returned.at(0, 16))
            dve.tensor_copy(in_order[:, 0], out_of_dram[:, 0]).then_inc(back_in_order.sem, 1)
            dve.wait_ge(small.sem, small.at(0, 32))
            for b in range(3):
                for g in BLOCKS[b]:
                    dve.wait_ge(pos_turned.sem, pos_turned.at(0, g + 1))
                    dve.tensor_tensor(S.x[:, g, :], S.ps[0:TILE, 6 + g % 2, 0:DIM], S.x[:, g, :], ALU.add).then_inc(pos_read.sem, 1)
                dve.wait_ge(pos_read.sem, pos_read.at(0, BLOCKS[b][-1] + 1))
                normalise(dve, own, S, BLOCKS[b], S.x, S.x, 1e-5, ln0[:, 0:DIM], ln0[:, DIM:])
                dve.wait_ge(own.sem, own.n)


def stage_decay_attention(nc, S, IN, prefix="h_"):
    with ExitStack() as ctx:
        sem = ctx.enter_context(stage_semaphores(nc))
        A = Names()

        def sb(name, shape):
            return ctx.enter_context(nc.sbuf_tensor(prefix + name, shape, F32))

        def loop(name, per):
            return Loop(sem(prefix + name), per)

        w, qkb, vb, decay = sb("qkv", [HALF, 2, 3 * DIM]), sb("qk_bias", [HALF, 4]), sb("v_bias", [TILE, DIM]), sb("decay", [TILE, TILE])
        st = sb("scores_T", [TILE, 2, TILE])
        loaded = loop("loaded", 64)
        A.x_ready, A.pe_xt, A.xt_out = loop("x_ready", TILES), loop("x_turned", TILES), loop("xt_out", TILES)
        qk_done, qk_out, v_done, v_out = loop("qk_done", 12), loop("qk_out", 12), loop("v_done", TILES), loop("v_out", TILES)
        s_done, s_out = loop("scores_done", TILES), loop("scores_out", TILES)
        A.pe_y, A.y_read = loop("out_done", TILES), loop("out_read", TILES)
        own_dve = sem(prefix + "dve_own")
        block = ctx.enter_context(nc.Block())

        @block.sync
        def _(sp):
            for dst, name in ((w[:, :, :], "qkv"), (qkb[:, :], "qk_bias"), (vb[:, :], "v_bias"), (decay[:, :], "decay")):
                sp.dma_start(dst, IN[prefix + name]).then_inc(loaded.sem, 16)

        @block.tensor
        def _(pe):
            for b in range(3):
                pe_transpose(pe, S, A, 0, b, S.x, A.x_ready, A.pe_xt, A.xt_out)
            pe.wait_ge(A.xt_out.sem, A.xt_out.at(0, TILES))
            pe.wait_ge(loaded.sem, loaded.at(0, 64))
            for b, tiles in enumerate(BLOCKS):
                c0, cols = tiles[0] * TILE, len(tiles) * TILE
                if b:
                    pe.wait_ge(s_out.sem, s_out.at(0, tiles[0]))
                for m in range(4):
                    for kc in range(2):
                        ins = pe.matmul(S.ps[0:HALF, m, 0:cols], w[:, kc, m * HALF:(m + 1) * HALF],
                                        S.xt[:, kc, c0:c0 + cols], start=kc == 0, stop=kc == 1)
                    ins.then_inc(qk_done.sem, 1)
                for g in tiles:
                    if g >= 2:
                        pe.wait_ge(v_out.sem, v_out.at(0, g - 1))
                    for kc in range(2):
                        ins = pe.matmul(S.ps[0:TILE, 4 + g % 2, 0:DIM], S.xt[:, kc, g * TILE:(g + 1) * TILE],
                                        w[:, kc, 2 * DIM:], start=kc == 0, stop=kc == 1)
                    ins.then_inc(v_done.sem, 1)
                pe.wait_ge(qk_out.sem, qk_out.at(0, 4 * (b + 1)))
                for s in range(len(tiles) + 1):
                    if s < len(tiles):
                        g = tiles[s]
                        if s >= 2:
                            pe.wait_ge(s_out.sem, s_out.at(0, g - 1))
                        for c in range(2):
                            ins = pe.matmul(S.ps[0:TILE, g % 2, 0:TILE], S.qt[0:HALF, 2 + c, s * TILE:(s + 1) * TILE],
                                            S.qt[0:HALF, c, s * TILE:(s + 1) * TILE], start=c == 0, stop=c == 1)
                        ins.then_inc(s_done.sem, 1)
                    if s:
                        g = tiles[s - 1]
                        pe.wait_ge(s_out.sem, s_out.at(0, g + 1))
                        pe.wait_ge(v_out.sem, v_out.at(0, g + 1))
                        if g >= 2:
                            pe.wait_ge(A.y_read.sem, A.y_read.at(0, g - 1))
                        pe.matmul(S.ps[0:TILE, 6 + g % 2, 0:DIM], st[:, g % 2, :], S.v[:, s - 1, 0:DIM],
                                  start=True, stop=True).then_inc(A.pe_y.sem, 1)

        @block.scalar
        def _(act):
            for b in range(3):
                act_transposed(act, S, A, 0, b, A.pe_xt, A.xt_out)
            act.wait_ge(loaded.sem, loaded.at(0, 64))
            for b, tiles in enumerate(BLOCKS):
                for m in range(4):
                    act.wait_ge(qk_done.sem, qk_done.at(0, 4 * b + m + 1))
                    act.activation(S.qt[0:HALF, m, 0:len(tiles) * TILE], S.ps[0:HALF, m, 0:len(tiles) * TILE],
                                   ACT.Identity, bias=qkb[:, m:m + 1]).then_inc(qk_out.sem, 1)

        @block.vector
        def _(dve):
            own = Own(own_dve)
            for b in range(3):
                normalise(dve, own, S, BLOCKS[b], S.h, S.x, 1e-5, done=A.x_ready.sem)
            dve.wait_ge(loaded.sem, loaded.at(0, 64))
            for b, tiles in enumerate(BLOCKS):
                for lg, g in enumerate(tiles):
                    dve.wait_ge(v_done.sem, v_done.at(0, g + 1))
                    dve.tensor_tensor(S.v[:, lg, 0:DIM], S.ps[0:TILE, 4 + g % 2, 0:DIM], vb[:, :], ALU.add).then_inc(v_out.sem, 1)
                for s in range(len(tiles) + 1):
                    if s < len(tiles):
                        g = tiles[s]
                        dve.wait_ge(s_done.sem, s_done.at(0, g + 1))
                        dve.scalar_tensor_tensor(st[:, g % 2, :], S.ps[0:TILE, g % 2, 0:TILE], DIM ** -0.5, decay[:, :],
                                                 ALU.mult, ALU.mult).then_inc(s_out.sem, 1)
                    if s:
                        dve_add_output(dve, S, A, 0, S.h, [tiles[s - 1]])


def stage_gated_experts(nc, S, IN, prefix="i_"):
    E, G, GROUPS, K, ALL = 16, 4, 2, 4, 18
    PER = 6
    TURNS, STEPS = ALL // PER, PER * 3
    with ExitStack() as ctx:
        sem = ctx.enter_context(stage_semaphores(nc))
        X = Mixture(nc, ctx, sem, prefix, E, ALL, bias_width=2 * E)
        R = X.R

        def sb(name, shape):
            return ctx.enter_context(nc.sbuf_tensor(prefix + name, shape, F32))

        def loop(name, per, lead=0):
            return Loop(sem(prefix + name), per, lead)

        w = [sb(f"w_{k}", [HALF, 3 * DIM + 2]) for k in range(2)]
        pair, top = sb("pair_sums", [TILE, TILES * G, 6]), sb("group_scores", [TILE, TILES, G])
        gmask = sb("group_mask", [TILE, TILES, G])
        chosen = sb("chosen", [TILE, TILES, E])
        silu, hidden = sb("silu", [HALF, 2, BLOCK_TILES * TILE]), sb("hidden", [HALF, 2, BLOCK_TILES * TILE])
        w_loaded = [loop(f"w_loaded_{k}", 16 * PER // 2) for k in range(2)]
        gu_done, silu_out = loop("gate_up_done", STEPS), loop("silu_out", STEPS)
        hidden_out = loop("hidden_out", STEPS, STEPS)
        pe_y, y_read = loop("expert_done", PER * TILES), loop("expert_read", PER * TILES, PER * TILES)
        block = ctx.enter_context(nc.Block())

        def up_gate(k, kc, part):
            c0 = kc * DIM + part * HALF
            return w[k % 2][:, c0:c0 + HALF]

        @block.sync
        def _(sp):
            X.sp_small(sp, IN, prefix, "before16")
            for k in range(2):
                sp.dma_start(w[k][:, :], IN[prefix + "w"][k]).then_inc(w_loaded[k].sem, 16)
            for e in range(2, ALL):
                sp.wait_ge(pe_y.sem, pe_y.at((e - 2) // PER, ((e - 2) % PER + 1) * TILES))
                sp.dma_start(w[e % 2][:, :], IN[prefix + "w"][e]).then_inc(w_loaded[e % 2].sem, 16)

        @block.tensor
        def _(pe):
            X.pe_start(pe, S)
            X.pe_bias(pe, S)
            pe.wait_ge(X.y_read.sem, X.y_read.at(0, TILES))
            with pe.Fori(0, TURNS) as q:
                for s in range(STEPS + 1):
                    if s < STEPS:
                        k, tiles = s // 3, BLOCKS[s % 3]
                        c0, cols = tiles[0] * TILE, len(tiles) * TILE
                        if s % 3 == 0:
                            pe.wait_ge(w_loaded[k % 2].sem, w_loaded[k % 2].at(q, 16 * (k // 2 + 1)))
                        pe.wait_ge(hidden_out.sem, hidden_out.at(q, s - 1))
                        for part in range(2):
                            for kc in range(2):
                                ins = pe.matmul(S.ps[0:HALF, 2 * (s % 2) + part, 0:cols], up_gate(k, kc, part),
                                                S.xt[:, kc, c0:c0 + cols], start=kc == 0, stop=kc == 1)
                        ins.then_inc(gu_done.sem, 1)
                    if s:
                        r = s - 1
                        k, tiles = r // 3, BLOCKS[r % 3]
                        pe.wait_ge(hidden_out.sem, hidden_out.at(q, r + 1))
                        for lg, g in enumerate(tiles):
                            n = k * TILES + g
                            pe.wait_ge(y_read.sem, y_read.at(q, n - 3))
                            pe.matmul(S.ps[0:TILE, 4 + n % 4, 0:DIM], hidden[:, r % 2, lg * TILE:(lg + 1) * TILE],
                                      w[k % 2][:, 2 * DIM:3 * DIM], start=True, stop=True).then_inc(pe_y.sem, 1)

        @block.scalar
        def _(act):
            X.act_start(act, S)
            act.wait_ge(R.shifted.sem, R.shifted.at(0, 1))
            act.activation(R.ex, R.ex, ACT.Sigmoid).then_inc(R.exped.sem, 1)
            X.act_bias(act, S)
            with act.Fori(0, TURNS) as q:
                for s in range(STEPS):
                    k, cols = s // 3, len(BLOCKS[s % 3]) * TILE
                    act.wait_ge(gu_done.sem, gu_done.at(q, s + 1))
                    act.activation(silu[:, s % 2, 0:cols], S.ps[0:HALF, 2 * (s % 2), 0:cols], ACT.Silu,
                                   bias=w[k % 2][:, 3 * DIM:3 * DIM + 1]).then_inc(silu_out.sem, 1)

        @block.vector
        def _(dve):
            own = Own(X.own_sem)
            dve.nop().then_inc(y_read.sem, PER * TILES)
            dve.nop().then_inc(hidden_out.sem, STEPS)
            for b in range(3):
                normalise(dve, own, S, BLOCKS[b], S.h, S.x, 1e-5, done=X.x_ready.sem)
            dve.wait_ge(X.small.sem, X.small.at(0, 64))
            dve.wait_ge(R.logits_done.sem, R.logits_done.at(0, 1))
            bias = X.router_bias

            def over_tiles(c):
                return c.unsqueeze(1).to_broadcast([TILE, TILES, E])

            dve.tensor_tensor(R.ex, S.ps[0:TILE, 4, 0:TILES * E].rearrange("p (g e) -> p g e", e=E),
                              over_tiles(bias[:, 0:E]), ALU.add).then_inc(R.shifted.sem, 1)
            dve.memset(X.cw[:, :, E:ALL], 1.0).then_inc(own.sem, own.up())
            dve.wait_ge(R.exped.sem, R.exped.at(0, 1))
            dve.tensor_tensor(chosen[:, :, :], R.ex, over_tiles(bias[:, E:2 * E]), ALU.add).then_inc(own.sem, own.up())
            dve.wait_ge(own.sem, own.n)
            c = chosen[:, :, :].rearrange("p t (g e) -> p (t g) e", g=G)
            dve.tensor_tensor(pair[:, :, 0:3], c[:, :, 0:3], c[:, :, 1:4], ALU.add).then_inc(own.sem, own.up())
            dve.tensor_tensor(pair[:, :, 3:5], c[:, :, 0:2], c[:, :, 2:4], ALU.add).then_inc(own.sem, own.up())
            dve.tensor_tensor(pair[:, :, 5:6], c[:, :, 0:1], c[:, :, 3:4], ALU.add).then_inc(own.sem, own.up())
            dve.wait_ge(own.sem, own.n)
            dve.tensor_reduce(top[:, :, :].rearrange("p t g -> p (t g)"), pair[:, :, :], AX.X, ALU.max).then_inc(own.sem, own.up())
            dve.wait_ge(own.sem, own.n)
            dve_top_mask(dve, own, S, R, gmask[:, :, :], top[:, :, :], G, GROUPS)
            dve.tensor_tensor(c, c, gmask[:, :, :].rearrange("p t g -> p (t g)").unsqueeze(2).to_broadcast(
                [TILE, TILES * G, E // G]), ALU.mult).then_inc(own.sem, own.up())
            dve.wait_ge(own.sem, own.n)
            dve_top_mask(dve, own, S, R, R.mask, chosen[:, :, :], E, K)
            dve.tensor_tensor(R.ex, R.ex, R.mask, ALU.mult).then_inc(own.sem, own.up())
            dve.wait_ge(own.sem, own.n)
            dve.tensor_reduce(R.col, R.ex, AX.X, ALU.add).then_inc(own.sem, own.up())
            dve.wait_ge(own.sem, own.n)
            dve.tensor_scalar(R.col, R.col, 1e-20, None, ALU.add).then_inc(own.sem, own.up())
            dve.wait_ge(own.sem, own.n)
            dve.reciprocal(R.col, R.col).then_inc(own.sem, own.up())
            dve.wait_ge(own.sem, own.n)
            dve.tensor_tensor(R.ex, R.ex, R.col.unsqueeze(2).to_broadcast([TILE, TILES, E]), ALU.mult).then_inc(own.sem, own.up())
            dve.wait_ge(own.sem, own.n)
            dve.tensor_scalar(X.cw[:, :, 0:E], R.ex, 2.5, None, ALU.mult).then_inc(own.sem, own.up())
            dve.wait_ge(own.sem, own.n)
            dve.nop().then_inc(X.cw_ready.sem, 1)
            dve_add_output(dve, S, X, 0, S.h, range(TILES))
            with dve.Fori(0, TURNS) as q:
                for s in range(STEPS + 1):
                    if s < STEPS:
                        k, cols = s // 3, len(BLOCKS[s % 3]) * TILE
                        dve.wait_ge(silu_out.sem, silu_out.at(q, s + 1))
                        dve.scalar_tensor_tensor(hidden[:, s % 2, 0:cols], S.ps[0:HALF, 2 * (s % 2) + 1, 0:cols],
                                                 w[k % 2][:, 3 * DIM + 1:3 * DIM + 2], silu[:, s % 2, 0:cols],
                                                 ALU.add, ALU.mult).then_inc(hidden_out.sem, 1)
                    if s:
                        r = s - 1
                        k, tiles = r // 3, BLOCKS[r % 3]
                        for g in tiles:
                            n = k * TILES + g
                            dve.wait_ge(pe_y.sem, pe_y.at(q, n + 1))
                            dve.wait_ge(y_read.sem, y_read.at(q, n + 1 - TILES))
                            dve.scalar_tensor_tensor(S.h[:, g, :], S.ps[0:TILE, 4 + n % 4, 0:DIM],
                                                     X.cw[:, g, bass.ds(PER * q + k, 1)], S.h[:, g, :],
                                                     ALU.mult, ALU.add).then_inc(y_read.sem, 1)
            dve.wait_ge(y_read.sem, y_read.at(TURNS - 1, PER * TILES))


def stage_end(nc, S, out):
    with ExitStack() as ctx:
        sem = ctx.enter_context(stage_semaphores(nc))
        stored = sem("stored")
        block = ctx.enter_context(nc.Block())

        @block.sync
        def _(sp):
            whole = TILES - 1
            sp.dma_start(out[0:whole * GROUP].rearrange("(g b) l d -> (b l) g d", b=GROUP),
                         S.h[:, 0:whole, :]).then_inc(stored, 16)
            left = IMAGES - whole * GROUP
            sp.dma_start(out[whole * GROUP:IMAGES].rearrange("b l d -> (b l) d"), S.h[0:left * LEN, whole, :]).then_inc(stored, 16)
            sp.wait_ge(stored, 32)


def vit_tower(nc, IN, out):
    scratch_in = nc.dram_tensor("conv_scratch_in", [DIM, TOKENS], F32).ap()
    scratch_out = nc.dram_tensor("conv_scratch_out", [DIM, TOKENS], F32).ap()
    with ExitStack() as ctx:
        S = allocate(nc, ctx)
        stage_start(nc, S, IN)
        stage_patches_and_convolution(nc, S, IN, scratch_in, scratch_out)
        stage_small_attention(nc, S, IN)
        stage_large_attention(nc, S, IN)
        stage_sharp_attention(nc, S, IN)
        stage_linear_experts(nc, S, IN)
        stage_difference_attention(nc, S, IN)
        stage_two_layer_experts(nc, S, IN)
        stage_decay_attention(nc, S, IN)
        stage_gated_experts(nc, S, IN)
        stage_end(nc, S, out)


def tiled(a):
    a = np.concatenate([a, a[-1:]], 0)
    return np.ascontiguousarray(a.reshape(TILES, TILE, -1).transpose(1, 0, 2))


def rows_of(w, rows):
    *lead, k, n = w.shape
    return np.ascontiguousarray(np.moveaxis(w.reshape(*lead, k // rows, rows, n), -3, -2))


def spread(v):
    return np.broadcast_to(v[..., None, :], (*v.shape[:-1], TILE, v.shape[-1])).copy()


def lay_out(i):
    f = np.float32
    o = {}
    img = np.arange(TILE) // LEN
    off = np.where(img[:, None] == img[None, :], 0.0, OFF).astype(f)
    o["ident"] = np.eye(128, dtype=f)
    o["image_mask"] = np.tile(off, (1, 6))
    rows = np.arange(128)
    o["hmask16"] = (rows[:, None] // 16 == np.arange(12)[None, :]).astype(f)
    o["hmask64"] = (rows[:, None] // 64 == np.arange(12)[None, :]).astype(f)
    a = {k[8:]: v for k, v in i.items() if k.startswith("L0_attn_")}
    nl = a["Wq"].shape[0]
    o["a_qkv"] = np.concatenate([rows_of(a[k], HALF) for k in ("Wq", "Wk", "Wv")], -1)
    apart = np.zeros((nl, 6, 16, 2, 6), f)
    for j in range(6):
        apart[:, j, :, :, j] = a["bk"].reshape(nl, 2, 6, 16)[:, :, j].transpose(0, 2, 1)
    o["a_qkvb"] = np.concatenate([a[k].reshape(nl, 2, HALF).transpose(0, 2, 1) for k in ("bq", "bk", "bv")]
                                 + [apart.reshape(nl, HALF, 12)], -1)
    o["a_ob"] = spread(a["bo"])
    own_image = (np.arange(GROUP)[:, None] == img[None, :]).astype(f)
    o["a_query_image"] = np.broadcast_to(own_image[:, None, None], (GROUP, 2, BLOCK_TILES, TILE)).reshape(GROUP, 2, -1)
    other = np.where(own_image > 0, f(0), f(OFF))
    o["a_key_off"] = np.broadcast_to(other[:, None, None, None], (GROUP, 2, BLOCK_TILES, 6, TILE)).reshape(
        GROUP, 2, BLOCK_TILES, 6 * TILE)
    o["a_wo"] = rows_of(a["Wo"], HALF)
    o["a_ln1"] = np.concatenate([spread(a["ln1_g"]), spread(a["ln1_b"])], -1)
    o["a_w1"] = rows_of(a["W1"], HALF)
    o["a_b1"] = a["b1"].reshape(nl, FCH, 128).transpose(0, 2, 1)
    o["a_w2"] = rows_of(a["W2"], 128)
    o["a_ln2"] = np.concatenate([spread(a[k]) for k in ("b2", "ln2_g", "ln2_b")], -1)
    b = {k[7:]: v for k, v in i.items() if k.startswith("L0_ffn_")}
    o["b_qkv"] = np.concatenate([rows_of(b[k], HALF) for k in ("attn_q", "attn_k", "attn_v")], -1)
    o["b_wo"] = rows_of(b["attn_o"], 128)
    o["b_w1"], o["b_w2"] = rows_of(b["ffn_wi"], HALF), rows_of(b["ffn_wo"], 128)
    o["b_m1"], o["b_m2"] = rows_of(b["moe_w1"], HALF), rows_of(b["moe_w2"], 128)
    o["b_gate"] = rows_of(b["gate_w"], HALF)
    gains = np.stack([b["ln1"], b["ln2"]], 1).reshape(-1, DIM)
    o["b_gains"] = spread(np.concatenate([gains, b["ln_f"][None]], 0)).transpose(1, 0, 2)
    pos = np.arange(TILE) % LEN
    far = pos[None, :] - pos[:, None]
    dist = np.abs(far)
    edges = np.array([8, 12, 16, 23, 32])
    bucket = 16 * (far > 0) + np.where(dist < 8, dist, 7 + (dist[..., None] >= edges).sum(-1))
    table = b["rel_emb"][bucket].transpose(0, 2, 1)
    o["b_bias"] = np.where((img[:, None] == img[None, :])[:, None, :], table, f(OFF)).reshape(TILE, 12 * TILE)
    e8 = np.arange(8)
    o["before8"] = np.broadcast_to((e8[None, :] < e8[:, None]).astype(f), (TILE, 8, 8))
    wt = i["L1_attn_W_qkv"].T
    o["g_qkv"] = rows_of(wt, HALF)
    o["g_wo"] = rows_of(i["L1_attn_W_out"].T, 128)
    o["e_router"] = rows_of(i["L1_ffn_router_w"].T, HALF)
    o["e_router_bias"] = spread(i["L1_ffn_router_b"])
    o["e_out_bias"] = i["L1_ffn_expert_b"]
    o["e_w"] = rows_of(i["L1_ffn_expert_w"].transpose(2, 0, 1).reshape(DIM, -1), HALF).reshape(HALF, 2, 8, DIM)
    o["d_qkv"] = rows_of(i["L2_attn_W_attn"].T, HALF)
    o["d_wo"] = rows_of(i["L2_attn_W_out"].T, HALF)
    o["d_lambda"] = spread(np.stack([i["L2_attn_lambda_" + k] for k in ("q1", "q2", "k1", "k2")])).transpose(1, 0, 2)
    o["f_router"] = rows_of(i["L2_ffn_gate_w"], HALF)
    o["f_router_bias"] = spread(i["L2_ffn_gate_b"])
    o["f_w1"], o["f_w2"] = rows_of(i["L2_ffn_w1"], HALF), rows_of(i["L2_ffn_w2"], 128)
    o["f_b1"] = i["L2_ffn_b1"].reshape(8, FCH, 128).transpose(0, 2, 1)
    o["f_out_bias"] = i["L2_ffn_b2"]
    o["h_qkv"] = rows_of(i["L3_attn_W_qkv"], HALF)
    o["h_qk_bias"] = i["L3_attn_b_qkv"][:2 * DIM].reshape(4, HALF).T
    o["h_v_bias"] = spread(i["L3_attn_b_qkv"][2 * DIM:])
    back = pos[None, :] - pos[:, None]
    o["h_decay"] = np.where((img[:, None] == img[None, :]) & (back >= 0), f(0.99) ** np.maximum(back, 0).astype(f), f(0))
    x = {k[7:]: v for k, v in i.items() if k.startswith("L3_ffn_")}
    o["i_router"] = rows_of(x["router_w"].T, HALF)
    o["i_router_bias"] = np.concatenate([spread(x["router_b"]), spread(x["corr_bias"])], -1)
    o["i_out_bias"] = np.concatenate([x["gbd"], x["sbd"][None], np.zeros((1, DIM), f)], 0)

    def halves(w):
        return np.stack([w[:, :HALF], w[:, HALF:]], 0)

    wg, wu = np.concatenate([x["gWg"], halves(x["sWg"])], 0), np.concatenate([x["gWu"], halves(x["sWu"])], 0)
    wd = np.concatenate([x["gWd"], x["sWd"].reshape(2, HALF, DIM)], 0)
    bg, bu = np.concatenate([x["gbg"], x["sbg"].reshape(2, HALF)], 0), np.concatenate([x["gbu"], x["sbu"].reshape(2, HALF)], 0)
    gu = rows_of(np.concatenate([wg, wu], -1), HALF).reshape(18, HALF, 2 * DIM)
    o["i_w"] = np.concatenate([gu, wd, bg[..., None], bu[..., None]], -1)
    e16 = np.arange(16)
    o["before16"] = np.broadcast_to((e16[None, :] < e16[:, None]).astype(f), (TILE, 16, 16))
    s = SIDE // PATCH
    im = np.concatenate([i["x"], i["x"][-1:]], 0).reshape(PADDED, CHANNELS, s, PATCH, s, PATCH)
    im = im.transpose(3, 5, 1, 0, 2, 4).reshape(PATCH_DIM, TOKENS)
    o["t_patches"] = rows_of(im, 128)
    o["t_w"] = rows_of(i["L0_tok_W"].T, 128)
    o["t_bias"] = spread(i["L0_tok_b"])
    o["t_ln0"] = np.concatenate([spread(a["ln0_g"]), spread(a["ln0_b"])], -1)
    cw = a["pos_conv_w"].reshape(CONV_GROUPS, CONV_CH, CONV_CH, CONV_K)
    apart = np.arange(CONV_D) - (CONV_BLOCKS - 1)
    j = np.arange(CONV_J)
    k = CONV_K // 2 + j[:, None, None] - j - CONV_J * apart[:, None]
    o["t_taps"] = cw[:, :, :, k].transpose(2, 3, 0, 4, 1, 5).reshape(TILE, CONV_GROUPS, CONV_D, TILE)
    o["t_conv_bias"] = np.repeat(a["pos_conv_b"].reshape(CONV_GROUPS, CONV_CH).T, CONV_J, 0)
    return {k: np.ascontiguousarray(v) for k, v in o.items()}


_SHAPE = (IMAGES, LEN, DIM)


def kernel(**inputs):
    import concourse.bacc as _bacc
    from concourse.bass_utils import run_bass_kernel_spmd as _run

    nc = _bacc.Bacc("TRN2", target_bir_lowering=False, num_devices=1)
    arrays, args = {}, {}
    for name, a in lay_out({k: np.asarray(v) for k, v in inputs.items()}).items():
        arrays[f"in_{name}"] = a
        args[name] = nc.dram_tensor(f"in_{name}", a.shape, mybir.dt.from_np(a.dtype), kind="ExternalInput").ap()
    out = nc.dram_tensor("out_tower", _SHAPE, F32, kind="ExternalOutput").ap()
    vit_tower(nc, args, out)
    return _run(nc, [arrays], core_ids=[0]).results[0]["out_tower"]
```
